# Optimizing a Trainium2 kernel written in Bass

```python
import numpy as np
import jax
import jax.numpy as jnp

def _softmax(x, axis=-1):
    return jax.nn.softmax(x, axis=axis)

def _gelu(x):
    return jax.nn.gelu(x, approximate=True)

def _silu(x):
    return jax.nn.silu(x)

def _sigmoid(x):
    return jax.nn.sigmoid(x)

def _layernorm(x, axis=-1, eps=1e-05):
    m = jnp.mean(x, axis=axis, keepdims=True)
    v = jnp.var(x, axis=axis, keepdims=True)
    return (x - m) / jnp.sqrt(v + eps)

def _scatter_add(tgt, idx, src, axis=0):
    return tgt.at[idx].add(src)

def _segment_sum(src, seg, n):
    return jax.ops.segment_sum(src, seg, n)
kernel_name = 'mk_decoder_postln_d1_seqx_r8_62f7e4'

def setup_inputs(seed: int=0):
    np.random.seed(seed)
    _w = jnp.asarray

    def _rec_inputs():
        import jax
        import jax.numpy as jnp
        _rk = jax.random.key(seed)
        x = -0.0005847 + 1 * jax.random.normal(jax.random.fold_in(_rk, 1), (32, 128, 128), jnp.float32)
        _lenS = 128 - jax.random.randint(jax.random.fold_in(_rk, 7), (32,), 0, max(1, 128 // 4) + 1, jnp.int32)
        _lenS2 = 128 - jax.random.randint(jax.random.fold_in(_rk, 8), (32,), 0, max(1, 128 // 4) + 1, jnp.int32)
        _ctx_1024P = jax.random.normal(jax.random.fold_in(_rk, 11), (32, 16, 128), jnp.float32)
        _ctx_1024c = jax.random.dirichlet(jax.random.fold_in(_rk, 511), 0.3 * jnp.ones((16,), jnp.float32), (32, 128))
        _ctx_1024t = jnp.einsum('bsk,bkd->bsd', _ctx_1024c, _ctx_1024P)
        _ctx_1024t = _ctx_1024t * jax.lax.rsqrt(jnp.mean(jnp.square(_ctx_1024t)) + 1e-12) * 0.953939
        ctx_1024 = 2.81802e-05 + 1.00001 * (_ctx_1024t + 0.3 * jax.random.normal(jax.random.fold_in(_rk, 611), (32, 128, 128), jnp.float32))
        _validS = jnp.arange(128)[None, :] < _lenS[:, None]
        _validS2 = jnp.arange(128)[None, :] < _lenS2[:, None]
        _causal = jnp.tril(jnp.ones((128, 128), dtype=bool))
        mask_BxS2_ik1 = jnp.where(jnp.broadcast_to(_validS2[:, :], (32, 128)), 1, 0).astype(jnp.int32)
        return (x, ctx_1024, mask_BxS2_ik1)
    x, ctx_1024, mask_BxS2_ik1 = _rec_inputs()

    def _L0_attn_setup():
        import jax, jax.numpy as jnp
        import numpy as np
        B, N, D = (4, 256, 128)
        H, HD = (8, 64)
        FF = 512
        ETA = 0.1
        DT = 0.01
        GAMMA_FLOOR = 0.1
        EPS = 1e-05

        def layernorm(x, g, b):
            m = jnp.mean(x, -1, keepdims=True)
            v = jnp.var(x, -1, keepdims=True)
            return (x - m) * jax.lax.rsqrt(v + EPS) * g + b

        def _cf_scan(d):
            dT = jnp.swapaxes(d, 0, 1)

            def step(c, di):
                a = di - 1.0 / c
                return (a, a)
            _, rest = jax.lax.scan(step, dT[0], dT[1:])
            return jnp.swapaxes(jnp.concatenate([dT[:1], rest], 0), 0, 1)

        def bk_core_diag(V, gamma):
            d = jax.lax.complex(V + 2.0, -gamma)
            a = _cf_scan(d)
            b = _cf_scan(d[:, ::-1])[:, ::-1]
            G = 1.0 / (a + b - d)
            return jnp.stack([G.real, G.imag], axis=-1)

        def hebbian_scan(q, k, v, gamma):
            qT = jnp.transpose(q, (1, 0, 2, 3))
            kT = jnp.transpose(k, (1, 0, 2, 3))
            vT = jnp.transpose(v, (1, 0, 2, 3))
            gT = jnp.swapaxes(gamma, 0, 1)
            W0 = jnp.zeros((q.shape[0], H, HD, HD), dtype=q.dtype)

            def step(W, inp):
                q_t, k_t, v_t, g_t = inp
                decay = jnp.exp(-g_t * DT)[:, None, None, None]
                W = decay * W + ETA * (k_t[..., :, None] * v_t[..., None, :])
                o = jnp.einsum('bhd,bhde->bhe', q_t, W)
                return (W, o)
            _, outs = jax.lax.scan(step, W0, (qT, kT, vT, gT))
            return jnp.transpose(outs, (1, 0, 2, 3)).reshape(q.shape[0], q.shape[1], H * HD)
        key = jax.random.key(seed)
        ks = jax.random.split(key, 12)
        s = lambda fan: 1.0 / np.sqrt(fan)
        return {'x': jax.random.normal(ks[0], (B, N, D), jnp.float32), 'ln1_g': jnp.ones((D,), jnp.float32), 'ln1_b': jnp.zeros((D,), jnp.float32), 'ln2_g': jnp.ones((D,), jnp.float32), 'ln2_b': jnp.zeros((D,), jnp.float32), 'ln3_g': jnp.ones((D,), jnp.float32), 'ln3_b': jnp.zeros((D,), jnp.float32), 'w_pot': jax.random.normal(ks[1], (D, 2), jnp.float32) * s(D), 'b_pot': jnp.zeros((2,), jnp.float32), 'w_bk': jax.random.normal(ks[2], (2, D), jnp.float32) * s(2), 'b_bk': jnp.zeros((D,), jnp.float32), 'w_qkv': jax.random.normal(ks[3], (D, 3 * H * HD), jnp.float32) * s(D), 'b_qkv': jnp.zeros((3 * H * HD,), jnp.float32), 'w_out': jax.random.normal(ks[4], (H * HD, D), jnp.float32) * s(H * HD), 'b_out': jnp.zeros((D,), jnp.float32), 'w_ff1': jax.random.normal(ks[5], (D, FF), jnp.float32) * s(D), 'b_ff1': jnp.zeros((FF,), jnp.float32), 'w_ff2': jax.random.normal(ks[6], (FF, D), jnp.float32) * s(FF), 'b_ff2': jnp.zeros((D,), jnp.float32)}
    _L0_attn_all = _L0_attn_setup()
    _L0_attn_in = {k: v for k, v in _L0_attn_all.items() if k in ('ln1_g', 'ln1_b', 'ln2_g', 'ln2_b', 'ln3_g', 'ln3_b', 'w_pot', 'b_pot', 'w_bk', 'b_bk', 'w_qkv', 'b_qkv', 'w_out', 'b_out', 'w_ff1', 'b_ff1', 'w_ff2', 'b_ff2')}
    del _L0_attn_all

    def _L0_xattn_setup():
        import jax, jax.numpy as jnp
        import numpy as np
        DIM = 128
        NUM_HEADS = 16
        HEAD_DIM = DIM // NUM_HEADS
        SCALE = HEAD_DIM ** (-0.5)

        def _split_heads(x):
            B, L, _ = x.shape
            return x.reshape(B, L, NUM_HEADS, HEAD_DIM).transpose(0, 2, 1, 3)
        key = jax.random.key(seed)
        ks = jax.random.split(key, 12)
        B, Q, S = (4, 900, 512)
        inp = {'query_vectors': jax.random.normal(ks[0], (B, Q, DIM), jnp.float32), 'key_input_flatten': jax.random.normal(ks[1], (B, S, DIM), jnp.float32), 'value_input_flatten': jax.random.normal(ks[2], (B, S, DIM), jnp.float32), 'attention_mask': jax.random.randint(ks[3], (B, S), 0, 2, jnp.int32), 'Wq': jax.random.normal(ks[4], (DIM, DIM), jnp.float32) * 0.02, 'bq': jnp.zeros((DIM,), jnp.float32), 'Wk': jax.random.normal(ks[5], (DIM, DIM), jnp.float32) * 0.02, 'bk': jnp.zeros((DIM,), jnp.float32), 'Wv': jax.random.normal(ks[6], (DIM, DIM), jnp.float32) * 0.02, 'bv': jnp.zeros((DIM,), jnp.float32), 'Wo': jax.random.normal(ks[7], (DIM, DIM), jnp.float32) * 0.02, 'bo': jnp.zeros((DIM,), jnp.float32)}
        return inp
    _L0_xattn_all = _L0_xattn_setup()
    _L0_xattn_in = {k: v for k, v in _L0_xattn_all.items() if k in ('Wq', 'bq', 'Wk', 'bk', 'Wv', 'bv', 'Wo', 'bo')}
    del _L0_xattn_all

    def _L0_ffn_setup():
        import jax, jax.numpy as jnp
        import numpy as np
        B, S, H, M, E, K = (4, 256, 128, 512, 8, 2)
        key = jax.random.key(seed)
        ks = jax.random.split(key, 6)
        x = jax.random.normal(ks[0], (B, S, H), dtype=jnp.float32)
        Wr = jax.random.normal(ks[1], (E, H), dtype=jnp.float32) * (1.0 / np.sqrt(H))
        W1 = jax.random.normal(ks[2], (E, M, H), dtype=jnp.float32) * np.sqrt(2.0 / (H + M))
        b1 = jax.random.normal(ks[3], (E, M), dtype=jnp.float32) * 1e-06
        W2 = jax.random.normal(ks[4], (E, H, M), dtype=jnp.float32) * np.sqrt(2.0 / (H + M))
        b2 = jax.random.normal(ks[5], (E, H), dtype=jnp.float32) * 1e-06
        return {'x': x, 'Wr': Wr, 'W1': W1, 'b1': b1, 'W2': W2, 'b2': b2}
    _L0_ffn_all = _L0_ffn_setup()
    _L0_ffn_in = {k: v for k, v in _L0_ffn_all.items() if k in ('Wr', 'W1', 'b1', 'W2', 'b2')}
    del _L0_ffn_all
    return {'x': x, 'ctx_1024': ctx_1024, 'mask_BxS2_ik1': mask_BxS2_ik1, 'L0_attn_ln1_g': _L0_attn_in['ln1_g'], 'L0_attn_ln1_b': _L0_attn_in['ln1_b'], 'L0_attn_ln2_g': _L0_attn_in['ln2_g'], 'L0_attn_ln2_b': _L0_attn_in['ln2_b'], 'L0_attn_ln3_g': _L0_attn_in['ln3_g'], 'L0_attn_ln3_b': _L0_attn_in['ln3_b'], 'L0_attn_w_pot': _L0_attn_in['w_pot'], 'L0_attn_b_pot': _L0_attn_in['b_pot'], 'L0_attn_w_bk': _L0_attn_in['w_bk'], 'L0_attn_b_bk': _L0_attn_in['b_bk'], 'L0_attn_w_qkv': _L0_attn_in['w_qkv'], 'L0_attn_b_qkv': _L0_attn_in['b_qkv'], 'L0_attn_w_out': _L0_attn_in['w_out'], 'L0_attn_b_out': _L0_attn_in['b_out'], 'L0_attn_w_ff1': _L0_attn_in['w_ff1'], 'L0_attn_b_ff1': _L0_attn_in['b_ff1'], 'L0_attn_w_ff2': _L0_attn_in['w_ff2'], 'L0_attn_b_ff2': _L0_attn_in['b_ff2'], 'L0_xattn_Wq': _L0_xattn_in['Wq'], 'L0_xattn_bq': _L0_xattn_in['bq'], 'L0_xattn_Wk': _L0_xattn_in['Wk'], 'L0_xattn_bk': _L0_xattn_in['bk'], 'L0_xattn_Wv': _L0_xattn_in['Wv'], 'L0_xattn_bv': _L0_xattn_in['bv'], 'L0_xattn_Wo': _L0_xattn_in['Wo'], 'L0_xattn_bo': _L0_xattn_in['bo'], 'L0_ffn_Wr': _L0_ffn_in['Wr'], 'L0_ffn_W1': _L0_ffn_in['W1'], 'L0_ffn_b1': _L0_ffn_in['b1'], 'L0_ffn_W2': _L0_ffn_in['W2'], 'L0_ffn_b2': _L0_ffn_in['b2']}

def reference(x, ctx_1024, mask_BxS2_ik1, L0_attn_ln1_g, L0_attn_ln1_b, L0_attn_ln2_g, L0_attn_ln2_b, L0_attn_ln3_g, L0_attn_ln3_b, L0_attn_w_pot, L0_attn_b_pot, L0_attn_w_bk, L0_attn_b_bk, L0_attn_w_qkv, L0_attn_b_qkv, L0_attn_w_out, L0_attn_b_out, L0_attn_w_ff1, L0_attn_b_ff1, L0_attn_w_ff2, L0_attn_b_ff2, L0_xattn_Wq, L0_xattn_bq, L0_xattn_Wk, L0_xattn_bk, L0_xattn_Wv, L0_xattn_bv, L0_xattn_Wo, L0_xattn_bo, L0_ffn_Wr, L0_ffn_W1, L0_ffn_b1, L0_ffn_W2, L0_ffn_b2):
    import jax
    import jax.numpy as jnp

    def _L0_attn_ref(x, ln1_g, ln1_b, ln2_g, ln2_b, ln3_g, ln3_b, w_pot, b_pot, w_bk, b_bk, w_qkv, b_qkv, w_out, b_out, w_ff1, b_ff1, w_ff2, b_ff2):
        import jax, jax.numpy as jnp
        import numpy as np
        B, N, D = (4, 256, 128)
        H, HD = (8, 64)
        FF = 512
        ETA = 0.1
        DT = 0.01
        GAMMA_FLOOR = 0.1
        EPS = 1e-05

        def layernorm(x, g, b):
            m = jnp.mean(x, -1, keepdims=True)
            v = jnp.var(x, -1, keepdims=True)
            return (x - m) * jax.lax.rsqrt(v + EPS) * g + b

        def _cf_scan(d):
            dT = jnp.swapaxes(d, 0, 1)

            def step(c, di):
                a = di - 1.0 / c
                return (a, a)
            _, rest = jax.lax.scan(step, dT[0], dT[1:])
            return jnp.swapaxes(jnp.concatenate([dT[:1], rest], 0), 0, 1)

        def bk_core_diag(V, gamma):
            d = jax.lax.complex(V + 2.0, -gamma)
            a = _cf_scan(d)
            b = _cf_scan(d[:, ::-1])[:, ::-1]
            G = 1.0 / (a + b - d)
            return jnp.stack([G.real, G.imag], axis=-1)

        def hebbian_scan(q, k, v, gamma):
            qT = jnp.transpose(q, (1, 0, 2, 3))
            kT = jnp.transpose(k, (1, 0, 2, 3))
            vT = jnp.transpose(v, (1, 0, 2, 3))
            gT = jnp.swapaxes(gamma, 0, 1)
            W0 = jnp.zeros((q.shape[0], H, HD, HD), dtype=q.dtype)

            def step(W, inp):
                q_t, k_t, v_t, g_t = inp
                decay = jnp.exp(-g_t * DT)[:, None, None, None]
                W = decay * W + ETA * (k_t[..., :, None] * v_t[..., None, :])
                o = jnp.einsum('bhd,bhde->bhe', q_t, W)
                return (W, o)
            _, outs = jax.lax.scan(step, W0, (qT, kT, vT, gT))
            return jnp.transpose(outs, (1, 0, 2, 3)).reshape(q.shape[0], q.shape[1], H * HD)
        b, n, d = x.shape
        xn1 = layernorm(x, ln1_g, ln1_b)
        pot = xn1 @ w_pot + b_pot
        V = pot[..., 0]
        gamma = jax.nn.softplus(pot[..., 1]) + GAMMA_FLOOR
        bk_features = bk_core_diag(V, gamma)
        x = x + bk_features @ w_bk + b_bk
        xn2 = layernorm(x, ln2_g, ln2_b)
        qkv = (xn2 @ w_qkv + b_qkv).reshape(b, n, 3, H, HD)
        q, k, v = (qkv[:, :, 0], qkv[:, :, 1], qkv[:, :, 2])
        heb = hebbian_scan(q, k, v, gamma)
        x = x + heb @ w_out + b_out
        xn3 = layernorm(x, ln3_g, ln3_b)
        x = x + jax.nn.gelu(xn3 @ w_ff1 + b_ff1) @ w_ff2 + b_ff2
        return x

    def _L0_xattn_ref(query_vectors, key_input_flatten, value_input_flatten, attention_mask, Wq, bq, Wk, bk, Wv, bv, Wo, bo):
        import jax, jax.numpy as jnp
        import numpy as np
        DIM = 128
        NUM_HEADS = 16
        HEAD_DIM = DIM // NUM_HEADS
        SCALE = HEAD_DIM ** (-0.5)

        def _split_heads(x):
            B, L, _ = x.shape
            return x.reshape(B, L, NUM_HEADS, HEAD_DIM).transpose(0, 2, 1, 3)
        B, Q, D = query_vectors.shape
        q = _split_heads(query_vectors @ Wq.T + bq) * SCALE
        k = _split_heads(key_input_flatten @ Wk.T + bk)
        v = _split_heads(value_input_flatten @ Wv.T + bv)
        scores = jnp.einsum('bhqd,bhsd->bhqs', q, k)
        scores = scores + attention_mask.astype(scores.dtype)[:, None, None, :] * -100.0
        probs = jax.nn.softmax(scores, axis=-1)
        ctx = jnp.einsum('bhqs,bhsd->bhqd', probs, v)
        ctx = ctx.transpose(0, 2, 1, 3).reshape(B, Q, D)
        return ctx @ Wo.T + bo

    def _L0_ffn_ref(x, Wr, W1, b1, W2, b2):
        import jax, jax.numpy as jnp
        import numpy as np
        B, S, H, M, E, K = (4, 256, 128, 512, 8, 2)
        logits = jnp.einsum('bsh,eh->bse', x, Wr)
        probs = jax.nn.softmax(logits, axis=-1)
        top_v, top_i = jax.lax.top_k(probs, K)
        top_v = top_v / jnp.sum(top_v, axis=-1, keepdims=True)
        out = jnp.zeros_like(x)
        for e in range(E):
            w_e = jnp.sum(jnp.where(top_i == e, top_v, 0.0), axis=-1)
            h = jnp.einsum('bsh,mh->bsm', x, W1[e]) + b1[e]
            h = jax.nn.gelu(h, approximate=False)
            y = jnp.einsum('bsm,hm->bsh', h, W2[e]) + b2[e]
            out = out + y * w_e[..., None]
        return out
    x = _layernorm(x + _L0_attn_ref(x, L0_attn_ln1_g, L0_attn_ln1_b, L0_attn_ln2_g, L0_attn_ln2_b, L0_attn_ln3_g, L0_attn_ln3_b, L0_attn_w_pot, L0_attn_b_pot, L0_attn_w_bk, L0_attn_b_bk, L0_attn_w_qkv, L0_attn_b_qkv, L0_attn_w_out, L0_attn_b_out, L0_attn_w_ff1, L0_attn_b_ff1, L0_attn_w_ff2, L0_attn_b_ff2), axis=-1)
    x = _layernorm(x + _L0_xattn_ref(x, ctx_1024, ctx_1024, mask_BxS2_ik1, L0_xattn_Wq, L0_xattn_bq, L0_xattn_Wk, L0_xattn_bk, L0_xattn_Wv, L0_xattn_bv, L0_xattn_Wo, L0_xattn_bo), axis=-1)
    x = _layernorm(x + _L0_ffn_ref(x, L0_ffn_Wr, L0_ffn_W1, L0_ffn_b1, L0_ffn_W2, L0_ffn_b2), axis=-1)
    return x

_drawn_inputs = setup_inputs


def setup_inputs(seed=0):
    import zlib

    import numpy as np

    out = dict(_drawn_inputs(seed))
    spreads = {'L0_attn_ln1_g': (1.0, 0.2),
     'L0_attn_ln1_b': (0.0, 0.1),
     'L0_attn_ln2_g': (1.0, 0.2),
     'L0_attn_ln2_b': (0.0, 0.1),
     'L0_attn_ln3_g': (1.0, 0.2),
     'L0_attn_ln3_b': (0.0, 0.268),
     'L0_attn_b_pot': (0.0, 0.1),
     'L0_attn_b_bk': (0.0, 0.1),
     'L0_attn_b_qkv': (0.0, 0.1),
     'L0_attn_b_out': (0.0, 0.1),
     'L0_attn_b_ff1': (0.0, 0.27),
     'L0_attn_b_ff2': (0.0, 0.1),
     'L0_xattn_bq': (0.0, 0.8),
     'L0_xattn_bk': (0.0, 2.0),
     'L0_xattn_bv': (0.0, 0.1),
     'L0_xattn_bo': (0.0, 0.1)}
    factors = {'L0_xattn_Wq': 7.667, 'L0_xattn_Wk': 7.659, 'L0_ffn_b1': 64.0, 'L0_ffn_b2': 64.0}
    for name, (base, spread) in spreads.items():
        noise = np.random.default_rng([zlib.crc32(name.encode()), seed]).standard_normal(out[name].shape)
        drawn = base * np.exp(spread * noise) if base else spread * noise
        out[name] = jnp.asarray(drawn.astype(out[name].dtype))
    for name, factor in factors.items():
        out[name] = (out[name] * factor).astype(out[name].dtype)
    return out
```

```python
from contextlib import ExitStack

import numpy as np

import concourse.bass as bass
from concourse import mybir

F32 = mybir.dt.float32
BF16 = mybir.dt.bfloat16
F32R = mybir.dt.float32r
I32 = mybir.dt.int32
ALU = mybir.AluOpType
ACT = mybir.ActivationFunctionType
AX = mybir.AxisListType

P = 128
SEQS = 32
T = 4
G = SEQS // T
GT = T * P
HEADS, HD = 8, 64
PAIRS = HEADS // 2
XH, XD = 16, 8
XC = XH // 4
FF = 512
FC = FF // P
EXP = 8
ETA, DT, GAMMA_FLOOR, EPS = 0.1, 0.01, 0.1, 1e-5
XSCALE = XD ** -0.5
MASKED = -100.0
CL = 8
CN = P // CL
FAR = 1.0e5

JOBS = (
    ["xh2T", "decay"]
    + [f"{n}{p}" for p in range(PAIRS) for n in ("q", "k")]
    + ["v0", "v1", "at0r0", "at0r1", "v2", "v3", "at1r0", "at1r1", "hpv0"]
    + ["at2r0", "at2r1", "hpv1", "wo0", "at3r0", "at3r1", "hpv2", "wo1", "hpv3", "wo2", "wo3"]
    + [f"kp{c}" for c in range(XC)] + ["cv", "xh3T"]
    + [f"ff1c{c}" for c in range(FC)] + [f"ff2t{t}" for t in range(T)]
    + ["xaT"] + [f"qp{c}" for c in range(XC)]
    + [f"mx0i{i}" for i in range(4)] + ["mT0"]
    + sum(([f"mx{t + 1}i{i}" for i in range(4)] + [f"st{t}i{i}" for i in range(4)]
           + [f"mT{t + 1}", f"xpv{t}", f"ctT{t}"] for t in range(T - 1)), [])
    + [f"st{T - 1}i{i}" for i in range(4)] + [f"xpv{T - 1}", f"ctT{T - 1}", "cxT"]
    + [f"xo{t}" for t in range(T)]
    + ["xbT", "rl", "wT", "by"]
    + [f"h{0}c{c}" for c in range(FC)]
    + sum(([f"h{e + 1}c{c}" for c in range(FC)] + [f"y{e}"] for e in range(EXP - 1)), [])
    + [f"y{EXP - 1}"]
)
NB = 8
BANK = {name: n % NB for n, name in enumerate(JOBS)}
NTH = {name: n // NB for n, name in enumerate(JOBS)}
PER_GROUP = [sum(1 for b in BANK.values() if b == n) for n in range(NB)]


def bass_decoder(nc, A):
    ctx = ExitStack()
    with ctx:
        def sb(name, shape, dt=F32):
            return ctx.enter_context(nc.sbuf_tensor(name, shape, dt))

        def sem(name):
            return ctx.enter_context(nc.semaphore(name))

        bank = [ctx.enter_context(nc.psum_tensor(f"bank{n}", [P, 512], F32)) for n in range(NB)]

        x_all = sb("x_all", [P, SEQS, P])
        ident = sb("ident", [P, P])
        antid = sb("antid", [P, P])
        tri = sb("tri", [P, P])
        after = sb("after", [P, P])
        ident_b = sb("ident_b", [P, P], BF16)
        future_b = sb("future_b", [P, P], BF16)
        ones = sb("ones", [P, P])
        pos_only = sb("pos_only", [1, P])
        pos_only_b = sb("pos_only_b", [1, P], BF16)
        mask_i = sb("mask_i", [1, GT], I32)
        mask_b = sb("mask_b", [1, GT], BF16)

        ln1_g, ln1_b = sb("ln1_g", [P, 1]), sb("ln1_b", [P, 1])
        ln2_g, ln2_b = sb("ln2_g", [P, 1]), sb("ln2_b", [P, 1])
        ln3_g, ln3_b = sb("ln3_g", [P, 1]), sb("ln3_b", [P, 1])
        w_pot, b_pot = sb("w_pot", [P, 2]), sb("b_pot", [1, 2])
        w_potg, w_potc = sb("w_potg", [P, 2]), sb("w_potc", [P, 2])
        pot_bias = sb("pot_bias", [P, 2])
        mean_w = sb("mean_w", [P, P])
        lnb_cols = sb("lnb_cols", [P, 3, P])
        w_bk_bc = sb("w_bk_bc", [P, 2, P])
        b_bk_bc = sb("b_bk_bc", [P, P])
        w_qkv = sb("w_qkv", [P, 3 * HEADS * HD])
        b_qk = sb("b_qk", [P, 2 * PAIRS])
        bg_qk = sb("bg_qk", [P, 2 * PAIRS])
        b_v_row = sb("b_v_row", [1, FF])
        bg_v = sb("bg_v", [P, FF])
        w_out = sb("w_out", [P, PAIRS, P])
        b_out_bc = sb("b_out_bc", [P, P])
        w_ff1 = sb("w_ff1", [P, FF])
        b_ff1, bg_ff1 = sb("b_ff1", [P, FC]), sb("bg_ff1", [P, FC])
        w_ff2 = sb("w_ff2", [P, FC, P])
        b_ff2_bc = sb("b_ff2_bc", [P, P])
        wq_pad, wk_pad = sb("wq_pad", [P, XC, P]), sb("wk_pad", [P, XC, P])
        bq_pad, bk_pad = sb("bq_pad", [P, XC]), sb("bk_pad", [P, XC])
        q_ones, k_ones = sb("q_ones", [P, XC]), sb("k_ones", [P, XC])
        low_rows = sb("low_rows", [P, 2])
        wv_t, wo_t = sb("wv_t", [P, P]), sb("wo_t", [P, P])
        bv_col, bo_row = sb("bv_col", [P, 1]), sb("bo_row", [1, P])
        bo_bc = sb("bo_bc", [P, P])
        wr_t = sb("wr_t", [P, EXP])
        w1_t = sb("w1_t", [P, EXP, FF])
        b1_c = sb("b1_c", [P, EXP, FC])
        w2_t = sb("w2_t", [P, EXP, FC, P])
        b2_r = sb("b2_r", [EXP, P])

        minus_half = sb("minus_half", [P, SEQS])
        gamma = sb("gamma", [P, SEQS])
        green = sb("green", [P, 2, SEQS])
        vpad = sb("vpad", [P, T, XH, 32])
        negmax = [sb(f"negmax{n}", [P, 4, 32]) for n in range(2)]

        group_ctx, ctx = ctx, ctx.enter_context(ExitStack())
        xT_all = sb("xT_all", [P, SEQS * P])
        future = sb("future", [P, P])
        st1 = sb("st1", [P, SEQS, 6])
        mv1 = sb("mv1", [P, SEQS, 2])
        rstd1 = sb("rstd1", [P, SEQS])
        zpot_row = sb("zpot_row", [2, SEQS * P])
        zpot_seq = sb("zpot_seq", [2 * SEQS, P])
        zpot = sb("zpot", [P, 2, SEQS])
        zabs, zln = sb("zabs", [P, SEQS]), sb("zln", [P, SEQS])
        diag = sb("diag", [P, 2, SEQS])
        d_row = sb("d_row", [2 * SEQS, 2, P])
        di_sign = sb("di_sign", [2 * SEQS, 2, P])
        Y = sb("Y", [2 * SEQS, CL + 2, 2, 2, CN])
        Ya = sb("Ya", [2 * SEQS, 2, 2, CN])
        Yb = sb("Yb", [2 * SEQS, 2, 2, CN])
        Yc = sb("Yc", [2 * SEQS, 2, 2, CN])
        C = sb("C", [2 * SEQS, CN, 2, 2, 4])
        Cs = sb("Cs", [2 * SEQS, CN, 16])
        cmax, crec = sb("cmax", [2 * SEQS, CN]), sb("crec", [2 * SEQS, CN])
        S = sb("S", [2 * SEQS, CN + 1, 4])
        Sp = sb("Sp", [2 * SEQS, 4, 4])
        Sa = sb("Sa", [2 * SEQS, 2, 2, CN])
        Sb = sb("Sb", [2 * SEQS, 2, 2, CN])
        Z = sb("Z", [2 * SEQS, CL + 1, 4, CN])
        Zb = sb("Zb", [2 * SEQS, CL + 1, 4, CN])
        Pr = sb("Pr", [2 * SEQS, CN, CL + 1])
        Pi = sb("Pi", [2 * SEQS, CN, CL + 1])
        ra, rb = sb("ra", [2 * SEQS, P]), sb("rb", [2 * SEQS, P])
        rc, rd = sb("rc", [2 * SEQS, P]), sb("rd", [2 * SEQS, P])
        re_, rf = sb("re_", [2 * SEQS, P]), sb("rf", [2 * SEQS, P])
        frac = sb("frac", [2 * SEQS, 2, P])
        neg_id = sb("neg_id", [SEQS, SEQS])
        fold_id = sb("fold_id", [2 * SEQS, SEQS])
        den = sb("den", [P, 2, SEQS])
        ga, gb = sb("ga", [P, SEQS]), sb("gb", [P, SEQS])

        ctx.close()
        ctx = group_ctx
        xbk = sb("xbk", [P, T, P])
        x1 = sb("x1", [P, T, P])
        xf = sb("xf", [P, T, P])
        x1b = sb("x1b", [P, T, P])
        x2 = sb("x2", [P, T, P])
        xsum = xf
        xn = sb("xn", [P, T, P])
        xnT = sb("xnT", [P, GT])
        stats = sb("stats", [P, T, 6])
        mv = sb("mv", [P, T, 2])
        vare = sb("vare", [P, T])
        rstd = sb("rstd", [P, T])
        qT, kT = sb("qT", [P, PAIRS, GT]), sb("kT", [P, PAIRS, GT])
        cumg = sb("cumg", [P, T, P])
        decay = sb("decay", [P, T, P])
        mix = sb("mix", [P, 2, 4 * XC * P])
        pT = [mix[:, n, :].rearrange("p (i c n) -> p i c n", i=4, c=XC) for n in range(2)]
        v_sb = mix[:, 0, :].rearrange("p (t n) -> p t n", t=T)
        at = [mix[:, 1, n * GT * 2:(n + 1) * GT * 2].rearrange("p (r a n) -> p r a n", r=2, a=PAIRS)
              for n in range(2)]
        hebT = [sb(f"hebT{n}", [P, PAIRS, P]) for n in range(2)]
        hT = [sb(f"hT{n}", [P, FC, GT]) for n in range(2)]
        ctxT = sb("ctxT", [P, GT])
        xa = sb("xa", [P, T, P])
        xab = xbk
        qp, kp = qT, kT
        high = [sb(f"high{n}", [P, GT], F32R) for n in range(2)]
        qr, kr = sb("qr", [P, XC, GT], F32R), sb("kr", [P, XC, GT], F32R)
        qm = [sb(f"qm{n}", [P, XC, P], F32R) for n in range(2)]
        cT = [sb(f"cT{n}", [P, XC, P]) for n in range(2)]
        rsum = sb("rsum", [P, T, XH])
        cx = sb("cx", [P, T, XH, XD])
        cxT = sb("cxT", [P, GT])
        xb = sb("xb", [P, T, P])
        top8 = sb("top8", [P, T, 8])
        lg = sb("lg", [P, T, EXP])
        keep = sb("keep", [P, T, EXP])
        lsh = sb("lsh", [P, T, EXP])
        lex = sb("lex", [P, T, EXP])
        wraw = sb("wraw", [P, T, EXP])
        wsum, wrec = sb("wsum", [P, T]), sb("wrec", [P, T])
        gate = sb("gate", [P, T, EXP])
        gateT = sb("gateT", [EXP, GT])
        acc = x1
        out_sb = sb("out_sb", [P, T, P])

        full = [sem(f"bank{n}_full") for n in range(NB)]
        free = [sem(f"bank{n}_drained") for n in range(NB)]
        pre_loaded = sem("pre_loaded")
        x_loaded = [sem(f"x_loaded{q}") for q in range(4)]
        weights_loaded = sem("weights_loaded")
        ctx_loaded = sem("ctx_loaded")
        zseq_loaded = sem("zseq_loaded")
        mask_loaded, maskb_ready = sem("mask_loaded"), sem("maskb_ready")
        out_stored = sem("out_stored")
        out_free = sem("out_free")
        pool_const = sem("pool_const")
        wpotg_ready, wpotc_ready = sem("wpotg_ready"), sem("wpotc_ready")
        wmean_mm, potbias_mm, potbias_ready = sem("wmean_mm"), sem("potbias_mm"), sem("potbias_ready")
        lnb_ready = sem("lnb_ready")
        zrow_mm, zrow_copied = sem("zrow_mm"), sem("zrow_copied")
        bn1_ready, mv1_ready, vare1_ready, rstd1_ready = (
            sem("bn1_ready"), sem("mv1_ready"), sem("vare1_ready"), sem("rstd1_ready"))
        zpos_mm, zlink = sem("zpos_mm"), sem("zlink")
        z_ready, zln_ready, gamma_ready = sem("z_ready"), sem("zln_ready"), sem("gamma_ready")
        abs_done, exp_done = sem("abs_done"), sem("exp_done")
        drow_mm, scan_link, frac_ready, den_mm, green_ready = (
            sem("drow_mm"), sem("scan_link"), sem("frac_ready"), sem("den_mm"), sem("green_ready"))
        folded = sem("folded")
        bias_mm, bias_ready = sem("bias_mm"), sem("bias_ready")
        xbk_ready = sem("xbk_ready")
        x1_part = sem("x1_part")
        cumg_ready = sem("cumg_ready")
        sum_ready = sem("sum_ready")
        bn_ready = sem("bn_ready")
        mv_ready = sem("mv_ready")
        vare_ready = sem("vare_ready")
        rstd_ready = sem("rstd_ready")
        xn_ready = sem("xn_ready")
        x1b_ready, xf_ready, xsum_ready, xab_ready = (
            sem("x1b_ready"), sem("xf_ready"), sem("xsum_ready"), sem("xab_ready"))
        qhigh_ready, khigh_ready = sem("qhigh_ready"), sem("khigh_ready")
        qr_ready, kr_ready = sem("qr_ready"), sem("kr_ready")
        negmax_ready = sem("negmax_ready")
        rsum_ready = sem("rsum_ready")
        lsh_ready, lex_ready, gate_link, gate_ready = (
            sem("lsh_ready"), sem("lex_ready"), sem("gate_link"), sem("gate_ready"))
        dve_held, pool_held = sem("dve_held"), sem("pool_held")

        LN2, LN3, LNA, LNB, LNC = range(5)
        NLN = 5 * T

        def take(pe, g, name):
            b = BANK[name]
            pe.wait_ge(free[b], g * PER_GROUP[b] + NTH[name] + 1)
            return bank[b]

        def filled(eng, g, name):
            b = BANK[name]
            eng.wait_ge(full[b], g * PER_GROUP[b] + NTH[name] + 1)
            return bank[b]

        def drained(eng, g, name):
            b = BANK[name]
            eng.wait_ge(free[b], g * PER_GROUP[b] + NTH[name] + 2)

        block = ctx.enter_context(nc.Block())

        PRE_LOADS = [
            (xT_all[:, :], A["xT"]), (w_pot[:, :], A["w_pot"]), (b_pot[:, :], A["b_pot"]),
            (ln1_g[:, :], A["ln1_g"]), (ln1_b[:, :], A["ln1_b"]), (ident[:, :], A["ident"]),
            (antid[:, :], A["antid"]), (fold_id[:, :], A["fold_id"]),
        ]
        LOADS = [
            (tri[:, :], A["tri"]), (after[:, :], A["after"]), (future[:, :], A["future"]),
            (pos_only[:, :], A["pos_only"]),
            (ln2_g[:, :], A["ln2_g"]), (ln2_b[:, :], A["ln2_b"]),
            (ln3_g[:, :], A["ln3_g"]), (ln3_b[:, :], A["ln3_b"]),
            (w_bk_bc[:, 0, :], A["w_bk"][0:1, :].broadcast_to([P, P])),
            (w_bk_bc[:, 1, :], A["w_bk"][1:2, :].broadcast_to([P, P])),
            (b_bk_bc[:, :], A["b_bk"].broadcast_to([P, P])),
            (w_qkv[:, :], A["w_qkv"]), (b_qk[:, :], A["b_qk"]), (b_v_row[:, :], A["b_v"]),
            (w_out[:, :, :], A["w_out"]), (b_out_bc[:, :], A["b_out"].broadcast_to([P, P])),
            (w_ff1[:, :], A["w_ff1"]), (b_ff1[:, :], A["b_ff1"]), (w_ff2[:, :, :], A["w_ff2"]),
            (b_ff2_bc[:, :], A["b_ff2"].broadcast_to([P, P])),
            (wq_pad[:, :, :], A["wq_pad"]), (wk_pad[:, :, :], A["wk_pad"]),
            (bq_pad[:, :], A["bq_pad"]), (bk_pad[:, :], A["bk_pad"]),
            (q_ones[:, :], A["q_ones"]), (k_ones[:, :], A["k_ones"]),
            (low_rows[:, :], A["low_rows"]),
            (wv_t[:, :], A["wv_t"]), (wo_t[:, :], A["wo_t"]), (bv_col[:, :], A["bv"]),
            (bo_row[:, :], A["bo"]), (wr_t[:, :], A["wr_t"]), (w1_t[:, :, :], A["w1_t"]),
            (b1_c[:, :, :], A["b1"]), (w2_t[:, :, :, :], A["w2_t"]), (b2_r[:, :], A["b2"]),
        ]


        @block.sync
        def _(sp):
            for dst, src in PRE_LOADS:
                sp.dma_start(dst, src).then_inc(pre_loaded, 16)
            for q in range(4):
                sp.dma_start(x_all[:, 8 * q:8 * q + 8, :],
                             A["x"][:, 8 * q:8 * q + 8, :]).then_inc(x_loaded[q], 16)
            sp.wait_ge(zrow_copied, G)
            for n in range(2):
                sp.dma_start(zpot_seq[SEQS * n:SEQS * n + SEQS, :],
                             zpot_row[n:n + 1, :].rearrange("a (s p) -> a s p", p=P)
                             ).then_inc(zseq_loaded, 16)
            sp.wait_ge(green_ready, 1)
            sp.dma_start(ctxT[:, :], A["ctxT"][:, 0:GT]).then_inc(ctx_loaded, 16)
            sp.dma_start(mask_i[:, :], A["mask"][:, 0:GT]).then_inc(mask_loaded, 16)
            with sp.Fori(0, G - 1) as g:
                filled(sp, g, "cv")
                sp.dma_start(ctxT[:, :], A["ctxT"][:, bass.ds(g * GT + GT, GT)]).then_inc(ctx_loaded, 16)
                sp.dma_start(mask_i[:, :], A["mask"][:, bass.ds(g * GT + GT, GT)]).then_inc(mask_loaded, 16)
                sp.wait_ge(xn_ready, g * NLN + NLN)
                sp.dma_start(A["out"][:, bass.ds(g * T, T), :], out_sb[:, :, :]).then_inc(out_stored, 16)
                sp.wait_ge(out_stored, g * 16 + 16)
                sp.sem_inc(out_free, 1)
            sp.wait_ge(xn_ready, G * NLN)
            sp.dma_start(A["out"][:, SEQS - T:SEQS, :], out_sb[:, :, :]).then_inc(out_stored, 16)
            sp.wait_ge(out_stored, 16 * G)

        @block.scalar
        def _(act):
            for dst, src in LOADS:
                act.dma_start(dst, src).then_inc(weights_loaded, 16)
            for n in range(G):
                act.wait_ge(zrow_mm, n + 1)
                nc.scalar.activation(zpot_row[:, n * GT:(n + 1) * GT], bank[n % 2][0:2, :],
                                     ACT.Copy).then_inc(zrow_copied, 1)
            act.wait_ge(z_ready, 1)
            nc.scalar.activation(zabs[:, :], zpot[:, 1, :], ACT.Abs).then_inc(abs_done, 1)
            act.wait_ge(abs_done, 1)
            nc.scalar.activation(zln[:, :], zabs[:, :], ACT.Exp, scale=-1.0).then_inc(exp_done, 1)
            act.wait_ge(exp_done, 1)
            nc.scalar.activation(zabs[:, :], zln[:, :], ACT.Ln, bias=1.0).then_inc(zln_ready, 1)
            act.wait_ge(bias_ready, 4)
            act.wait_ge(folded, 9)

            with act.Fori(0, G) as g:
                def drain(name, dst, func=ACT.Copy, bias=None, scale=1.0, src=None):
                    b = filled(act, g, name)
                    src_ap = b[:, :] if src is None else src(b)
                    kw = {} if bias is None else {"bias": bias}
                    nc.scalar.activation(dst, src_ap, func, scale=scale, **kw).then_inc(
                        free[BANK[name]], 1)

                drain("xh2T", xnT[:, :])
                drain("decay", decay[:, :, :].rearrange("p t n -> p (t n)"), ACT.Exp, scale=-DT)
                for p in range(PAIRS):
                    drain(f"q{p}", qT[:, p, :], ACT.Identity, bias=bg_qk[:, p:p + 1])
                for t in range(T):
                    drain(f"hpv{t}", hebT[t % 2][:, :, :].rearrange("p a n -> p (a n)"))
                def split(name, which, c, full, bias, high_ready, split_ready):
                    b = filled(act, g, name)
                    if c >= 2:
                        act.wait_ge(split_ready, g * XC + c - 1)
                    elif name[0] == "q":
                        act.wait_ge(kr_ready, g * XC + c + 3)
                    nc.scalar.activation(high[c % 2][:, :], b[:, :], ACT.Identity, bias=bias
                                         ).then_inc(high_ready, 1)
                    nc.scalar.activation(full, b[:, :], ACT.Identity, bias=bias
                                         ).then_inc(free[BANK[name]], 1)

                for c in range(XC):
                    split(f"kp{c}", 1, c, kp[:, c, :], bk_pad[:, c:c + 1], khigh_ready, kr_ready)
                drain("cv", vpad[:, :, :, 0:XD].rearrange("p t h d -> p (t h) d"),
                      src=lambda b: b[:, :].rearrange("p (n d) -> p n d", d=XD))
                drain("xh3T", xnT[:, :])
                for c in range(FC):
                    drain(f"ff1c{c}", hT[0][:, c, :], ACT.Gelu_apprx_tanh, bias=bg_ff1[:, c:c + 1])
                drain("xaT", xnT[:, :])
                for c in range(XC):
                    split(f"qp{c}", 0, c, qp[:, c, :], bq_pad[:, c:c + 1], qhigh_ready, qr_ready)
                for t in range(T):
                    for i in range(4):
                        drain(f"st{t}i{i}", pT[t % 2][:, i, :, :].rearrange("p c n -> p (c n)"), ACT.Exp)
                    drain(f"xpv{t}", cT[t % 2][:, :, :].rearrange("p c n -> p (c n)"))
                drain("cxT", cxT[:, :])
                drain("xbT", xnT[:, :])
                act.wait_ge(lsh_ready, g + 1)
                nc.scalar.activation(lex[:, :, :], lsh[:, :, :], ACT.Exp).then_inc(lex_ready, 1)
                drain("wT", gateT[:, :], src=lambda b: b[0:EXP, :])
                for e in range(EXP):
                    for c in range(FC):
                        drain(f"h{e}c{c}", hT[e % 2][:, c, :], ACT.Gelu, bias=b1_c[:, e, c:c + 1])

        @block.gpsimd
        def _(pool):
            nc.gpsimd.memset(ones[:, :], 1.0).then_inc(pool_const, 1)
            nc.gpsimd.memset(mean_w[:, :], 1.0 / P).then_inc(pool_const, 1)
            nc.gpsimd.memset(minus_half[:, :], -0.5).then_inc(pool_const, 1)
            nc.gpsimd.memset(Y[:, 0:2, :, :, :], 0.0).then_inc(pool_const, 1)
            nc.gpsimd.memset(S[:, 0, :], 0.0).then_inc(pool_const, 1)
            nc.gpsimd.memset(vpad[:, :, :, :], 0.0).then_inc(pool_const, 1)
            for n in range(2):
                nc.gpsimd.memset(negmax[n][:, :, :], 0.0).then_inc(pool_const, 1)
            pool.wait_ge(pool_const, 8)
            nc.gpsimd.memset(Y[:, 0, 0, 0, :], 1.0).then_inc(pool_const, 1)
            nc.gpsimd.memset(Y[:, 1, 1, 0, :], 1.0).then_inc(pool_const, 1)
            nc.gpsimd.memset(S[:, 0, 2:3], 1.0).then_inc(pool_const, 1)
            nc.gpsimd.memset(vpad[:, :, :, XD:XD + 1], 1.0).then_inc(pool_const, 1)
            pool.wait_ge(mv1_ready, 1)
            nc.gpsimd.tensor_scalar(rstd1[:, :], mv1[:, :, 1], EPS, None, ALU.add).then_inc(vare1_ready, 1)
            pool.wait_ge(vare1_ready, 1)
            nc.gpsimd.tensor_tensor(rstd1[:, :], rstd1[:, :], minus_half[:, :], ALU.pow
                                    ).then_inc(rstd1_ready, 1)
            pool.wait_ge(weights_loaded, 16 * len(LOADS))
            nc.gpsimd.tensor_copy(ident_b[:, :], ident[:, :]).then_inc(folded, 1)
            nc.gpsimd.tensor_copy(future_b[:, :], future[:, :]).then_inc(folded, 1)
            nc.gpsimd.tensor_copy(pos_only_b[:, :], pos_only[:, :]).then_inc(folded, 1)
            pool.wait_ge(green_ready, 1)
            for q in range(4):
                pool.wait_ge(x_loaded[q], 16)

            with pool.Fori(0, G) as g:
                def ln_scale(stage, t):
                    n = stage * T + t
                    pool.wait_ge(mv_ready, g * NLN + n + 1)
                    pool.sem_inc(pool_held, 1)
                    nc.gpsimd.tensor_scalar(vare[:, t:t + 1], mv[:, t, 1:2], EPS, None, ALU.add
                                            ).then_inc(vare_ready, 1)
                    pool.wait_ge(vare_ready, g * NLN + n + 1)
                    nc.gpsimd.tensor_tensor(rstd[:, t:t + 1], vare[:, t:t + 1], minus_half[:, 0:1],
                                            ALU.pow).then_inc(rstd_ready, 1)

                pool.wait_ge(mask_loaded, g * 16 + 16)
                pool.sem_inc(pool_held, 1)
                nc.gpsimd.tensor_copy(mask_b[:, :], mask_i[:, :]).then_inc(maskb_ready, 1)
                nc.gpsimd.tensor_tensor(
                    xbk[:, :, :], x_all[:, bass.ds(g * T, T), :],
                    b_bk_bc[:, :].unsqueeze(1).broadcast_to([P, T, P]), ALU.add).then_inc(xbk_ready, 1)
                nc.gpsimd.tensor_tensor(
                    cumg[:, :, :], gamma[:, bass.ds(g * T, T)].unsqueeze(2).broadcast_to([P, T, P]),
                    tri[:, :].unsqueeze(1).broadcast_to([P, T, P]), ALU.mult).then_inc(cumg_ready, 1)
                for t in range(T):
                    ln_scale(LN2, t)
                nc.gpsimd.tensor_tensor(
                    x1b[:, :, :], x1[:, :, :],
                    b_out_bc[:, :].unsqueeze(1).broadcast_to([P, T, P]), ALU.add).then_inc(x1b_ready, 1)
                nc.gpsimd.tensor_tensor(
                    xf[:, :, :], x_all[:, bass.ds(g * T, T), :],
                    b_ff2_bc[:, :].unsqueeze(1).broadcast_to([P, T, P]), ALU.add).then_inc(xf_ready, 1)
                for t in range(T):
                    ln_scale(LN3, t)
                pool.wait_ge(xf_ready, g + 1)
                nc.gpsimd.tensor_tensor(xsum[:, :, :], xf[:, :, :], x2[:, :, :], ALU.add
                                        ).then_inc(xsum_ready, 1)
                for t in range(T):
                    ln_scale(LNA, t)
                pool.wait_ge(xn_ready, g * NLN + (LNA + 1) * T)
                nc.gpsimd.tensor_tensor(
                    xab[:, :, :], xa[:, :, :],
                    bo_bc[:, :].unsqueeze(1).broadcast_to([P, T, P]), ALU.add).then_inc(xab_ready, 1)
                for t in range(T):
                    ln_scale(LNB, t)
                for t in range(T):
                    ln_scale(LNC, t)

        @block.vector
        def _(dve):
            dve.wait_ge(pre_loaded, 16 * len(PRE_LOADS))
            dve.wait_ge(pool_const, 12)
            nc.vector.tensor_scalar(w_potg[:, :], w_pot[:, :], ln1_g[:, 0:1], None, ALU.mult
                                    ).then_inc(wpotg_ready, 1)
            nc.vector.tensor_scalar(lnb_cols[:, 0, :], ones[:, :], ln1_b[:, 0:1], None, ALU.mult
                                    ).then_inc(lnb_ready, 1)
            dve.wait_ge(wmean_mm, 1)
            nc.vector.tensor_tensor(w_potc[:, :], w_potg[:, :], bank[2][:, 0:2], ALU.subtract
                                    ).then_inc(wpotc_ready, 1)
            dve.wait_ge(potbias_mm, 1)
            nc.vector.tensor_copy(pot_bias[:, :], bank[3][:, 0:2]).then_inc(potbias_ready, 1)
            for q in range(4):
                dve.wait_ge(x_loaded[q], 16)
                for n in range(8 * q, 8 * q + 8):
                    nc.vector.bn_stats(st1[:, n, :], x_all[:, n, :]).then_inc(bn1_ready, 1)
            dve.wait_ge(bn1_ready, SEQS)
            for n in range(SEQS):
                last = nc.vector.bn_aggr(mv1[:, n, :], st1[:, n, :])
            last.then_inc(mv1_ready, 1)
            dve.wait_ge(zpos_mm, 1)
            dve.wait_ge(rstd1_ready, 1)
            dve.wait_ge(potbias_ready, 1)
            nc.vector.tensor_tensor(
                zpot[:, :, :], bank[4][:, 0:2 * SEQS].rearrange("p (a s) -> p a s", a=2),
                rstd1[:, :].unsqueeze(1).broadcast_to([P, 2, SEQS]), ALU.mult).then_inc(zlink, 1)
            dve.wait_ge(zlink, 1)
            nc.vector.tensor_scalar(zpot[:, 1, :], zpot[:, 1, :], pot_bias[:, 1:2], None, ALU.add
                                    ).then_inc(z_ready, 1)
            nc.vector.tensor_scalar(diag[:, 0, :], zpot[:, 0, :], pot_bias[:, 0:1], 2.0, ALU.add,
                                    ALU.add).then_inc(zlink, 1)
            dve.wait_ge(zln_ready, 1)
            dve.wait_ge(z_ready, 1)
            nc.vector.scalar_tensor_tensor(out=gamma[:, :], in0=zpot[:, 1, :], scalar=0.0,
                                           in1=zabs[:, :], op0=ALU.max, op1=ALU.add).then_inc(zlink, 1)
            dve.wait_ge(zlink, 3)
            nc.vector.tensor_scalar(diag[:, 1, :], gamma[:, :], GAMMA_FLOOR, -1.0, ALU.add, ALU.mult
                                    ).then_inc(zlink, 1)
            dve.wait_ge(zlink, 4)
            nc.vector.tensor_scalar(gamma[:, :], gamma[:, :], GAMMA_FLOOR, None, ALU.add
                                    ).then_inc(gamma_ready, 1)

            links = [0]

            def link(ins):
                links[0] += 1
                ins.then_inc(scan_link, 1)
                dve.wait_ge(scan_link, links[0])

            dve.wait_ge(drow_mm, 1)
            rows = 2 * SEQS
            link(nc.vector.tensor_copy(d_row[:, :, :].rearrange("p a n -> p (a n)"), bank[5][0:rows, 0:2 * P]))
            link(nc.vector.tensor_scalar(di_sign[:, 0, :], d_row[:, 1, :], -1.0, None, ALU.mult))
            link(nc.vector.tensor_copy(di_sign[:, 1, :], d_row[:, 1, :]))
            dre = d_row[:, 0, :].rearrange("p (c j) -> p c j", j=CL)
            dim = di_sign[:, :, :].rearrange("p a (c j) -> p a c j", j=CL)
            for j in range(CL):
                y1 = Y[:, j + 1, :, :, :]
                link(nc.vector.tensor_tensor(
                    Ya[:, :, :, :].rearrange("p a b c -> p (a b) c"), y1.rearrange("p a b c -> p (a b) c"),
                    dre[:, :, j].unsqueeze(1).broadcast_to([rows, 4, CN]), ALU.mult))
                link(nc.vector.tensor_tensor(
                    Yb[:, :, :, :], y1[:, :, ::-1, :],
                    dim[:, :, :, j].unsqueeze(1).broadcast_to([rows, 2, 2, CN]), ALU.mult))
                link(nc.vector.tensor_tensor(Yc[:, :, :, :], Ya[:, :, :, :], Y[:, j, :, :, :], ALU.subtract))
                link(nc.vector.tensor_tensor(Y[:, j + 2, :, :, :], Yc[:, :, :, :], Yb[:, :, :, :], ALU.add))
            for out_j in range(2):
                yj = Y[:, CL + out_j, :, :, :]
                for out_r, in_r, part, sign in ((0, 0, 0, 1.0), (0, 1, 1, -1.0), (1, 0, 1, 1.0), (1, 1, 0, 1.0)):
                    link(nc.vector.tensor_scalar(
                        C[:, :, out_j, out_r, in_r:in_r + 3:2].rearrange("p c a -> p a c"),
                        yj[:, :, part, :], sign, None, ALU.mult))
            Cf = C[:, :, :, :, :].rearrange("p c a b n -> p c (a b n)")
            link(nc.vector.tensor_reduce(cmax[:, :], Cf, AX.X, ALU.max, apply_absolute_value=True))
            link(nc.vector.reciprocal(crec[:, :], cmax[:, :]))
            link(nc.vector.tensor_tensor(Cs[:, :, :], Cf, crec[:, :].unsqueeze(2).broadcast_to([rows, CN, 16]),
                                         ALU.mult))
            for c in range(CN - 1):
                link(nc.vector.tensor_tensor(
                    Sp[:, :, :], Cs[:, c, :].rearrange("p (o n) -> p o n", o=4),
                    S[:, c, :].unsqueeze(1).broadcast_to([rows, 4, 4]), ALU.mult))
                link(nc.vector.tensor_reduce(S[:, c + 1, :], Sp[:, :, :], AX.X, ALU.add))
            Sc = S[:, 0:CN, :].rearrange("p c (a b) -> p a b c", a=2)
            link(nc.vector.tensor_copy(Sa[:, :, 0, :], Sc[:, :, 0, :]))
            link(nc.vector.tensor_scalar(Sa[:, :, 1, :], Sc[:, :, 1, :], -1.0, None, ALU.mult))
            link(nc.vector.tensor_copy(Sb[:, :, 0, :], Sc[:, :, 1, :]))
            link(nc.vector.tensor_copy(Sb[:, :, 1, :], Sc[:, :, 0, :]))
            Yf = Y[:, 1:CL + 2, :, :, :].rearrange("p j a b c -> p j (a b c)")
            for Sx, Zx, Px in ((Sa, Z, Pr), (Sb, Zb, Pi)):
                link(nc.vector.tensor_tensor(
                    Zx[:, :, :, :].rearrange("p j n c -> p j (n c)"), Yf,
                    Sx[:, :, :, :].rearrange("p a b c -> p (a b c)").unsqueeze(1).broadcast_to(
                        [rows, CL + 1, 4 * CN]), ALU.mult))
                link(nc.vector.tensor_reduce(Px[:, :, :].rearrange("p c j -> p j c"),
                                             Zx[:, :, :, :].rearrange("p j n c -> p j c n"), AX.X, ALU.add))
            pr1, pi1 = Pr[:, :, 1:CL + 1], Pi[:, :, 1:CL + 1]
            pr0, pi0 = Pr[:, :, 0:CL], Pi[:, :, 0:CL]

            def v3(buf):
                return buf[:, :].rearrange("p (c j) -> p c j", j=CL)

            link(nc.vector.tensor_tensor(v3(ra), pr0, pr0, ALU.mult))
            link(nc.vector.tensor_tensor(v3(rb), pi0, pi0, ALU.mult))
            link(nc.vector.tensor_tensor(rc[:, :], ra[:, :], rb[:, :], ALU.add))
            link(nc.vector.reciprocal(rd[:, :], rc[:, :]))
            for part, (p0, q0, p1, q1, op) in enumerate(((pr1, pr0, pi1, pi0, ALU.add),
                                                         (pi1, pr0, pr1, pi0, ALU.subtract))):
                link(nc.vector.tensor_tensor(v3(ra), p0, q0, ALU.mult))
                link(nc.vector.tensor_tensor(v3(rb), p1, q1, ALU.mult))
                link(nc.vector.tensor_tensor(rc[:, :], ra[:, :], rb[:, :], op))
                link(nc.vector.tensor_tensor(frac[0:SEQS, part, :], rc[0:SEQS, :], rd[0:SEQS, :], ALU.mult))
                link(nc.vector.tensor_tensor(frac[SEQS:rows, part, ::-1], rc[SEQS:rows, :], rd[SEQS:rows, :],
                                             ALU.mult))
            nc.vector.tensor_scalar(neg_id[:, :], ident[0:SEQS, 0:SEQS], -1.0, None, ALU.mult
                                    ).then_inc(frac_ready, 1)
            dve.wait_ge(den_mm, 1)
            link(nc.vector.tensor_copy(den[:, :, :].rearrange("p a s -> p (a s)"), bank[6][:, 0:2 * SEQS]))
            link(nc.vector.tensor_tensor(ga[:, :], den[:, 0, :], den[:, 0, :], ALU.mult))
            link(nc.vector.tensor_tensor(gb[:, :], den[:, 1, :], den[:, 1, :], ALU.mult))
            link(nc.vector.tensor_tensor(ga[:, :], ga[:, :], gb[:, :], ALU.add))
            link(nc.vector.reciprocal(gb[:, :], ga[:, :]))
            link(nc.vector.tensor_tensor(green[:, 0, :], den[:, 0, :], gb[:, :], ALU.mult))
            nc.vector.scalar_tensor_tensor(out=green[:, 1, :], in0=den[:, 1, :], scalar=-1.0,
                                           in1=gb[:, :], op0=ALU.mult, op1=ALU.mult).then_inc(green_ready, 1)

            dve.wait_ge(weights_loaded, 16 * len(LOADS))
            nc.vector.tensor_scalar(w_out[:, :, :], w_out[:, :, :], ETA, None, ALU.mult).then_inc(folded, 1)
            nc.vector.tensor_scalar(wq_pad[:, :, :], wq_pad[:, :, :], XSCALE, None, ALU.mult).then_inc(folded, 1)
            nc.vector.scalar_tensor_tensor(out=bq_pad[:, :], in0=bq_pad[:, :], scalar=XSCALE, in1=q_ones[:, :],
                                           op0=ALU.mult, op1=ALU.add).then_inc(folded, 1)
            nc.vector.tensor_tensor(bk_pad[:, :], bk_pad[:, :], k_ones[:, :], ALU.add).then_inc(folded, 1)
            nc.vector.tensor_scalar(lnb_cols[:, 1, :], ones[:, :], ln2_b[:, 0:1], None, ALU.mult
                                    ).then_inc(lnb_ready, 1)
            nc.vector.tensor_scalar(lnb_cols[:, 2, :], ones[:, :], bv_col[:, 0:1], None, ALU.mult
                                    ).then_inc(lnb_ready, 1)
            dve.wait_ge(bias_mm, 1)
            nc.vector.tensor_tensor(bg_qk[:, :], bank[7][:, 0:2 * PAIRS], b_qk[:, :], ALU.add
                                    ).then_inc(bias_ready, 1)
            dve.wait_ge(bias_mm, 2)
            nc.vector.tensor_copy(bg_v[:, :], bank[2][:, :]).then_inc(bias_ready, 1)
            dve.wait_ge(bias_mm, 3)
            nc.vector.tensor_tensor(bg_ff1[:, :], bank[3][:, 0:FC], b_ff1[:, :], ALU.add).then_inc(bias_ready, 1)
            dve.wait_ge(bias_mm, 4)
            nc.vector.tensor_copy(bo_bc[:, :], bank[4][:, 0:P]).then_inc(bias_ready, 1)
            nc.vector.tensor_scalar(w_qkv[:, :], w_qkv[:, :], ln2_g[:, 0:1], None, ALU.mult).then_inc(folded, 1)
            nc.vector.tensor_scalar(w_ff1[:, :], w_ff1[:, :], ln3_g[:, 0:1], None, ALU.mult).then_inc(folded, 1)

            dve.sem_inc(out_free, 1)
            with dve.Fori(0, G) as g:
                def ln_stats(stage, t, src):
                    n = stage * T + t
                    dve.wait_ge(sum_ready, g * NLN + n + 1)
                    nc.vector.bn_stats(stats[:, t, :], src).then_inc(bn_ready, 1)
                    dve.wait_ge(bn_ready, g * NLN + n + 1)
                    dve.sem_inc(dve_held, 1)
                    nc.vector.bn_aggr(mv[:, t, :], stats[:, t, :]).then_inc(mv_ready, 1)

                def ln_apply(stage, t, src, dst):
                    dve.wait_ge(rstd_ready, g * NLN + stage * T + t + 1)
                    nc.vector.tensor_scalar(dst, src, mv[:, t, 0:1], rstd[:, t:t + 1], ALU.subtract,
                                            ALU.mult).then_inc(xn_ready, 1)

                dve.wait_ge(xbk_ready, g + 1)
                for t in range(T):
                    nc.vector.scalar_tensor_tensor(
                        out=x1[:, t, :], in0=w_bk_bc[:, 0, :], scalar=green[:, 0, bass.ds(g * T + t, 1)],
                        in1=xbk[:, t, :], op0=ALU.mult, op1=ALU.add).then_inc(x1_part, 1)
                for t in range(T):
                    dve.wait_ge(x1_part, g * T + t + 1)
                    nc.vector.scalar_tensor_tensor(
                        out=x1[:, t, :], in0=w_bk_bc[:, 1, :], scalar=green[:, 1, bass.ds(g * T + t, 1)],
                        in1=x1[:, t, :], op0=ALU.mult, op1=ALU.add).then_inc(sum_ready, 1)
                    ln_stats(LN2, t, x1[:, t, :])
                for t in range(T):
                    ln_apply(LN2, t, x1[:, t, :], xn[:, t, :])
                for p in range(PAIRS):
                    b = filled(dve, g, f"k{p}")
                    nc.vector.tensor_scalar(kT[:, p, :], b[:, :], bg_qk[:, PAIRS + p:PAIRS + p + 1], None,
                                            ALU.add).then_inc(free[BANK[f"k{p}"]], 1)

                def values(t):
                    b = filled(dve, g, f"v{t}")
                    nc.vector.tensor_tensor(v_sb[:, t, :], b[:, :], bg_v[:, :], ALU.add
                                            ).then_inc(free[BANK[f"v{t}"]], 1)

                def decayed(t):
                    if t == 0:
                        drained(dve, g, "decay")
                    for r in range(2):
                        b = filled(dve, g, f"at{t}r{r}")
                        nc.vector.tensor_tensor(
                            at[t % 2][:, r, :, :], b[:, :].rearrange("p (a n) -> p a n", a=PAIRS),
                            decay[:, t, :].unsqueeze(1).broadcast_to([P, PAIRS, P]), ALU.mult
                        ).then_inc(free[BANK[f"at{t}r{r}"]], 1)

                def heb_sum(t):
                    if t == 0:
                        dve.wait_ge(x1b_ready, g + 1)
                    b = filled(dve, g, f"wo{t}")
                    nc.vector.tensor_tensor(x2[:, t, :], b[:, 0:P], x1b[:, t, :], ALU.add
                                            ).then_inc(free[BANK[f"wo{t}"]], 1)
                    drained(dve, g, f"wo{t}")
                    dve.sem_inc(sum_ready, 1)
                    ln_stats(LN3, t, x2[:, t, :])

                values(0)
                values(1)
                decayed(0)
                values(2)
                values(3)
                decayed(1)
                decayed(2)
                heb_sum(0)
                decayed(3)
                heb_sum(1)
                ln_apply(LN3, 0, x2[:, 0, :], xn[:, 0, :])
                heb_sum(2)
                ln_apply(LN3, 1, x2[:, 1, :], xn[:, 1, :])
                heb_sum(3)
                ln_apply(LN3, 2, x2[:, 2, :], xn[:, 2, :])
                ln_apply(LN3, 3, x2[:, 3, :], xn[:, 3, :])

                def split(name, which, c, full, out, high_ready, split_ready):
                    dve.wait_ge(high_ready, g * XC + c + 1)
                    drained(dve, g, name)
                    nc.vector.scalar_tensor_tensor(
                        out=out, in0=high[c % 2][:, :].bitcast(F32),
                        scalar=low_rows[:, which:which + 1], in1=full, op0=ALU.mult, op1=ALU.add
                    ).then_inc(split_ready, 1)

                for c in range(XC):
                    split(f"kp{c}", 1, c, kp[:, c, :], kr[:, c, :], khigh_ready, kr_ready)

                def residual(stage, name, t, dst, other):
                    b = filled(dve, g, name)
                    nc.vector.tensor_tensor(dst, b[:, 0:P], other, ALU.add).then_inc(free[BANK[name]], 1)
                    drained(dve, g, name)
                    dve.sem_inc(sum_ready, 1)
                    ln_stats(stage, t, dst)

                dve.wait_ge(xsum_ready, g + 1)
                for t in range(T):
                    residual(LNA, f"ff2t{t}", t, x2[:, t, :], xsum[:, t, :])
                for t in range(T):
                    ln_apply(LNA, t, x2[:, t, :], xa[:, t, :])

                def maxima(t):
                    for i in range(4):
                        b = filled(dve, g, f"mx{t}i{i}")
                        nc.vector.tensor_reduce(
                            negmax[t % 2][:, i, 28:28 + XC], b[:, :].rearrange("p (c n) -> p c n", c=XC),
                            AX.X, ALU.max, negate=True).then_inc(free[BANK[f"mx{t}i{i}"]], 1)
                    b = filled(dve, g, f"mT{t}")
                    nc.vector.tensor_tensor(
                        qm[t % 2][:, :, :], b[:, 0:P].unsqueeze(1).broadcast_to([P, XC, P]),
                        qr[:, :, t * P:(t + 1) * P].bitcast(F32), ALU.add).then_inc(free[BANK[f"mT{t}"]], 1)

                def normalise(t):
                    b = filled(dve, g, f"ctT{t}")
                    heads = b[:, :].rearrange("p (h n) -> p h n", n=32)
                    nc.vector.reciprocal(rsum[:, t, :], heads[:, :, XD]).then_inc(rsum_ready, 1)
                    dve.wait_ge(rsum_ready, g * T + t + 1)
                    nc.vector.tensor_tensor(
                        cx[:, t, :, :], heads[:, :, 0:XD],
                        rsum[:, t, :].unsqueeze(2).broadcast_to([P, XH, XD]), ALU.mult
                    ).then_inc(free[BANK[f"ctT{t}"]], 1)

                for c in range(XC):
                    split(f"qp{c}", 0, c, qp[:, c, :], qr[:, c, :], qhigh_ready, qr_ready)
                maxima(0)
                for t in range(T):
                    if t + 1 < T:
                        maxima(t + 1)
                    normalise(t)
                dve.wait_ge(xab_ready, g + 1)
                for t in range(T):
                    residual(LNB, f"xo{t}", t, x2[:, t, :], xab[:, t, :])
                for t in range(T):
                    ln_apply(LNB, t, x2[:, t, :], xb[:, t, :])

                b = filled(dve, g, "rl")
                nc.vector.tensor_copy(lg[:, :, :].rearrange("p t e -> p (t e)"), b[:, 0:T * EXP]
                                      ).then_inc(free[BANK["rl"]], 1)
                drained(dve, g, "rl")
                dve.sem_inc(dve_held, 1)
                for t in range(T):
                    nc.vector.max(top8[:, t, :], lg[:, t, :]).then_inc(gate_link, 1)
                dve.wait_ge(gate_link, g * 8 + 4)
                nc.vector.tensor_tensor(lsh[:, :, :], lg[:, :, :], top8[:, :, 0:1].broadcast_to([P, T, EXP]),
                                        ALU.subtract).then_inc(lsh_ready, 1)
                nc.vector.tensor_tensor(keep[:, :, :], lg[:, :, :], top8[:, :, 1:2].broadcast_to([P, T, EXP]),
                                        ALU.is_ge).then_inc(gate_link, 1)
                dve.wait_ge(gate_link, g * 8 + 5)
                dve.wait_ge(lex_ready, g + 1)
                nc.vector.tensor_tensor(wraw[:, :, :], lex[:, :, :], keep[:, :, :], ALU.mult
                                        ).then_inc(gate_link, 1)
                dve.wait_ge(gate_link, g * 8 + 6)
                nc.vector.tensor_reduce(wsum[:, :], wraw[:, :, :], AX.X, ALU.add).then_inc(gate_link, 1)
                dve.wait_ge(gate_link, g * 8 + 7)
                nc.vector.reciprocal(wrec[:, :], wsum[:, :]).then_inc(gate_link, 1)
                dve.wait_ge(gate_link, g * 8 + 8)
                nc.vector.tensor_tensor(gate[:, :, :], wraw[:, :, :],
                                        wrec[:, :].unsqueeze(2).broadcast_to([P, T, EXP]), ALU.mult
                                        ).then_inc(gate_ready, 1)
                dve.wait_ge(gate_ready, g + 1)
                b = filled(dve, g, "by")
                nc.vector.tensor_tensor(acc[:, :, :].rearrange("p t n -> p (t n)"), b[:, :],
                                        xb[:, :, :].rearrange("p t n -> p (t n)"), ALU.add
                                        ).then_inc(free[BANK["by"]], 1)
                drained(dve, g, "by")
                for e in range(EXP):
                    b = filled(dve, g, f"y{e}")
                    if e:
                        drained(dve, g, f"y{e - 1}")
                    for t in range(T):
                        ins = nc.vector.scalar_tensor_tensor(
                            out=acc[:, t, :], in0=b[:, t * P:(t + 1) * P], scalar=gate[:, t, e:e + 1],
                            in1=acc[:, t, :], op0=ALU.mult, op1=ALU.add)
                    ins.then_inc(free[BANK[f"y{e}"]], 1)
                drained(dve, g, f"y{EXP - 1}")
                for t in range(T):
                    dve.sem_inc(sum_ready, 1)
                    ln_stats(LNC, t, acc[:, t, :])
                dve.wait_ge(out_free, g + 1)
                for t in range(T):
                    ln_apply(LNC, t, acc[:, t, :], out_sb[:, t, :])
                dve.wait_ge(xn_ready, g * NLN + NLN)

        @block.tensor
        def _(pe):
            mm = nc.tensor.matmul
            pe.wait_ge(pre_loaded, 16 * len(PRE_LOADS))
            pe.wait_ge(pool_const, 12)
            pe.wait_ge(wpotg_ready, 1)
            mm(bank[2][:, 0:2], mean_w[:, :], w_potg[:, :], start=True, stop=True).then_inc(wmean_mm, 1)
            pe.wait_ge(lnb_ready, 1)
            mm(bank[3][:, 0:2], lnb_cols[:, 0, :], w_pot[:, :], start=True, stop=False)
            mm(bank[3][:, 0:2], ones[0:1, :], b_pot[:, :], start=False, stop=True).then_inc(potbias_mm, 1)
            pe.wait_ge(wpotc_ready, 1)
            for n in range(G):
                if n >= 2:
                    pe.wait_ge(zrow_copied, n - 1)
                mm(bank[n % 2][0:2, :], w_potc[:, :], xT_all[:, n * GT:(n + 1) * GT], start=True,
                   stop=True).then_inc(zrow_mm, 1)
            pe.wait_ge(zseq_loaded, 32)
            nc.tensor.transpose(bank[4][:, 0:2 * SEQS], zpot_seq[:, :], ident[0:2 * SEQS, 0:2 * SEQS]
                                ).then_inc(zpos_mm, 1)
            pe.wait_ge(zlink, 4)
            for part in range(2):
                for way, perm in enumerate((ident, antid)):
                    last = mm(bank[5][SEQS * way:SEQS * way + SEQS, P * part:P * part + P],
                              diag[:, part, :], perm[:, :], start=True, stop=True)
            last.then_inc(drow_mm, 1)
            pe.wait_ge(frac_ready, 1)
            for part in range(2):
                o = bank[6][:, SEQS * part:SEQS * part + SEQS]
                mm(o, frac[0:2 * SEQS, part, :], fold_id[:, :], start=True, stop=False)
                last = mm(o, d_row[0:SEQS, part, :], neg_id[:, :], start=False, stop=True)
            last.then_inc(den_mm, 1)
            pe.wait_ge(weights_loaded, 16 * len(LOADS))
            for j in range(2 * PAIRS):
                last = mm(bank[7][:, j:j + 1], w_qkv[:, j * P:(j + 1) * P], ln2_b[:, :], start=True, stop=True)
            last.then_inc(bias_mm, 1)
            pe.wait_ge(lnb_ready, 3)
            mm(bank[2][:, :], lnb_cols[:, 1, :], w_qkv[:, 2 * FF:3 * FF], start=True, stop=False)
            mm(bank[2][:, :], ones[0:1, :], b_v_row[:, :], start=False, stop=True).then_inc(bias_mm, 1)
            for j in range(FC):
                last = mm(bank[3][:, j:j + 1], w_ff1[:, j * P:(j + 1) * P], ln3_b[:, :], start=True, stop=True)
            last.then_inc(bias_mm, 1)
            mm(bank[4][:, 0:P], lnb_cols[:, 2, :], wo_t[:, :], start=True, stop=False)
            mm(bank[4][:, 0:P], ones[0:1, :], bo_row[:, :], start=False, stop=True).then_inc(bias_mm, 1)
            pe.wait_ge(bias_ready, 4)
            pe.wait_ge(folded, 9)
            for b in range(NB):
                pe.sem_inc(free[b], 1)

            with pe.Fori(0, G) as g:
                def done(ins, name):
                    ins.then_inc(full[BANK[name]], 1)

                def turn(name, stage, src):
                    for t in range(T):
                        pe.wait_ge(xn_ready, g * NLN + stage * T + t + 1)
                        if t == 0:
                            b = take(pe, g, name)
                        ins = nc.tensor.transpose(b[:, t * P:(t + 1) * P], src[:, t, :], ident[:, :])
                    done(ins, name)

                def wide(name, lhsT, rhs):
                    b = take(pe, g, name)
                    done(mm(b[:, :], lhsT, rhs, start=True, stop=True), name)

                turn("xh2T", LN2, xn)
                pe.wait_ge(cumg_ready, g + 1)
                b = take(pe, g, "decay")
                mm(b[:, :], after[:, :], cumg[:, :, :].rearrange("p t n -> p (t n)"), start=True, stop=True)
                for t in range(T):
                    ins = mm(b[:, t * P:(t + 1) * P], ident_b[:, :], future_b[:, :], start=False,
                             stop=True, skip_group_check=True)
                done(ins, "decay")
                drained(pe, g, "xh2T")
                for p in range(PAIRS):
                    wide(f"q{p}", w_qkv[:, p * P:(p + 1) * P], xnT[:, :])
                    wide(f"k{p}", w_qkv[:, FF + p * P:FF + (p + 1) * P], xnT[:, :])

                def tile(t):
                    return slice(t * P, (t + 1) * P)

                def values(t):
                    wide(f"v{t}", xnT[:, tile(t)], w_qkv[:, 2 * FF:3 * FF])

                def scores(t):
                    if t == 0:
                        for p in range(PAIRS):
                            drained(pe, g, f"q{p}")
                            drained(pe, g, f"k{p}")
                    for r in range(2):
                        b = take(pe, g, f"at{t}r{r}")
                        rows = slice(HD * r, HD * r + HD)
                        for p in range(PAIRS):
                            ins = mm(b[:, tile(p)], kT[rows, p, tile(t)], qT[rows, p, tile(t)],
                                     start=True, stop=True)
                        done(ins, f"at{t}r{r}")

                def weigh(t):
                    drained(pe, g, f"v{t}")
                    b = take(pe, g, f"hpv{t}")
                    for r in range(2):
                        drained(pe, g, f"at{t}r{r}")
                        for p in range(PAIRS):
                            h = 2 * p + r
                            ins = mm(b[HD * r:HD * r + HD, tile(p)], v_sb[:, t, h * HD:(h + 1) * HD],
                                     at[t % 2][:, r, p, :], start=True, stop=True)
                    done(ins, f"hpv{t}")

                def heb_out(t):
                    drained(pe, g, f"hpv{t}")
                    b = take(pe, g, f"wo{t}")
                    for p in range(PAIRS):
                        ins = mm(b[:, 0:P], hebT[t % 2][:, p, :], w_out[:, p, :], start=(p == 0),
                                 stop=(p == PAIRS - 1))
                    done(ins, f"wo{t}")

                values(0)
                values(1)
                scores(0)
                values(2)
                values(3)
                scores(1)
                weigh(0)
                scores(2)
                weigh(1)
                heb_out(0)
                scores(3)
                weigh(2)
                heb_out(1)
                weigh(3)
                heb_out(2)
                heb_out(3)

                pe.wait_ge(ctx_loaded, g * 16 + 16)
                pe.wait_ge(maskb_ready, g + 1)
                for c in range(XC):
                    b = take(pe, g, f"kp{c}")
                    mm(b[:, :], wk_pad[:, c, :], ctxT[:, :], start=True, stop=False)
                    done(mm(b[:, :], pos_only_b[:, :], mask_b[:, :], start=False,
                            stop=True), f"kp{c}")
                b = take(pe, g, "cv")
                for t in range(T):
                    ins = mm(b[:, tile(t)], ctxT[:, tile(t)], wv_t[:, :], start=True, stop=True)
                done(ins, "cv")

                turn("xh3T", LN3, xn)
                drained(pe, g, "xh3T")
                for c in range(FC):
                    wide(f"ff1c{c}", w_ff1[:, tile(c)], xnT[:, :])
                for t in range(T):
                    b = take(pe, g, f"ff2t{t}")
                    for c in range(FC):
                        if t == 0:
                            drained(pe, g, f"ff1c{c}")
                        ins = mm(b[:, 0:P], hT[0][:, c, tile(t)], w_ff2[:, c, :], start=(c == 0),
                                 stop=(c == FC - 1))
                    done(ins, f"ff2t{t}")

                turn("xaT", LNA, xa)
                drained(pe, g, "xaT")
                for c in range(XC):
                    wide(f"qp{c}", wq_pad[:, c, :], xnT[:, :])

                def max_scores(t):
                    if t == 0:
                        pe.wait_ge(qr_ready, g * XC + XC)
                        pe.wait_ge(kr_ready, g * XC + XC)
                    for i in range(4):
                        b = take(pe, g, f"mx{t}i{i}")
                        rows = slice(32 * i, 32 * i + 32)
                        for c in range(XC):
                            ins = mm(b[:, tile(c)], qr[rows, c, tile(t)], kr[rows, c, tile(t)],
                                     start=True, stop=True)
                        done(ins, f"mx{t}i{i}")

                def turn_max(t):
                    for i in range(4):
                        drained(pe, g, f"mx{t}i{i}")
                    b = take(pe, g, f"mT{t}")
                    done(nc.tensor.transpose(b[:, 0:P], negmax[t % 2][:, :, :].rearrange("p i n -> p (i n)"),
                                             ident[:, :]), f"mT{t}")

                def key_scores(t):
                    drained(pe, g, f"mT{t}")
                    for i in range(4):
                        b = take(pe, g, f"st{t}i{i}")
                        rows = slice(32 * i, 32 * i + 32)
                        for c in range(XC):
                            ins = mm(b[:, tile(c)], kr[rows, c, tile(t)], qm[t % 2][rows, c, :],
                                     start=True, stop=True)
                        done(ins, f"st{t}i{i}")

                def attend(t):
                    b = take(pe, g, f"xpv{t}")
                    for i in range(4):
                        drained(pe, g, f"st{t}i{i}")
                        for c in range(XC):
                            ins = mm(b[32 * i:32 * i + 32, tile(c)], vpad[:, t, 4 * c + i, :],
                                     pT[t % 2][:, i, c, :], start=True, stop=True)
                    done(ins, f"xpv{t}")
                    drained(pe, g, f"xpv{t}")
                    b = take(pe, g, f"ctT{t}")
                    for c in range(XC):
                        ins = nc.tensor.transpose(b[:, tile(c)], cT[t % 2][:, c, :], ident[:, :])
                    done(ins, f"ctT{t}")

                max_scores(0)
                turn_max(0)
                for t in range(T):
                    if t + 1 < T:
                        max_scores(t + 1)
                    key_scores(t)
                    if t + 1 < T:
                        turn_max(t + 1)
                    attend(t)
                b = take(pe, g, "cxT")
                for t in range(T):
                    drained(pe, g, f"ctT{t}")
                    ins = nc.tensor.transpose(b[:, tile(t)], cx[:, t, :, :].rearrange("p h d -> p (h d)"),
                                              ident[:, :])
                done(ins, "cxT")
                drained(pe, g, "cxT")
                for t in range(T):
                    b = take(pe, g, f"xo{t}")
                    done(mm(b[:, 0:P], cxT[:, tile(t)], wo_t[:, :], start=True, stop=True), f"xo{t}")

                turn("xbT", LNB, xb)
                drained(pe, g, "xbT")
                b = take(pe, g, "rl")
                for t in range(T):
                    ins = mm(b[:, t * EXP:(t + 1) * EXP], xnT[:, tile(t)], wr_t[:, :], start=True, stop=True)
                done(ins, "rl")
                pe.wait_ge(gate_ready, g + 1)
                b = take(pe, g, "wT")
                for t in range(T):
                    ins = nc.tensor.transpose(b[0:EXP, tile(t)], gate[:, t, :], ident[:, :])
                done(ins, "wT")
                drained(pe, g, "wT")
                b = take(pe, g, "by")
                for t in range(T):
                    ins = mm(b[:, tile(t)], gateT[:, tile(t)], b2_r[:, :], start=True, stop=True)
                done(ins, "by")

                def expert_out(e):
                    b = take(pe, g, f"y{e}")
                    for c in range(FC):
                        drained(pe, g, f"h{e}c{c}")
                    for t in range(T):
                        for c in range(FC):
                            ins = mm(b[:, tile(t)], hT[e % 2][:, c, tile(t)], w2_t[:, e, c, :],
                                     start=(c == 0), stop=(c == FC - 1))
                    done(ins, f"y{e}")

                for e in range(EXP):
                    for c in range(FC):
                        wide(f"h{e}c{c}", w1_t[:, e, tile(c)], xnT[:, :])
                    if e:
                        expert_out(e - 1)
                expert_out(EXP - 1)


def host_layout(inp):
    f = {k: np.asarray(v) for k, v in inp.items()}
    i128 = np.arange(P)
    c = np.ascontiguousarray

    def quadrants(w):
        src = w.reshape(XC, 4, XD, -1)
        dst = np.zeros((XC, 4, 32, src.shape[-1]), w.dtype)
        for n in range(3):
            dst[:, :, n * XD:(n + 1) * XD] = src
        return c(dst.reshape(XC, P, -1).transpose(2, 0, 1))

    row_one = np.zeros((4, 32, XC), np.float32)
    row_one[:, 24, :] = 1.0
    k_one = np.zeros((4, 32, XC), np.float32)
    for n in range(XC):
        k_one[:, 28 + n, n] = 1.0
    pos = np.zeros((1, 4, 32), np.float32)
    pos[:, :, 24] = MASKED
    low = np.zeros((4, 32, 2), np.float32)
    low[:, 16:24, 0] = -1.0
    low[:, 8:16, 1] = -1.0
    b = f["L0_attn_b_qkv"]
    return {
        "x": c(f["x"].transpose(1, 0, 2)), "xT": c(f["x"].reshape(SEQS * P, P).T),
        "ctxT": c(f["ctx_1024"].reshape(SEQS * P, P).T), "mask": c(f["mask_BxS2_ik1"].reshape(1, -1)),
        "w_pot": f["L0_attn_w_pot"], "b_pot": f["L0_attn_b_pot"].reshape(1, 2),
        "ln1_g": f["L0_attn_ln1_g"].reshape(P, 1), "ln1_b": f["L0_attn_ln1_b"].reshape(P, 1),
        "ln2_g": f["L0_attn_ln2_g"].reshape(P, 1), "ln2_b": f["L0_attn_ln2_b"].reshape(P, 1),
        "ln3_g": f["L0_attn_ln3_g"].reshape(P, 1), "ln3_b": f["L0_attn_ln3_b"].reshape(P, 1),
        "ident": np.eye(P, dtype=np.float32), "antid": c(np.eye(P, dtype=np.float32)[::-1]),
        "tri": (i128[:, None] <= i128[None, :]).astype(np.float32),
        "after": (i128[:, None] > i128[None, :]).astype(np.float32),
        "future": (i128[None, :] < i128[:, None]).astype(np.float32) * np.float32(FAR),
        "pos_only": pos.reshape(1, P),
        "fold_id": c(np.tile(np.eye(SEQS, dtype=np.float32), (2, 1))),
        "w_bk": f["L0_attn_w_bk"], "b_bk": f["L0_attn_b_bk"].reshape(1, P),
        "w_qkv": f["L0_attn_w_qkv"], "b_qk": c(b[:2 * FF].reshape(2 * PAIRS, P).T),
        "b_v": c(b[2 * FF:].reshape(1, FF)),
        "w_out": c(f["L0_attn_w_out"].reshape(PAIRS, P, P).transpose(1, 0, 2)),
        "b_out": f["L0_attn_b_out"].reshape(1, P),
        "w_ff1": f["L0_attn_w_ff1"], "b_ff1": c(f["L0_attn_b_ff1"].reshape(FC, P).T),
        "w_ff2": c(f["L0_attn_w_ff2"].reshape(FC, P, P).transpose(1, 0, 2)),
        "b_ff2": f["L0_attn_b_ff2"].reshape(1, P),
        "wq_pad": quadrants(f["L0_xattn_Wq"]), "wk_pad": quadrants(f["L0_xattn_Wk"]),
        "bq_pad": c(quadrants(f["L0_xattn_bq"].reshape(P, 1))[0].T),
        "bk_pad": c(quadrants(f["L0_xattn_bk"].reshape(P, 1))[0].T),
        "q_ones": row_one.reshape(P, XC), "k_ones": k_one.reshape(P, XC),
        "low_rows": low.reshape(P, 2),
        "wv_t": c(f["L0_xattn_Wv"].T), "wo_t": c(f["L0_xattn_Wo"].T),
        "bv": f["L0_xattn_bv"].reshape(P, 1), "bo": f["L0_xattn_bo"].reshape(1, P),
        "wr_t": c(f["L0_ffn_Wr"].T),
        "w1_t": c(f["L0_ffn_W1"].transpose(2, 0, 1)),
        "b1": c(f["L0_ffn_b1"].reshape(EXP, FC, P).transpose(2, 0, 1)),
        "w2_t": c(f["L0_ffn_W2"].reshape(EXP, P, FC, P).transpose(3, 0, 2, 1)),
        "b2": f["L0_ffn_b2"],
    }


def kernel(**inputs):
    import concourse.bacc as bacc
    from concourse.bass_utils import run_bass_kernel_spmd

    arrays = {"in_" + k: np.ascontiguousarray(v) for k, v in host_layout(inputs).items()}
    nc = bacc.Bacc("TRN2", target_bir_lowering=False, num_devices=1)
    A = {k[3:]: nc.dram_tensor(k, v.shape, mybir.dt.from_np(v.dtype), kind="ExternalInput").ap()
         for k, v in arrays.items()}
    A["out"] = nc.dram_tensor("out", (P, SEQS, P), F32, kind="ExternalOutput").ap()
    bass_decoder(nc, A)
    r = run_bass_kernel_spmd(nc, [arrays], core_ids=[0])
    return np.ascontiguousarray(r.results[0]["out"].transpose(1, 0, 2))
```

```python
from contextlib import ExitStack

import numpy as np

import concourse.bass as bass
from concourse import mybir

F32 = mybir.dt.float32
BF16 = mybir.dt.bfloat16
U32 = mybir.dt.uint32
F32R = mybir.dt.float32r
I32 = mybir.dt.int32
ALU = mybir.AluOpType
ACT = mybir.ActivationFunctionType
AX = mybir.AxisListType

P = 128
SEQS = 32
T = 4
G = SEQS // T
GT = T * P
HEADS, HD = 8, 64
PAIRS = HEADS // 2
XH, XD = 16, 8
XC = XH // 4
FF = 512
FC = FF // P
EXP = 8
TOPK = 2
TILES = SEQS * TOPK + EXP
UNROLL = 4
REGION = (SEQS + TILES - SEQS * TOPK + 1) * P
ETA, DT, GAMMA_FLOOR, EPS = 0.1, 0.01, 0.1, 1e-5
XSCALE = XD ** -0.5
MASKED = -100.0
CL = 8
CN = P // CL
FAR = 1.0e5

AHEAD = (["xh2T", "decay"] + [f"{n}{p}" for p in range(PAIRS) for n in ("q", "k")]
         + [f"v{t}" for t in range(T)] + [f"at{t}r{r}" for t in range(2) for r in range(2)])


def attention_jobs():
    jobs = [f"mx0i{i}" for i in range(4)] + ["q2", "mT0"]
    filler = ["k2", "q3", "k3", "v0"]
    for t in range(T):
        if t + 1 < T:
            jobs += [f"mx{t + 1}i{i}" for i in range(4)]
        jobs += [f"st{t}i{i}" for i in range(4)]
        if t + 1 < T:
            jobs += [f"mT{t + 1}"]
        jobs += [f"xpv{t}", filler[t], f"ctT{t}"]
    return jobs


JOBS = (
    ["hpv0", "at2r0", "at2r1", "hpv1", "wo0", "at3r0", "at3r1", "hpv2", "wo1", "hpv3", "wo2", "wo3"]
    + [f"kp{c}" for c in range(XC)] + ["cv", "xh3T"]
    + [f"ff1c{c}" for c in range(FC)] + [f"ff2t{t}" for t in range(T)]
    + ["xh2T", "decay", "xaT"] + [f"qp{c}" for c in range(XC)] + ["q0", "k0", "q1", "k1"]
    + attention_jobs() + ["cxT", "v1"] + [f"xo{t}" for t in range(T)]
    + ["v2", "v3", "at0r0", "at0r1", "xbT", "at1r0", "rl", "at1r1", "rank"]
)
NB = 8
BANK = {name: n % NB for n, name in enumerate(JOBS)}
NTH = {name: sum(BANK[m] == BANK[name] for m in JOBS[:n]) for n, name in enumerate(JOBS)}
PER_GROUP = [sum(1 for b in BANK.values() if b == n) for n in range(NB)]
NTH_FIRST = {name: sum(BANK[m] == BANK[name] for m in AHEAD[:n]) for n, name in enumerate(AHEAD)}
FIRST = [sum(BANK[m] == n for m in AHEAD) for n in range(NB)]


def bass_decoder(nc, A):
    ctx = ExitStack()
    with ctx:
        def sb(name, shape, dt=F32):
            return ctx.enter_context(nc.sbuf_tensor(name, shape, dt))

        def sem(name):
            return ctx.enter_context(nc.semaphore(name))

        bank = [ctx.enter_context(nc.psum_tensor(f"bank{n}", [P, 512], F32)) for n in range(NB)]

        x_all = sb("x_all", [P, SEQS + T, P])
        ident = sb("ident", [P, P])
        antid = sb("antid", [P, P])
        tri = sb("tri", [P, P])
        after = sb("after", [P, P])
        ident_b = sb("ident_b", [P, P], BF16)
        future_b = sb("future_b", [P, P], BF16)
        ones = sb("ones", [P, P])
        pos_only = sb("pos_only", [1, P])
        pos_only_b = sb("pos_only_b", [1, P], BF16)
        mask_i = sb("mask_i", [1, GT], I32)
        mask_b = sb("mask_b", [1, GT], BF16)

        ln1_g, ln1_b = sb("ln1_g", [P, 1]), sb("ln1_b", [P, 1])
        ln2_g, ln2_b = sb("ln2_g", [P, 1]), sb("ln2_b", [P, 1])
        ln3_g, ln3_b = sb("ln3_g", [P, 1]), sb("ln3_b", [P, 1])
        w_pot, b_pot = sb("w_pot", [P, 2]), sb("b_pot", [1, 2])
        w_potg, w_potc = sb("w_potg", [P, 2]), sb("w_potc", [P, 2])
        pot_bias = sb("pot_bias", [P, 2])
        mean_w = sb("mean_w", [P, P])
        lnb_cols = sb("lnb_cols", [P, 3, P])
        w_bk_bc = sb("w_bk_bc", [P, 2, P])
        b_bk_bc = sb("b_bk_bc", [P, P])
        w_qkv = sb("w_qkv", [P, 3 * HEADS * HD])
        b_qk = sb("b_qk", [P, 2 * PAIRS])
        bg_qk = sb("bg_qk", [P, 2 * PAIRS])
        b_v_row = sb("b_v_row", [1, FF])
        bg_v = sb("bg_v", [P, FF])
        w_out = sb("w_out", [P, PAIRS, P])
        b_out_bc = sb("b_out_bc", [P, P])
        w_ff1 = sb("w_ff1", [P, FF])
        b_ff1, bg_ff1 = sb("b_ff1", [P, FC]), sb("bg_ff1", [P, FC])
        w_ff2 = sb("w_ff2", [P, FC, P])
        b_ff2_bc = sb("b_ff2_bc", [P, P])
        wq_pad, wk_pad = sb("wq_pad", [P, XC, P]), sb("wk_pad", [P, XC, P])
        bq_pad, bk_pad = sb("bq_pad", [P, XC]), sb("bk_pad", [P, XC])
        q_ones, k_ones = sb("q_ones", [P, XC]), sb("k_ones", [P, XC])
        low_rows = sb("low_rows", [P, 2])
        wv_t, wo_t = sb("wv_t", [P, P]), sb("wo_t", [P, P])
        bv_col, bo_row = sb("bv_col", [P, 1]), sb("bo_row", [1, P])
        bo_bc = sb("bo_bc", [P, P])
        wr_t = sb("wr_t", [P, EXP])
        w1_t = sb("w1_t", [P, EXP, FF + FC])
        w2_t = sb("w2_t", [P, EXP, FC, P])
        b2_bc = sb("b2_bc", [P, EXP, P])

        iota_e = sb("iota_e", [P, EXP])
        iota_t = sb("iota_t", [1, TILES])
        counts = sb("counts", [P, EXP])
        slot_base = sb("slot_base", [P, EXP])
        tri_b = sb("tri_b", [P, P], BF16)
        ones_b = sb("ones_b", [P, P], BF16)
        zeros = sb("zeros", [P, P])
        slot_all = sb("slot_all", [P, SEQS, TOPK])
        exp_all = sb("exp_all", [P, SEQS, TOPK])
        gate_all = sb("gate_all", [P, SEQS, TOPK])
        n_rows = sb("n_rows", [P, EXP])
        n_rows_i = sb("n_rows_i", [P, EXP], I32)
        n_tiles_i = sb("n_tiles_i", [P, EXP], I32)
        n_tiles = sb("n_tiles", [P, EXP])
        starts = sb("starts", [1, EXP])
        ends_i = sb("ends_i", [1, EXP], I32)
        step_rows = sb("step_rows", [P, EXP])
        tab_f = sb("tab_f", [1, 2, TILES])
        tab = sb("tab", [1, 2, TILES], I32)

        minus_half = sb("minus_half", [P, SEQS])
        gamma = sb("gamma", [P, SEQS + T])
        green = sb("green", [P, 2, SEQS + T])
        vpad = sb("vpad", [P, T, XH, 32])
        negmax = [sb(f"negmax{n}", [P, 4, 32]) for n in range(2)]

        group_ctx, ctx = ctx, ctx.enter_context(ExitStack())
        xT_all = sb("xT_all", [P, SEQS * P])
        future = sb("future", [P, P])
        st1 = sb("st1", [P, SEQS, 6])
        mv1 = sb("mv1", [P, SEQS, 2])
        rstd1 = sb("rstd1", [P, SEQS])
        zpot_row = sb("zpot_row", [2, SEQS * P])
        zpot_seq = sb("zpot_seq", [2 * SEQS, P])
        zpot = sb("zpot", [P, 2, SEQS])
        zabs, zln = sb("zabs", [P, SEQS]), sb("zln", [P, SEQS])
        diag = sb("diag", [P, 2, SEQS])
        d_row = sb("d_row", [2 * SEQS, 2, P])
        di_sign = sb("di_sign", [2 * SEQS, 2, P])
        Y = sb("Y", [2 * SEQS, CL + 2, 2, 2, CN])
        Ya = sb("Ya", [2 * SEQS, 2, 2, CN])
        Yb = sb("Yb", [2 * SEQS, 2, 2, CN])
        Yc = sb("Yc", [2 * SEQS, 2, 2, CN])
        C = sb("C", [2 * SEQS, CN, 2, 2, 4])
        Cs = sb("Cs", [2 * SEQS, CN, 16])
        cmax, crec = sb("cmax", [2 * SEQS, CN]), sb("crec", [2 * SEQS, CN])
        S = sb("S", [2 * SEQS, CN + 1, 4])
        Sp = sb("Sp", [2 * SEQS, 4, 4])
        Sa = sb("Sa", [2 * SEQS, 2, 2, CN])
        Sb = sb("Sb", [2 * SEQS, 2, 2, CN])
        Z = sb("Z", [2 * SEQS, CL + 1, 4, CN])
        Zb = sb("Zb", [2 * SEQS, CL + 1, 4, CN])
        Pr = sb("Pr", [2 * SEQS, CN, CL + 1])
        Pi = sb("Pi", [2 * SEQS, CN, CL + 1])
        ra, rb = sb("ra", [2 * SEQS, P]), sb("rb", [2 * SEQS, P])
        rc, rd = sb("rc", [2 * SEQS, P]), sb("rd", [2 * SEQS, P])
        re_, rf = sb("re_", [2 * SEQS, P]), sb("rf", [2 * SEQS, P])
        frac = sb("frac", [2 * SEQS, 2, P])
        neg_id = sb("neg_id", [SEQS, SEQS])
        fold_id = sb("fold_id", [2 * SEQS, SEQS])
        den = sb("den", [P, 2, SEQS])
        ga, gb = sb("ga", [P, SEQS]), sb("gb", [P, SEQS])

        ctx.close()
        ctx = group_ctx
        xbk = sb("xbk", [P, T, P])
        xqT = sb("xqT", [P, GT])
        x1 = sb("x1", [P, T, P])
        xf = sb("xf", [P, T, P])
        x1b = sb("x1b", [P, T, P])
        x2 = sb("x2", [P, T, P])
        xsum = xf
        xn = sb("xn", [P, T, P])
        xnT = sb("xnT", [P, GT])
        stats = sb("stats", [P, T, 6])
        mv = sb("mv", [P, T, 2])
        vare = sb("vare", [P, T])
        rstd = sb("rstd", [P, T])
        qT, kT = sb("qT", [P, PAIRS, GT]), sb("kT", [P, PAIRS, GT])
        cumg = sb("cumg", [P, T, P])
        decay = sb("decay", [P, T, P])
        mix = sb("mix", [P, 2, 4 * XC * P])
        pT = [mix[:, n, :].rearrange("p (i c n) -> p i c n", i=4, c=XC) for n in range(2)]
        v_sb = mix[:, 0, :].rearrange("p (t n) -> p t n", t=T)
        at = [mix[:, 1, n * GT * 2:(n + 1) * GT * 2].rearrange("p (r a n) -> p r a n", r=2, a=PAIRS)
              for n in range(2)]
        hebT = [sb(f"hebT{n}", [P, PAIRS, P]) for n in range(2)]
        hT = sb("hT", [P, FC, GT])
        ctxT = sb("ctxT", [P, GT])
        xa = sb("xa", [P, T, P])
        xab = sb("xab", [P, T, P])
        qp, kp = qT, kT
        high = [sb(f"high{n}", [P, GT], F32R) for n in range(2)]
        qr, kr = sb("qr", [P, XC, GT], F32R), sb("kr", [P, XC, GT], F32R)
        qm = [sb(f"qm{n}", [P, XC, P], F32R) for n in range(2)]
        cT = [sb(f"cT{n}", [P, XC, P]) for n in range(2)]
        rsum = sb("rsum", [P, T, XH])
        cx = sb("cx", [P, T, XH, XD])
        cxT = sb("cxT", [P, GT])
        xb = sb("xb", [P, T, P])
        top8 = sb("top8", [P, T, 8])
        lg = sb("lg", [P, T, EXP])
        top_i = sb("top_i", [P, T, 8], U32)
        top_f = sb("top_f", [P, T, TOPK])
        onehot = sb("onehot", [P, T, TOPK, EXP], BF16)
        chosen = sb("chosen", [P, T, EXP], BF16)
        below = sb("below", [P, T])
        ratio = sb("ratio", [P, T])
        wsum, wrec = sb("wsum", [P, T]), sb("wrec", [P, T])
        places = sb("places", [P, T, EXP])
        picked = sb("picked", [P, T, TOPK, EXP])
        slot_f = sb("slot_f", [P, T, TOPK])
        slot_u = sb("slot_u", [P, T, TOPK], U32)

        xt = [xn[:, n, :] for n in range(UNROLL)]
        xtT = [xnT[:, n * P:(n + 1) * P] for n in range(2)]
        w1c = [qT[:, :, :].rearrange("p a n -> p (a n)")[:, n * (FF + FC):(n + 1) * (FF + FC)]
               for n in range(2)]
        hx = [hT[:, :, n * P:(n + 1) * P] for n in range(2)]
        ysb = [xa[:, n, :] for n in range(UNROLL)]
        begun, begun_w = (kT[0:1, n, 0:(EXP - 1) * TILES].rearrange("p (e j) -> p e j", e=EXP - 1)
                          for n in range(2))
        x1r = x1[:, :, :].rearrange("p t n -> p (t n)")
        picked_rows = [mix[:, n, 0:2 * GT].rearrange("p (t k n) -> p t k n", t=T, k=TOPK) for n in range(2)]
        idx_now = [sb(f"idx_now{n}", [P, T, TOPK], U32) for n in range(2)]
        gather_f = sb("gather_f", [P, SEQS * TOPK])
        gather_u = sb("gather_u", [P, SEQS * TOPK], U32)
        acc = x1
        out_tiles = [x2, xb]

        full = [sem(f"bank{n}_full") for n in range(NB)]
        free = [sem(f"bank{n}_drained") for n in range(NB)]
        pre_loaded = sem("pre_loaded")
        x_loaded = [sem(f"x_loaded{q}") for q in range(4)]
        weights_loaded = sem("weights_loaded")
        ctx_loaded = sem("ctx_loaded")
        zseq_loaded = sem("zseq_loaded")
        mask_loaded, maskb_ready = sem("mask_loaded"), sem("maskb_ready")
        pool_const = sem("pool_const")
        wpotg_ready, wpotc_ready = sem("wpotg_ready"), sem("wpotc_ready")
        wmean_mm, potbias_mm, potbias_ready = sem("wmean_mm"), sem("potbias_mm"), sem("potbias_ready")
        lnb_ready = sem("lnb_ready")
        zrow_mm, zrow_copied = sem("zrow_mm"), sem("zrow_copied")
        bn1_ready, mv1_ready, vare1_ready, rstd1_ready = (
            sem("bn1_ready"), sem("mv1_ready"), sem("vare1_ready"), sem("rstd1_ready"))
        zpos_mm, zlink = sem("zpos_mm"), sem("zlink")
        z_ready, zln_ready, gamma_ready = sem("z_ready"), sem("zln_ready"), sem("gamma_ready")
        abs_done, exp_done = sem("abs_done"), sem("exp_done")
        drow_mm, scan_link, frac_ready, den_mm, green_ready = (
            sem("drow_mm"), sem("scan_link"), sem("frac_ready"), sem("den_mm"), sem("green_ready"))
        folded = sem("folded")
        bias_mm, bias_ready = sem("bias_mm"), sem("bias_ready")
        xbk_ready = sem("xbk_ready")
        x1_part = sem("x1_part")
        cumg_ready = sem("cumg_ready")
        sum_ready = sem("sum_ready")
        bn_ready = sem("bn_ready")
        mv_ready = sem("mv_ready")
        vare_ready = sem("vare_ready")
        rstd_ready = sem("rstd_ready")
        xn_ready = sem("xn_ready")
        x1b_ready, xf_ready, xsum_ready, xab_ready = (
            sem("x1b_ready"), sem("xf_ready"), sem("xsum_ready"), sem("xab_ready"))
        qhigh_ready, khigh_ready = sem("qhigh_ready"), sem("khigh_ready")
        qr_ready, kr_ready = sem("qr_ready"), sem("kr_ready")
        negmax_ready = sem("negmax_ready")
        rsum_ready = sem("rsum_ready")
        below_ready, ratio_ready, route_link = sem("below_ready"), sem("ratio_ready"), sem("route_link")
        places_ready = sem("places_ready")
        chosen_ready, slot_ready = sem("chosen_ready"), sem("slot_ready")
        xkept = sem("xkept")
        scattered, xb_free = sem("scattered"), sem("xb_free")
        table_link, table_ready, gidx_ready = sem("table_link"), sem("table_ready"), sem("gidx_ready")
        padded = sem("padded")
        x_in = [sem(f"x_in{n}") for n in range(UNROLL)]
        y_out = [sem(f"y_out{n}") for n in range(UNROLL)]
        turned, turned_copied = sem("turned"), sem("turned_copied")
        w1_in, h_mm, gelu_done, y_mm, y_added = (
            sem("w1_in"), sem("h_mm"), sem("gelu_done"), sem("y_mm"), sem("y_added"))
        idx_copied, combined = sem("idx_copied"), sem("combined")
        gathered = [[sem(f"gathered{n}{t}") for t in range(T)] for n in range(2)]
        acc_ready, bnc_ready, mvc_ready, varc_ready, rstdc_ready, outc_ready = (
            sem("acc_ready"), sem("bnc_ready"), sem("mvc_ready"), sem("varc_ready"),
            sem("rstdc_ready"), sem("outc_ready"))
        stored = [sem(f"stored{n}") for n in range(2)]
        dve_held, pool_held = sem("dve_held"), sem("pool_held")

        LN3, LN2, LNA, LNB = range(4)
        NLN = 4 * T
        xs = nc.dram_tensor("expert_in", (EXP * REGION, P), F32, kind="Internal").ap()
        ys = nc.dram_tensor("expert_out", (TILES * P, P), F32, kind="Internal").ap()

        def nth(g, name):
            b = BANK[name]
            return NTH_FIRST[name] if g is None else g * PER_GROUP[b] + (FIRST[b] + NTH[name])

        def take(pe, g, name):
            b = BANK[name]
            pe.wait_ge(free[b], nth(g, name) + 1)
            return bank[b]

        def filled(eng, g, name):
            b = BANK[name]
            eng.wait_ge(full[b], nth(g, name) + 1)
            return bank[b]

        def drained(eng, g, name):
            eng.wait_ge(free[BANK[name]], nth(g, name) + 2)

        def ln_nth(g, stage, t):
            return t if g is None else g * NLN + (T + stage * T + t)

        block = ctx.enter_context(nc.Block())

        PRE_LOADS = [
            (xT_all[:, :], A["xT"]), (w_pot[:, :], A["w_pot"]), (b_pot[:, :], A["b_pot"]),
            (ln1_g[:, :], A["ln1_g"]), (ln1_b[:, :], A["ln1_b"]), (ident[:, :], A["ident"]),
            (antid[:, :], A["antid"]), (fold_id[:, :], A["fold_id"]),
        ]
        LOADS = [
            (tri[:, :], A["tri"]), (after[:, :], A["after"]), (future[:, :], A["future"]),
            (pos_only[:, :], A["pos_only"]),
            (ln2_g[:, :], A["ln2_g"]), (ln2_b[:, :], A["ln2_b"]),
            (ln3_g[:, :], A["ln3_g"]), (ln3_b[:, :], A["ln3_b"]),
            (w_bk_bc[:, 0, :], A["w_bk"][0:1, :].broadcast_to([P, P])),
            (w_bk_bc[:, 1, :], A["w_bk"][1:2, :].broadcast_to([P, P])),
            (b_bk_bc[:, :], A["b_bk"].broadcast_to([P, P])),
            (w_qkv[:, :], A["w_qkv"]), (b_qk[:, :], A["b_qk"]), (b_v_row[:, :], A["b_v"]),
            (w_out[:, :, :], A["w_out"]), (b_out_bc[:, :], A["b_out"].broadcast_to([P, P])),
            (w_ff1[:, :], A["w_ff1"]), (b_ff1[:, :], A["b_ff1"]), (w_ff2[:, :, :], A["w_ff2"]),
            (b_ff2_bc[:, :], A["b_ff2"].broadcast_to([P, P])),
            (wq_pad[:, :, :], A["wq_pad"]), (wk_pad[:, :, :], A["wk_pad"]),
            (bq_pad[:, :], A["bq_pad"]), (bk_pad[:, :], A["bk_pad"]),
            (q_ones[:, :], A["q_ones"]), (k_ones[:, :], A["k_ones"]),
            (low_rows[:, :], A["low_rows"]),
            (wv_t[:, :], A["wv_t"]), (wo_t[:, :], A["wo_t"]), (bv_col[:, :], A["bv"]),
            (bo_row[:, :], A["bo"]), (wr_t[:, :], A["wr_t"]), (w1_t[:, :, :], A["w1_t"]),
            (w2_t[:, :, :, :], A["w2_t"]),
            (b2_bc[:, :, :], A["b2"].unsqueeze(0).broadcast_to([P, EXP, P])),
            (iota_e[:, :], A["iota_e"].broadcast_to([P, EXP])), (iota_t[:, :], A["iota_t"]),
            (slot_base[:, :], A["slot_base"].broadcast_to([P, EXP])),
        ]


        @block.sync
        def _(sp):
            for dst, src in PRE_LOADS:
                sp.dma_start(dst, src).then_inc(pre_loaded, 16)
            for q in range(4):
                sp.dma_start(x_all[:, 8 * q:8 * q + 8, :],
                             A["x"][:, 8 * q:8 * q + 8, :]).then_inc(x_loaded[q], 16)
            sp.wait_ge(zrow_copied, G)
            for n in range(2):
                sp.dma_start(zpot_seq[SEQS * n:SEQS * n + SEQS, :],
                             zpot_row[n:n + 1, :].rearrange("a (s p) -> a s p", p=P)
                             ).then_inc(zseq_loaded, 16)
            sp.wait_ge(green_ready, 1)
            sp.dma_start(ctxT[:, :], A["ctxT"][:, 0:GT]).then_inc(ctx_loaded, 16)
            sp.dma_start(mask_i[:, :], A["mask"][:, 0:GT]).then_inc(mask_loaded, 16)
            with sp.Fori(0, G - 1) as g:
                filled(sp, g, "cv")
                sp.dma_start(ctxT[:, :], A["ctxT"][:, bass.ds(g * GT + GT, GT)]).then_inc(ctx_loaded, 16)
                sp.dma_start(mask_i[:, :], A["mask"][:, bass.ds(g * GT + GT, GT)]).then_inc(mask_loaded, 16)
                sp.wait_ge(scattered, g * (16 * T * TOPK) + 16 * T * TOPK)
                sp.sem_inc(xb_free, 1)

            filled(sp, G - 1, "cv")
            sp.dma_start(mask_i[:, :], A["mask"][:, 0:GT]).then_inc(mask_loaded, 16)

            sp.wait_ge(scattered, 16 * SEQS * TOPK)
            sp.wait_ge(table_ready, 1)
            for e in range(EXP):
                n_pad = 1 if e < EXP - 1 else TILES - SEQS * TOPK + 1
                end = sp.value_load(ends_i[0:1, e:e + 1], min_val=e * REGION, max_val=e * REGION + SEQS * P)
                sp.dma_start(xs[bass.ds(end, n_pad * P), :].rearrange("(a p) n -> p a n", p=P),
                             zeros[:, :].unsqueeze(1).broadcast_to([P, n_pad, P])).then_inc(padded, 16)
            sp.wait_ge(padded, 16 * EXP)

            def rows_in(j, n):
                row = sp.value_load(tab[0:1, 1, bass.ds(j, 1)], min_val=0, max_val=(EXP * REGION) - P)
                sp.wait_ge(turned, j + 1)
                sp.dma_start(xt[n], xs[bass.ds(row, P), :]).then_inc(x_in[n], 16)

            def results_out(j, n):
                sp.wait_ge(y_added, j + 1 + 2)
                sp.dma_start(ys[bass.ds(j * P, P), :], ysb[n]).then_inc(y_out[n], 16)

            ahead = UNROLL + 1
            for n in range(ahead):
                rows_in(n, n % UNROLL)
            with sp.Fori(0, TILES // UNROLL - 2) as i:
                for n in range(UNROLL):
                    results_out(i * UNROLL + n, n)
                    rows_in(i * UNROLL + (n + ahead), (n + ahead) % UNROLL)
            for j in range(TILES - 2 * UNROLL, TILES):
                results_out(j, j % UNROLL)
                if j + ahead < TILES:
                    rows_in(j + ahead, (j + ahead) % UNROLL)

            with sp.Fori(0, G // 2) as i:
                for n in range(2):
                    sp.wait_ge(outc_ready, i * (2 * T) + (n * T + T))
                    sp.dma_start(A["out"][:, bass.ds(i * (2 * T) + n * T, T), :], out_tiles[n][:, :, :]
                                 ).then_inc(stored[n], 16)
            for n in range(2):
                sp.wait_ge(stored[n], 16 * (G // 2) + 1)

        @block.scalar
        def _(act):
            for dst, src in LOADS:
                act.dma_start(dst, src).then_inc(weights_loaded, 16)
            for n in range(G):
                act.wait_ge(zrow_mm, n + 1)
                nc.scalar.activation(zpot_row[:, n * GT:(n + 1) * GT], bank[n % 2][0:2, :],
                                     ACT.Copy).then_inc(zrow_copied, 1)
            act.wait_ge(z_ready, 1)
            nc.scalar.activation(zabs[:, :], zpot[:, 1, :], ACT.Abs).then_inc(abs_done, 1)
            act.wait_ge(abs_done, 1)
            nc.scalar.activation(zln[:, :], zabs[:, :], ACT.Exp, scale=-1.0).then_inc(exp_done, 1)
            act.wait_ge(exp_done, 1)
            nc.scalar.activation(zabs[:, :], zln[:, :], ACT.Ln, bias=1.0).then_inc(zln_ready, 1)
            act.wait_ge(bias_ready, 4)
            act.wait_ge(folded, 12)

            def drain(g, name, dst, func=ACT.Copy, bias=None, scale=1.0, src=None):
                b = filled(act, g, name)
                src_ap = b[:, :] if src is None else src(b)
                kw = {} if bias is None else {"bias": bias}
                nc.scalar.activation(dst, src_ap, func, scale=scale, **kw).then_inc(free[BANK[name]], 1)

            def turned_and_decay(g):
                drain(g, "xh2T", xqT[:, :])
                drain(g, "decay", decay[:, :, :].rearrange("p t n -> p (t n)"), ACT.Exp, scale=-DT)

            def queries(g, p):
                if g is not None:
                    act.wait_ge(qr_ready, g * XC + p + 1)
                drain(g, f"q{p}", qT[:, p, :], ACT.Identity, bias=bg_qk[:, p:p + 1])

            turned_and_decay(None)
            for p in range(PAIRS):
                queries(None, p)

            with act.Fori(0, G) as g:
                for t in range(T):
                    drain(g, f"hpv{t}", hebT[t % 2][:, :, :].rearrange("p a n -> p (a n)"))
                def split(name, which, c, full, bias, high_ready, split_ready):
                    b = filled(act, g, name)
                    if c >= 2:
                        act.wait_ge(split_ready, g * XC + c - 1)
                    elif name[0] == "q":
                        act.wait_ge(kr_ready, g * XC + c + 3)
                    nc.scalar.activation(high[c % 2][:, :], b[:, :], ACT.Identity, bias=bias
                                         ).then_inc(high_ready, 1)
                    nc.scalar.activation(full, b[:, :], ACT.Identity, bias=bias
                                         ).then_inc(free[BANK[name]], 1)

                for c in range(XC):
                    split(f"kp{c}", 1, c, kp[:, c, :], bk_pad[:, c:c + 1], khigh_ready, kr_ready)
                drain(g, "cv", vpad[:, :, :, 0:XD].rearrange("p t h d -> p (t h) d"),
                      src=lambda b: b[:, :].rearrange("p (n d) -> p n d", d=XD))
                drain(g, "xh3T", xnT[:, :])
                for c in range(FC):
                    drain(g, f"ff1c{c}", hT[:, c, :], ACT.Gelu_apprx_tanh, bias=bg_ff1[:, c:c + 1])
                turned_and_decay(g)
                drain(g, "xaT", xnT[:, :])
                for c in range(XC):
                    split(f"qp{c}", 0, c, qp[:, c, :], bq_pad[:, c:c + 1], qhigh_ready, qr_ready)
                queries(g, 0)
                queries(g, 1)
                queries(g, 2)
                for t in range(T):
                    for i in range(4):
                        drain(g, f"st{t}i{i}", pT[t % 2][:, i, :, :].rearrange("p c n -> p (c n)"), ACT.Exp)
                    drain(g, f"xpv{t}", cT[t % 2][:, :, :].rearrange("p c n -> p (c n)"))
                    if t == 1:
                        queries(g, 3)
                drain(g, "cxT", cxT[:, :])
                drain(g, "xbT", xnT[:, :])
                act.wait_ge(below_ready, g + 1)
                nc.scalar.activation(ratio[:, :], below[:, :], ACT.Exp).then_inc(ratio_ready, 1)

            act.sem_inc(gelu_done, 2)

            def gelu(j, n):
                act.wait_ge(h_mm, j + 1 + 2)
                act.wait_ge(y_mm, j + 1)
                for c in range(FC):
                    ins = nc.scalar.activation(hx[n][:, c, :], bank[2 + n][:, c * P:(c + 1) * P], ACT.Gelu,
                                               bias=w1c[n][:, FF + c:FF + c + 1])
                ins.then_inc(gelu_done, 1)

            with act.Fori(0, TILES // (2 * UNROLL)) as i:
                for n in range(2 * UNROLL):
                    gelu(i * (2 * UNROLL) + n, n % 2)

        @block.gpsimd
        def _(pool):
            nc.gpsimd.memset(ones[:, :], 1.0).then_inc(pool_const, 1)
            nc.gpsimd.memset(mean_w[:, :], 1.0 / P).then_inc(pool_const, 1)
            nc.gpsimd.memset(minus_half[:, :], -0.5).then_inc(pool_const, 1)
            nc.gpsimd.memset(Y[:, 0:2, :, :, :], 0.0).then_inc(pool_const, 1)
            nc.gpsimd.memset(S[:, 0, :], 0.0).then_inc(pool_const, 1)
            nc.gpsimd.memset(vpad[:, :, :, :], 0.0).then_inc(pool_const, 1)
            nc.gpsimd.memset(zeros[:, :], 0.0).then_inc(pool_const, 1)
            nc.gpsimd.memset(ones_b[:, :], 1.0).then_inc(pool_const, 1)
            for n in range(2):
                nc.gpsimd.memset(negmax[n][:, :, :], 0.0).then_inc(pool_const, 1)
            pool.wait_ge(pool_const, 10)
            nc.gpsimd.memset(Y[:, 0, 0, 0, :], 1.0).then_inc(pool_const, 1)
            nc.gpsimd.memset(Y[:, 1, 1, 0, :], 1.0).then_inc(pool_const, 1)
            nc.gpsimd.memset(S[:, 0, 2:3], 1.0).then_inc(pool_const, 1)
            nc.gpsimd.memset(vpad[:, :, :, XD:XD + 1], 1.0).then_inc(pool_const, 1)
            pool.wait_ge(mv1_ready, 1)
            nc.gpsimd.tensor_scalar(rstd1[:, :], mv1[:, :, 1], EPS, None, ALU.add).then_inc(vare1_ready, 1)
            pool.wait_ge(vare1_ready, 1)
            nc.gpsimd.tensor_tensor(rstd1[:, :], rstd1[:, :], minus_half[:, :], ALU.pow
                                    ).then_inc(rstd1_ready, 1)
            pool.wait_ge(weights_loaded, 16 * len(LOADS))
            nc.gpsimd.tensor_copy(ident_b[:, :], ident[:, :]).then_inc(folded, 1)
            nc.gpsimd.tensor_copy(future_b[:, :], future[:, :]).then_inc(folded, 1)
            nc.gpsimd.tensor_copy(pos_only_b[:, :], pos_only[:, :]).then_inc(folded, 1)
            nc.gpsimd.tensor_copy(tri_b[:, :], tri[:, :]).then_inc(folded, 1)
            nc.gpsimd.tensor_copy(counts[:, :], slot_base[:, :]).then_inc(folded, 1)
            nc.gpsimd.memset(x_all[:, SEQS:, :], 0.0).then_inc(folded, 1)
            pool.wait_ge(green_ready, 1)
            for q in range(4):
                pool.wait_ge(x_loaded[q], 16)

            def ln_scale(g, stage, t):
                n = ln_nth(g, stage, t)
                pool.wait_ge(mv_ready, n + 1)
                pool.sem_inc(pool_held, 1)
                nc.gpsimd.tensor_scalar(vare[:, t:t + 1], mv[:, t, 1:2], EPS, None, ALU.add
                                        ).then_inc(vare_ready, 1)
                pool.wait_ge(vare_ready, n + 1)
                nc.gpsimd.tensor_tensor(rstd[:, t:t + 1], vare[:, t:t + 1], minus_half[:, 0:1],
                                        ALU.pow).then_inc(rstd_ready, 1)

            def first_sums(k):
                nc.gpsimd.tensor_tensor(
                    xbk[:, :, :], x_all[:, bass.ds(k * T, T), :],
                    b_bk_bc[:, :].unsqueeze(1).broadcast_to([P, T, P]), ALU.add).then_inc(xbk_ready, 1)
                nc.gpsimd.tensor_tensor(
                    cumg[:, :, :], gamma[:, bass.ds(k * T, T)].unsqueeze(2).broadcast_to([P, T, P]),
                    tri[:, :].unsqueeze(1).broadcast_to([P, T, P]), ALU.mult).then_inc(cumg_ready, 1)

            def masks(k):
                pool.wait_ge(mask_loaded, k * 16 + 16)
                pool.sem_inc(pool_held, 1)
                nc.gpsimd.tensor_copy(mask_b[:, :], mask_i[:, :]).then_inc(maskb_ready, 1)

            def residuals(k):
                nc.gpsimd.tensor_tensor(
                    x1b[:, :, :], x1[:, :, :],
                    b_out_bc[:, :].unsqueeze(1).broadcast_to([P, T, P]), ALU.add).then_inc(x1b_ready, 1)
                nc.gpsimd.tensor_tensor(
                    xf[:, :, :], x_all[:, bass.ds(k * T, T), :],
                    b_ff2_bc[:, :].unsqueeze(1).broadcast_to([P, T, P]), ALU.add).then_inc(xf_ready, 1)

            masks(0)
            first_sums(0)
            for t in range(T):
                ln_scale(None, LN2, t)
            residuals(0)

            with pool.Fori(0, G) as g:
                for t in range(T):
                    ln_scale(g, LN3, t)
                first_sums(g + 1)
                pool.wait_ge(xf_ready, g + 1)
                nc.gpsimd.tensor_tensor(xsum[:, :, :], xf[:, :, :], x2[:, :, :], ALU.add
                                        ).then_inc(xsum_ready, 1)
                for t in range(T):
                    ln_scale(g, LN2, t)
                for t in range(T):
                    ln_scale(g, LNA, t)
                pool.wait_ge(xn_ready, ln_nth(g, LNA, T - 1) + 1)
                nc.gpsimd.tensor_tensor(
                    xab[:, :, :], xa[:, :, :],
                    bo_bc[:, :].unsqueeze(1).broadcast_to([P, T, P]), ALU.add).then_inc(xab_ready, 1)
                filled(pool, g, "cv")
                masks(g + 1)
                residuals(g + 1)
                for t in range(T):
                    ln_scale(g, LNB, t)
                pool.wait_ge(xn_ready, ln_nth(g, LNB, T - 1) + 1)
                pool.sem_inc(pool_held, 1)
                nc.gpsimd.tensor_copy(x_all[:, bass.ds(g * T, T), :], xb[:, :, :]).then_inc(xkept, 1)
                pool.wait_ge(slot_ready, g + 1)
                pool.sem_inc(pool_held, 1)
                for t in range(T):
                    for k in range(TOPK):
                        nc.gpsimd.indirect_dma_start(
                            xs[:, :], bass.IndirectOffsetOnAxis(ap=slot_u[:, t, k:k + 1], axis=0),
                            xb[:, t, :], None).then_inc(scattered, 16)

            pool.wait_ge(gidx_ready, 1)
            for n in range(UNROLL):
                pool.wait_ge(y_out[n], 16 * (TILES // UNROLL) + 1)

            def gather(g, n):
                nc.gpsimd.tensor_copy(idx_now[n][:, :, :].rearrange("p t k -> p (t k)"),
                                      gather_u[:, bass.ds(g * (T * TOPK), T * TOPK)]).then_inc(idx_copied, 1)
                pool.wait_ge(idx_copied, g + 1)
                for t in range(T):
                    pool.wait_ge(combined, g * T + t + 1)
                    pool.sem_inc(pool_held, 1)
                    for k in range(TOPK):
                        nc.gpsimd.indirect_dma_start(
                            picked_rows[n][:, t, k, :], None, ys[:, :],
                            bass.IndirectOffsetOnAxis(ap=idx_now[n][:, t, k:k + 1], axis=0)
                        ).then_inc(gathered[n][t], 16)

            def last_scale(g):
                pool.wait_ge(mvc_ready, g * T + T)
                pool.sem_inc(pool_held, 1)
                nc.gpsimd.tensor_scalar(vare[:, :], mv[:, :, 1], EPS, None, ALU.add).then_inc(varc_ready, 1)
                pool.wait_ge(varc_ready, g + 1)
                nc.gpsimd.tensor_tensor(rstd[:, :], vare[:, :], minus_half[:, 0:T], ALU.pow
                                        ).then_inc(rstdc_ready, 1)

            gather(0, 0)
            with pool.Fori(0, G // 2 - 1) as i:
                for n in range(2):
                    gather(i * 2 + (n + 1), 1 - n)
                    last_scale(i * 2 + n)
            gather(G - 1, 1)
            last_scale(G - 2)
            last_scale(G - 1)

        @block.vector
        def _(dve):
            nc.vector.memset(gamma[:, SEQS:], 0.0).then_inc(scan_link, 1)
            nc.vector.memset(green[:, :, SEQS:], 0.0).then_inc(scan_link, 1)
            dve.wait_ge(pre_loaded, 16 * len(PRE_LOADS))
            dve.wait_ge(pool_const, 14)
            nc.vector.tensor_scalar(w_potg[:, :], w_pot[:, :], ln1_g[:, 0:1], None, ALU.mult
                                    ).then_inc(wpotg_ready, 1)
            nc.vector.tensor_scalar(lnb_cols[:, 0, :], ones[:, :], ln1_b[:, 0:1], None, ALU.mult
                                    ).then_inc(lnb_ready, 1)
            dve.wait_ge(wmean_mm, 1)
            nc.vector.tensor_tensor(w_potc[:, :], w_potg[:, :], bank[2][:, 0:2], ALU.subtract
                                    ).then_inc(wpotc_ready, 1)
            dve.wait_ge(potbias_mm, 1)
            nc.vector.tensor_copy(pot_bias[:, :], bank[3][:, 0:2]).then_inc(potbias_ready, 1)
            for q in range(4):
                dve.wait_ge(x_loaded[q], 16)
                for n in range(8 * q, 8 * q + 8):
                    nc.vector.bn_stats(st1[:, n, :], x_all[:, n, :]).then_inc(bn1_ready, 1)
            dve.wait_ge(bn1_ready, SEQS)
            for n in range(SEQS):
                last = nc.vector.bn_aggr(mv1[:, n, :], st1[:, n, :])
            last.then_inc(mv1_ready, 1)
            dve.wait_ge(zpos_mm, 1)
            dve.wait_ge(rstd1_ready, 1)
            dve.wait_ge(potbias_ready, 1)
            nc.vector.tensor_tensor(
                zpot[:, :, :], bank[4][:, 0:2 * SEQS].rearrange("p (a s) -> p a s", a=2),
                rstd1[:, :].unsqueeze(1).broadcast_to([P, 2, SEQS]), ALU.mult).then_inc(zlink, 1)
            dve.wait_ge(zlink, 1)
            nc.vector.tensor_scalar(zpot[:, 1, :], zpot[:, 1, :], pot_bias[:, 1:2], None, ALU.add
                                    ).then_inc(z_ready, 1)
            nc.vector.tensor_scalar(diag[:, 0, :], zpot[:, 0, :], pot_bias[:, 0:1], 2.0, ALU.add,
                                    ALU.add).then_inc(zlink, 1)
            dve.wait_ge(zln_ready, 1)
            dve.wait_ge(z_ready, 1)
            nc.vector.scalar_tensor_tensor(out=gamma[:, 0:SEQS], in0=zpot[:, 1, :], scalar=0.0,
                                           in1=zabs[:, :], op0=ALU.max, op1=ALU.add).then_inc(zlink, 1)
            dve.wait_ge(zlink, 3)
            nc.vector.tensor_scalar(diag[:, 1, :], gamma[:, 0:SEQS], GAMMA_FLOOR, -1.0, ALU.add, ALU.mult
                                    ).then_inc(zlink, 1)
            dve.wait_ge(zlink, 4)
            nc.vector.tensor_scalar(gamma[:, 0:SEQS], gamma[:, 0:SEQS], GAMMA_FLOOR, None, ALU.add
                                    ).then_inc(gamma_ready, 1)

            links = [2]

            def link(ins):
                links[0] += 1
                ins.then_inc(scan_link, 1)
                dve.wait_ge(scan_link, links[0])

            dve.wait_ge(drow_mm, 1)
            rows = 2 * SEQS
            link(nc.vector.tensor_copy(d_row[:, :, :].rearrange("p a n -> p (a n)"), bank[5][0:rows, 0:2 * P]))
            link(nc.vector.tensor_scalar(di_sign[:, 0, :], d_row[:, 1, :], -1.0, None, ALU.mult))
            link(nc.vector.tensor_copy(di_sign[:, 1, :], d_row[:, 1, :]))
            dre = d_row[:, 0, :].rearrange("p (c j) -> p c j", j=CL)
            dim = di_sign[:, :, :].rearrange("p a (c j) -> p a c j", j=CL)
            for j in range(CL):
                y1 = Y[:, j + 1, :, :, :]
                link(nc.vector.tensor_tensor(
                    Ya[:, :, :, :].rearrange("p a b c -> p (a b) c"), y1.rearrange("p a b c -> p (a b) c"),
                    dre[:, :, j].unsqueeze(1).broadcast_to([rows, 4, CN]), ALU.mult))
                link(nc.vector.tensor_tensor(
                    Yb[:, :, :, :], y1[:, :, ::-1, :],
                    dim[:, :, :, j].unsqueeze(1).broadcast_to([rows, 2, 2, CN]), ALU.mult))
                link(nc.vector.tensor_tensor(Yc[:, :, :, :], Ya[:, :, :, :], Y[:, j, :, :, :], ALU.subtract))
                link(nc.vector.tensor_tensor(Y[:, j + 2, :, :, :], Yc[:, :, :, :], Yb[:, :, :, :], ALU.add))
            for out_j in range(2):
                yj = Y[:, CL + out_j, :, :, :]
                for out_r, in_r, part, sign in ((0, 0, 0, 1.0), (0, 1, 1, -1.0), (1, 0, 1, 1.0), (1, 1, 0, 1.0)):
                    link(nc.vector.tensor_scalar(
                        C[:, :, out_j, out_r, in_r:in_r + 3:2].rearrange("p c a -> p a c"),
                        yj[:, :, part, :], sign, None, ALU.mult))
            Cf = C[:, :, :, :, :].rearrange("p c a b n -> p c (a b n)")
            link(nc.vector.tensor_reduce(cmax[:, :], Cf, AX.X, ALU.max, apply_absolute_value=True))
            link(nc.vector.reciprocal(crec[:, :], cmax[:, :]))
            link(nc.vector.tensor_tensor(Cs[:, :, :], Cf, crec[:, :].unsqueeze(2).broadcast_to([rows, CN, 16]),
                                         ALU.mult))
            for c in range(CN - 1):
                link(nc.vector.tensor_tensor(
                    Sp[:, :, :], Cs[:, c, :].rearrange("p (o n) -> p o n", o=4),
                    S[:, c, :].unsqueeze(1).broadcast_to([rows, 4, 4]), ALU.mult))
                link(nc.vector.tensor_reduce(S[:, c + 1, :], Sp[:, :, :], AX.X, ALU.add))
            Sc = S[:, 0:CN, :].rearrange("p c (a b) -> p a b c", a=2)
            link(nc.vector.tensor_copy(Sa[:, :, 0, :], Sc[:, :, 0, :]))
            link(nc.vector.tensor_scalar(Sa[:, :, 1, :], Sc[:, :, 1, :], -1.0, None, ALU.mult))
            link(nc.vector.tensor_copy(Sb[:, :, 0, :], Sc[:, :, 1, :]))
            link(nc.vector.tensor_copy(Sb[:, :, 1, :], Sc[:, :, 0, :]))
            Yf = Y[:, 1:CL + 2, :, :, :].rearrange("p j a b c -> p j (a b c)")
            for Sx, Zx, Px in ((Sa, Z, Pr), (Sb, Zb, Pi)):
                link(nc.vector.tensor_tensor(
                    Zx[:, :, :, :].rearrange("p j n c -> p j (n c)"), Yf,
                    Sx[:, :, :, :].rearrange("p a b c -> p (a b c)").unsqueeze(1).broadcast_to(
                        [rows, CL + 1, 4 * CN]), ALU.mult))
                link(nc.vector.tensor_reduce(Px[:, :, :].rearrange("p c j -> p j c"),
                                             Zx[:, :, :, :].rearrange("p j n c -> p j c n"), AX.X, ALU.add))
            pr1, pi1 = Pr[:, :, 1:CL + 1], Pi[:, :, 1:CL + 1]
            pr0, pi0 = Pr[:, :, 0:CL], Pi[:, :, 0:CL]

            def v3(buf):
                return buf[:, :].rearrange("p (c j) -> p c j", j=CL)

            link(nc.vector.tensor_tensor(v3(ra), pr0, pr0, ALU.mult))
            link(nc.vector.tensor_tensor(v3(rb), pi0, pi0, ALU.mult))
            link(nc.vector.tensor_tensor(rc[:, :], ra[:, :], rb[:, :], ALU.add))
            link(nc.vector.reciprocal(rd[:, :], rc[:, :]))
            for part, (p0, q0, p1, q1, op) in enumerate(((pr1, pr0, pi1, pi0, ALU.add),
                                                         (pi1, pr0, pr1, pi0, ALU.subtract))):
                link(nc.vector.tensor_tensor(v3(ra), p0, q0, ALU.mult))
                link(nc.vector.tensor_tensor(v3(rb), p1, q1, ALU.mult))
                link(nc.vector.tensor_tensor(rc[:, :], ra[:, :], rb[:, :], op))
                link(nc.vector.tensor_tensor(frac[0:SEQS, part, :], rc[0:SEQS, :], rd[0:SEQS, :], ALU.mult))
                link(nc.vector.tensor_tensor(frac[SEQS:rows, part, ::-1], rc[SEQS:rows, :], rd[SEQS:rows, :],
                                             ALU.mult))
            nc.vector.tensor_scalar(neg_id[:, :], ident[0:SEQS, 0:SEQS], -1.0, None, ALU.mult
                                    ).then_inc(frac_ready, 1)
            dve.wait_ge(den_mm, 1)
            link(nc.vector.tensor_copy(den[:, :, :].rearrange("p a s -> p (a s)"), bank[6][:, 0:2 * SEQS]))
            link(nc.vector.tensor_tensor(ga[:, :], den[:, 0, :], den[:, 0, :], ALU.mult))
            link(nc.vector.tensor_tensor(gb[:, :], den[:, 1, :], den[:, 1, :], ALU.mult))
            link(nc.vector.tensor_tensor(ga[:, :], ga[:, :], gb[:, :], ALU.add))
            link(nc.vector.reciprocal(gb[:, :], ga[:, :]))
            link(nc.vector.tensor_tensor(green[:, 0, 0:SEQS], den[:, 0, :], gb[:, :], ALU.mult))
            nc.vector.scalar_tensor_tensor(out=green[:, 1, 0:SEQS], in0=den[:, 1, :], scalar=-1.0,
                                           in1=gb[:, :], op0=ALU.mult, op1=ALU.mult).then_inc(green_ready, 1)

            dve.wait_ge(weights_loaded, 16 * len(LOADS))
            nc.vector.tensor_scalar(w_out[:, :, :], w_out[:, :, :], ETA, None, ALU.mult).then_inc(folded, 1)
            nc.vector.tensor_scalar(wq_pad[:, :, :], wq_pad[:, :, :], XSCALE, None, ALU.mult).then_inc(folded, 1)
            nc.vector.scalar_tensor_tensor(out=bq_pad[:, :], in0=bq_pad[:, :], scalar=XSCALE, in1=q_ones[:, :],
                                           op0=ALU.mult, op1=ALU.add).then_inc(folded, 1)
            nc.vector.tensor_tensor(bk_pad[:, :], bk_pad[:, :], k_ones[:, :], ALU.add).then_inc(folded, 1)
            nc.vector.tensor_scalar(lnb_cols[:, 1, :], ones[:, :], ln2_b[:, 0:1], None, ALU.mult
                                    ).then_inc(lnb_ready, 1)
            nc.vector.tensor_scalar(lnb_cols[:, 2, :], ones[:, :], bv_col[:, 0:1], None, ALU.mult
                                    ).then_inc(lnb_ready, 1)
            dve.wait_ge(bias_mm, 1)
            nc.vector.tensor_tensor(bg_qk[:, :], bank[7][:, 0:2 * PAIRS], b_qk[:, :], ALU.add
                                    ).then_inc(bias_ready, 1)
            dve.wait_ge(bias_mm, 2)
            nc.vector.tensor_copy(bg_v[:, :], bank[2][:, :]).then_inc(bias_ready, 1)
            dve.wait_ge(bias_mm, 3)
            nc.vector.tensor_tensor(bg_ff1[:, :], bank[3][:, 0:FC], b_ff1[:, :], ALU.add).then_inc(bias_ready, 1)
            dve.wait_ge(bias_mm, 4)
            nc.vector.tensor_copy(bo_bc[:, :], bank[4][:, 0:P]).then_inc(bias_ready, 1)
            nc.vector.tensor_scalar(w_qkv[:, :], w_qkv[:, :], ln2_g[:, 0:1], None, ALU.mult).then_inc(folded, 1)
            nc.vector.tensor_scalar(w_ff1[:, :], w_ff1[:, :], ln3_g[:, 0:1], None, ALU.mult).then_inc(folded, 1)

            def ln_stats(g, stage, t, src):
                n = ln_nth(g, stage, t)
                dve.wait_ge(sum_ready, n + 1)
                nc.vector.bn_stats(stats[:, t, :], src).then_inc(bn_ready, 1)
                dve.wait_ge(bn_ready, n + 1)
                dve.sem_inc(dve_held, 1)
                nc.vector.bn_aggr(mv[:, t, :], stats[:, t, :]).then_inc(mv_ready, 1)

            def ln_apply(g, stage, t, src, dst):
                dve.wait_ge(rstd_ready, ln_nth(g, stage, t) + 1)
                nc.vector.tensor_scalar(dst, src, mv[:, t, 0:1], rstd[:, t:t + 1], ALU.subtract,
                                        ALU.mult).then_inc(xn_ready, 1)

            def first_sums(g, k):
                dve.wait_ge(xbk_ready, k + 1)
                for t in range(T):
                    nc.vector.scalar_tensor_tensor(
                        out=x1[:, t, :], in0=w_bk_bc[:, 0, :], scalar=green[:, 0, bass.ds(k * T + t, 1)],
                        in1=xbk[:, t, :], op0=ALU.mult, op1=ALU.add).then_inc(x1_part, 1)
                for t in range(T):
                    dve.wait_ge(x1_part, k * T + t + 1)
                    nc.vector.scalar_tensor_tensor(
                        out=x1[:, t, :], in0=w_bk_bc[:, 1, :], scalar=green[:, 1, bass.ds(k * T + t, 1)],
                        in1=x1[:, t, :], op0=ALU.mult, op1=ALU.add).then_inc(sum_ready, 1)
                    ln_stats(g, LN2, t, x1[:, t, :])
                if g is not None:
                    filled(dve, g, "xh3T")
                for t in range(T):
                    ln_apply(g, LN2, t, x1[:, t, :], xn[:, t, :])

            def keys(g, p):
                b = filled(dve, g, f"k{p}")
                nc.vector.tensor_scalar(kT[:, p, :], b[:, :], bg_qk[:, PAIRS + p:PAIRS + p + 1], None,
                                        ALU.add).then_inc(free[BANK[f"k{p}"]], 1)

            def values(g, t):
                b = filled(dve, g, f"v{t}")
                nc.vector.tensor_tensor(v_sb[:, t, :], b[:, :], bg_v[:, :], ALU.add
                                        ).then_inc(free[BANK[f"v{t}"]], 1)

            def decayed(g, t):
                if t == 0:
                    drained(dve, g, "decay")
                for r in range(2):
                    b = filled(dve, g, f"at{t}r{r}")
                    nc.vector.tensor_tensor(
                        at[t % 2][:, r, :, :], b[:, :].rearrange("p (a n) -> p a n", a=PAIRS),
                        decay[:, t, :].unsqueeze(1).broadcast_to([P, PAIRS, P]), ALU.mult
                    ).then_inc(free[BANK[f"at{t}r{r}"]], 1)

            dve.sem_inc(xb_free, 1)
            first_sums(None, 0)
            for p in range(PAIRS):
                keys(None, p)
            for t in range(T):
                values(None, t)
            decayed(None, 0)
            decayed(None, 1)

            with dve.Fori(0, G) as g:
                def heb_sum(t):
                    if t == 0:
                        dve.wait_ge(x1b_ready, g + 1)
                    b = filled(dve, g, f"wo{t}")
                    nc.vector.tensor_tensor(x2[:, t, :], b[:, 0:P], x1b[:, t, :], ALU.add
                                            ).then_inc(free[BANK[f"wo{t}"]], 1)
                    drained(dve, g, f"wo{t}")
                    dve.sem_inc(sum_ready, 1)
                    ln_stats(g, LN3, t, x2[:, t, :])

                decayed(g, 2)
                heb_sum(0)
                decayed(g, 3)
                heb_sum(1)
                ln_apply(g, LN3, 0, x2[:, 0, :], xn[:, 0, :])
                heb_sum(2)
                ln_apply(g, LN3, 1, x2[:, 1, :], xn[:, 1, :])
                heb_sum(3)
                ln_apply(g, LN3, 2, x2[:, 2, :], xn[:, 2, :])
                ln_apply(g, LN3, 3, x2[:, 3, :], xn[:, 3, :])

                def split(name, which, c, full, out, high_ready, split_ready):
                    dve.wait_ge(high_ready, g * XC + c + 1)
                    drained(dve, g, name)
                    nc.vector.scalar_tensor_tensor(
                        out=out, in0=high[c % 2][:, :].bitcast(F32),
                        scalar=low_rows[:, which:which + 1], in1=full, op0=ALU.mult, op1=ALU.add
                    ).then_inc(split_ready, 1)

                for c in range(XC):
                    split(f"kp{c}", 1, c, kp[:, c, :], kr[:, c, :], khigh_ready, kr_ready)

                first_sums(g, g + 1)

                def residual(stage, name, t, dst, other):
                    b = filled(dve, g, name)
                    nc.vector.tensor_tensor(dst, b[:, 0:P], other, ALU.add).then_inc(free[BANK[name]], 1)
                    drained(dve, g, name)
                    dve.sem_inc(sum_ready, 1)
                    ln_stats(g, stage, t, dst)

                dve.wait_ge(xsum_ready, g + 1)
                for t in range(T):
                    residual(LNA, f"ff2t{t}", t, x2[:, t, :], xsum[:, t, :])
                for t in range(T):
                    ln_apply(g, LNA, t, x2[:, t, :], xa[:, t, :])

                def maxima(t):
                    for i in range(4):
                        b = filled(dve, g, f"mx{t}i{i}")
                        nc.vector.tensor_reduce(
                            negmax[t % 2][:, i, 28:28 + XC], b[:, :].rearrange("p (c n) -> p c n", c=XC),
                            AX.X, ALU.max, negate=True).then_inc(free[BANK[f"mx{t}i{i}"]], 1)
                    b = filled(dve, g, f"mT{t}")
                    nc.vector.tensor_tensor(
                        qm[t % 2][:, :, :], b[:, 0:P].unsqueeze(1).broadcast_to([P, XC, P]),
                        qr[:, :, t * P:(t + 1) * P].bitcast(F32), ALU.add).then_inc(free[BANK[f"mT{t}"]], 1)

                def normalise(t):
                    b = filled(dve, g, f"ctT{t}")
                    heads = b[:, :].rearrange("p (h n) -> p h n", n=32)
                    nc.vector.reciprocal(rsum[:, t, :], heads[:, :, XD]).then_inc(rsum_ready, 1)
                    dve.wait_ge(rsum_ready, g * T + t + 1)
                    nc.vector.tensor_tensor(
                        cx[:, t, :, :], heads[:, :, 0:XD],
                        rsum[:, t, :].unsqueeze(2).broadcast_to([P, XH, XD]), ALU.mult
                    ).then_inc(free[BANK[f"ctT{t}"]], 1)

                for c in range(XC):
                    split(f"qp{c}", 0, c, qp[:, c, :], qr[:, c, :], qhigh_ready, qr_ready)
                keys(g, 0)
                keys(g, 1)
                maxima(0)
                for t in range(T):
                    if t + 1 < T:
                        maxima(t + 1)
                    if t == 0:
                        keys(g, 2)
                    if t == 2:
                        keys(g, 3)
                    if t == 3:
                        values(g, 0)
                    normalise(t)
                dve.wait_ge(xab_ready, g + 1)
                for t in range(T):
                    residual(LNB, f"xo{t}", t, x2[:, t, :], xab[:, t, :])
                dve.wait_ge(xb_free, g + 1)
                for t in range(T):
                    ln_apply(g, LNB, t, x2[:, t, :], xb[:, t, :])
                for t in range(1, T):
                    values(g, t)
                decayed(g, 0)

                b = filled(dve, g, "rl")
                nc.vector.tensor_copy(lg[:, :, :].rearrange("p t e -> p (t e)"), b[:, 0:T * EXP]
                                      ).then_inc(free[BANK["rl"]], 1)
                drained(dve, g, "rl")
                dve.sem_inc(dve_held, 1)
                for t in range(T):
                    ins = nc.vector.max(top8[:, t, :], lg[:, t, :])
                ins.then_inc(route_link, 1)
                dve.wait_ge(route_link, g * 6 + 1)
                dve.sem_inc(dve_held, 1)
                nc.vector.tensor_tensor(below[:, :], top8[:, :, 1], top8[:, :, 0], ALU.subtract
                                        ).then_inc(below_ready, 1)
                for t in range(T):
                    ins = nc.vector.max_index(top_i[:, t, :], top8[:, t, :], lg[:, t, :])
                ins.then_inc(route_link, 1)
                dve.wait_ge(route_link, g * 6 + 2)
                nc.vector.tensor_copy(top_f[:, :, :], top_i[:, :, 0:TOPK]).then_inc(route_link, 1)
                dve.wait_ge(route_link, g * 6 + 3)
                nc.vector.tensor_tensor(
                    onehot[:, :, :, :].rearrange("p t k e -> p (t k) e"),
                    iota_e[:, :].unsqueeze(1).broadcast_to([P, T * TOPK, EXP]),
                    top_f[:, :, :].rearrange("p t k -> p (t k)").unsqueeze(2).broadcast_to(
                        [P, T * TOPK, EXP]), ALU.is_equal).then_inc(route_link, 1)
                dve.wait_ge(route_link, g * 6 + 4)
                nc.vector.tensor_tensor(chosen[:, :, :], onehot[:, :, 0, :], onehot[:, :, 1, :], ALU.add
                                        ).then_inc(chosen_ready, 1)
                nc.vector.tensor_copy(exp_all[:, bass.ds(g * T, T), :], top_f[:, :, :])
                dve.wait_ge(ratio_ready, g + 1)
                nc.vector.tensor_scalar(wsum[:, :], ratio[:, :], 1.0, None, ALU.add).then_inc(route_link, 1)
                dve.wait_ge(route_link, g * 6 + 5)
                nc.vector.reciprocal(gate_all[:, bass.ds(g * T, T), 0], wsum[:, :])
                nc.vector.reciprocal(wrec[:, :], wsum[:, :]).then_inc(route_link, 1)
                dve.wait_ge(route_link, g * 6 + 6)
                nc.vector.tensor_tensor(gate_all[:, bass.ds(g * T, T), 1], ratio[:, :], wrec[:, :], ALU.mult)
                decayed(g, 1)
                b = filled(dve, g, "rank")
                nc.vector.tensor_tensor(
                    places[:, :, :], b[:, 0:T * EXP].rearrange("p (t e) -> p t e", t=T),
                    counts[:, :].unsqueeze(1).broadcast_to([P, T, EXP]), ALU.add).then_inc(places_ready, 1)
                dve.wait_ge(places_ready, g * 3 + 1)
                nc.vector.tensor_tensor(counts[:, :], counts[:, :], b[:, T * EXP:T * EXP + EXP], ALU.add
                                        ).then_inc(free[BANK["rank"]], 1)
                for k in range(TOPK):
                    ins = nc.vector.tensor_tensor(picked[:, :, k, :], onehot[:, :, k, :], places[:, :, :],
                                                  ALU.mult)
                ins.then_inc(places_ready, 1)
                dve.wait_ge(places_ready, g * 3 + 2)
                nc.vector.tensor_reduce(slot_f[:, :, :], picked[:, :, :, :], AX.X, ALU.add
                                        ).then_inc(places_ready, 1)
                dve.wait_ge(places_ready, g * 3 + 3)
                nc.vector.tensor_copy(slot_u[:, :, :], slot_f[:, :, :]).then_inc(slot_ready, 1)
                nc.vector.tensor_copy(slot_all[:, bass.ds(g * T, T), :], slot_f[:, :, :])

            tl = [0]

            def tlink(ins):
                tl[0] += 1
                ins.then_inc(table_link, 1)
                dve.wait_ge(table_link, tl[0])

            drained(dve, G - 1, "rank")
            tlink(nc.vector.tensor_tensor(n_rows[:, :], counts[:, :], slot_base[:, :], ALU.subtract))
            tlink(nc.vector.tensor_scalar(n_rows[:, :], n_rows[:, :], float(P - 1), None, ALU.add))
            tlink(nc.vector.tensor_copy(n_rows_i[:, :], n_rows[:, :]))
            tlink(nc.vector.tensor_scalar(n_tiles_i[:, :], n_rows_i[:, :], 7, None, ALU.arith_shift_right))
            tlink(nc.vector.tensor_copy(n_tiles[:, :], n_tiles_i[:, :]))
            tlink(nc.vector.tensor_scalar(ends_i[:, :], counts[0:1, :], 1.0, None, ALU.add))
            tlink(nc.vector.tensor_scalar(step_rows[:, :], n_tiles[:, :], -float(P), float(REGION), ALU.mult,
                                          ALU.add))
            tlink(nc.vector.tensor_copy(starts[:, 1:2], n_tiles[0:1, 0:1]))
            for e in range(2, EXP):
                tlink(nc.vector.tensor_tensor(starts[:, e:e + 1], starts[:, e - 1:e], n_tiles[0:1, e - 1:e],
                                              ALU.add))
            tlink(nc.vector.tensor_tensor(
                begun, iota_t[:, :].unsqueeze(1).broadcast_to([1, EXP - 1, TILES]),
                starts[:, 1:EXP].unsqueeze(2).broadcast_to([1, EXP - 1, TILES]), ALU.is_ge))
            tlink(nc.vector.tensor_tensor(
                begun_w, begun,
                step_rows[0:1, 0:EXP - 1].unsqueeze(2).broadcast_to([1, EXP - 1, TILES]), ALU.mult))
            tlink(nc.vector.tensor_reduce(tab_f[:, 0, :], begun.rearrange("p e j -> p j e"),
                                          AX.X, ALU.add))
            tlink(nc.vector.tensor_reduce(tab_f[:, 1, :], begun_w.rearrange("p e j -> p j e"),
                                          AX.X, ALU.add))
            tlink(nc.vector.scalar_tensor_tensor(out=tab_f[:, 1, :], in0=iota_t[:, :], scalar=float(P),
                                                 in1=tab_f[:, 1, :], op0=ALU.mult, op1=ALU.add))
            nc.vector.tensor_copy(tab[:, :, :], tab_f[:, :, :]).then_inc(table_ready, 1)
            slots = slot_all[:, :, :].rearrange("p s k -> p (s k)")
            pairs = SEQS * TOPK
            begun_p = x1r[:, 0:pairs * (EXP - 1)].rearrange("p (s e) -> p s e", e=EXP - 1)
            tlink(nc.vector.tensor_tensor(
                begun_p, exp_all[:, :, :].rearrange("p s k -> p (s k)").unsqueeze(2).broadcast_to(
                    [P, pairs, EXP - 1]),
                iota_e[:, 1:EXP].unsqueeze(1).broadcast_to([P, pairs, EXP - 1]), ALU.is_ge))
            tlink(nc.vector.tensor_tensor(
                begun_p, begun_p, step_rows[:, 0:EXP - 1].unsqueeze(1).broadcast_to([P, pairs, EXP - 1]),
                ALU.mult))
            tlink(nc.vector.tensor_reduce(gather_f[:, :], begun_p, AX.X, ALU.add))
            tlink(nc.vector.tensor_tensor(gather_f[:, :], slots, gather_f[:, :], ALU.subtract))
            nc.vector.tensor_copy(gather_u[:, :], gather_f[:, :]).then_inc(gidx_ready, 1)

            dve.sem_inc(turned_copied, 2)
            dve.sem_inc(y_added, 2)
            dve.sem_inc(combined, 2 * T)
            for n in range(UNROLL):
                dve.sem_inc(y_out[n], 1)
            for n in range(2):
                dve.sem_inc(stored[n], 1)

            def turned_rows(j, n):
                dve.wait_ge(turned, j + 1 + UNROLL)
                dve.wait_ge(h_mm, j + 1)
                nc.vector.tensor_copy(xtT[n], bank[n][:, 0:P]).then_inc(turned_copied, 1)

            def weights(j, n):
                e = dve.value_load(tab[0:1, 0, bass.ds(j, 1)], min_val=0, max_val=EXP - 1)
                dve.wait_ge(gelu_done, j + 1)
                nc.vector.tensor_copy(w1c[n], w1_t[:, bass.ds(e, 1), :].rearrange("p a n -> p (a n)")
                                      ).then_inc(w1_in, 1)

            def results(j, i, n):
                e = dve.value_load(tab[0:1, 0, bass.ds(j, 1)], min_val=0, max_val=EXP - 1)
                dve.wait_ge(y_mm, j + 1 + 2)
                dve.wait_ge(y_out[n], i * 16 + 1)
                nc.vector.tensor_tensor(ysb[n], bank[4 + n % 2][:, 0:P],
                                        b2_bc[:, bass.ds(e, 1), :].rearrange("p a n -> p (a n)"), ALU.add
                                        ).then_inc(y_added, 1)

            dve.wait_ge(table_ready, 1)
            weights(0, 0)
            weights(1, 1)
            turned_rows(0, 0)
            turned_rows(1, 1)
            with dve.Fori(0, TILES // UNROLL - 1) as i:
                for n in range(UNROLL):
                    turned_rows(i * UNROLL + (n + 2), n % 2)
                    weights(i * UNROLL + (n + 2), n % 2)
                    results(i * UNROLL + n, i, n)
            for n in range(UNROLL):
                j = TILES - UNROLL + n
                if j + 2 < TILES:
                    turned_rows(j + 2, n % 2)
                    weights(j + 2, n % 2)
                results(j, TILES // UNROLL - 1, n)

            with dve.Fori(0, G // 2) as i:
                for n in range(2):
                    g = i * 2 + n
                    for t in range(T):
                        dve.wait_ge(gathered[n][t], i * 32 + 32)
                        nc.vector.scalar_tensor_tensor(
                            out=acc[:, t, :], in0=picked_rows[n][:, t, 0, :],
                            scalar=gate_all[:, bass.ds(g * T + t, 1), 0],
                            in1=x_all[:, bass.ds(g * T + t, 1), :].rearrange("p a n -> p (a n)"),
                            op0=ALU.mult, op1=ALU.add).then_inc(acc_ready, 1)
                    for t in range(T):
                        dve.wait_ge(acc_ready, g * T + t + 1)
                        nc.vector.scalar_tensor_tensor(
                            out=acc[:, t, :], in0=picked_rows[n][:, t, 1, :],
                            scalar=gate_all[:, bass.ds(g * T + t, 1), 1],
                            in1=acc[:, t, :], op0=ALU.mult, op1=ALU.add).then_inc(combined, 1)
                    for t in range(T):
                        dve.wait_ge(combined, g * T + (t + 1 + 2 * T))
                        nc.vector.bn_stats(stats[:, t, :], acc[:, t, :]).then_inc(bnc_ready, 1)
                    for t in range(T):
                        dve.wait_ge(bnc_ready, g * T + t + 1)
                        dve.sem_inc(dve_held, 1)
                        nc.vector.bn_aggr(mv[:, t, :], stats[:, t, :]).then_inc(mvc_ready, 1)
                    dve.wait_ge(rstdc_ready, g + 1)
                    dve.wait_ge(stored[n], i * 16 + 1)
                    for t in range(T):
                        nc.vector.tensor_scalar(out_tiles[n][:, t, :], acc[:, t, :], mv[:, t, 0:1],
                                                rstd[:, t:t + 1], ALU.subtract, ALU.mult
                                                ).then_inc(outc_ready, 1)
                    dve.wait_ge(outc_ready, g * T + T)

        @block.tensor
        def _(pe):
            mm = nc.tensor.matmul
            pe.wait_ge(pre_loaded, 16 * len(PRE_LOADS))
            pe.wait_ge(pool_const, 14)
            pe.wait_ge(wpotg_ready, 1)
            mm(bank[2][:, 0:2], mean_w[:, :], w_potg[:, :], start=True, stop=True).then_inc(wmean_mm, 1)
            pe.wait_ge(lnb_ready, 1)
            mm(bank[3][:, 0:2], lnb_cols[:, 0, :], w_pot[:, :], start=True, stop=False)
            mm(bank[3][:, 0:2], ones[0:1, :], b_pot[:, :], start=False, stop=True).then_inc(potbias_mm, 1)
            pe.wait_ge(wpotc_ready, 1)
            for n in range(G):
                if n >= 2:
                    pe.wait_ge(zrow_copied, n - 1)
                mm(bank[n % 2][0:2, :], w_potc[:, :], xT_all[:, n * GT:(n + 1) * GT], start=True,
                   stop=True).then_inc(zrow_mm, 1)
            pe.wait_ge(zseq_loaded, 32)
            nc.tensor.transpose(bank[4][:, 0:2 * SEQS], zpot_seq[:, :], ident[0:2 * SEQS, 0:2 * SEQS]
                                ).then_inc(zpos_mm, 1)
            pe.wait_ge(zlink, 4)
            for part in range(2):
                for way, perm in enumerate((ident, antid)):
                    last = mm(bank[5][SEQS * way:SEQS * way + SEQS, P * part:P * part + P],
                              diag[:, part, :], perm[:, :], start=True, stop=True)
            last.then_inc(drow_mm, 1)
            pe.wait_ge(frac_ready, 1)
            for part in range(2):
                o = bank[6][:, SEQS * part:SEQS * part + SEQS]
                mm(o, frac[0:2 * SEQS, part, :], fold_id[:, :], start=True, stop=False)
                last = mm(o, d_row[0:SEQS, part, :], neg_id[:, :], start=False, stop=True)
            last.then_inc(den_mm, 1)
            pe.wait_ge(weights_loaded, 16 * len(LOADS))
            for j in range(2 * PAIRS):
                last = mm(bank[7][:, j:j + 1], w_qkv[:, j * P:(j + 1) * P], ln2_b[:, :], start=True, stop=True)
            last.then_inc(bias_mm, 1)
            pe.wait_ge(lnb_ready, 3)
            mm(bank[2][:, :], lnb_cols[:, 1, :], w_qkv[:, 2 * FF:3 * FF], start=True, stop=False)
            mm(bank[2][:, :], ones[0:1, :], b_v_row[:, :], start=False, stop=True).then_inc(bias_mm, 1)
            for j in range(FC):
                last = mm(bank[3][:, j:j + 1], w_ff1[:, j * P:(j + 1) * P], ln3_b[:, :], start=True, stop=True)
            last.then_inc(bias_mm, 1)
            mm(bank[4][:, 0:P], lnb_cols[:, 2, :], wo_t[:, :], start=True, stop=False)
            mm(bank[4][:, 0:P], ones[0:1, :], bo_row[:, :], start=False, stop=True).then_inc(bias_mm, 1)
            pe.wait_ge(bias_ready, 4)
            pe.wait_ge(folded, 12)
            for b in range(NB):
                pe.sem_inc(free[b], 1)

            def done(ins, name):
                ins.then_inc(full[BANK[name]], 1)

            def tile(t):
                return slice(t * P, (t + 1) * P)

            def turn(g, name, stage, src):
                for t in range(T):
                    pe.wait_ge(xn_ready, ln_nth(g, stage, t) + 1)
                    if t == 0:
                        b = take(pe, g, name)
                    ins = nc.tensor.transpose(b[:, tile(t)], src[:, t, :], ident[:, :])
                done(ins, name)

            def wide(g, name, lhsT, rhs):
                b = take(pe, g, name)
                done(mm(b[:, :], lhsT, rhs, start=True, stop=True), name)

            def turn_and_decay(g, k):
                turn(g, "xh2T", LN2, xn)
                pe.wait_ge(cumg_ready, k + 1)
                b = take(pe, g, "decay")
                mm(b[:, :], after[:, :], cumg[:, :, :].rearrange("p t n -> p (t n)"), start=True, stop=True)
                for t in range(T):
                    ins = mm(b[:, tile(t)], ident_b[:, :], future_b[:, :], start=False,
                             stop=True, skip_group_check=True)
                done(ins, "decay")

            def queries(g, p):
                if p == 0:
                    drained(pe, g, "xh2T")
                wide(g, f"q{p}", w_qkv[:, tile(p)], xqT[:, :])

            def keys(g, p):
                wide(g, f"k{p}", w_qkv[:, FF + p * P:FF + (p + 1) * P], xqT[:, :])

            def values(g, t):
                wide(g, f"v{t}", xqT[:, tile(t)], w_qkv[:, 2 * FF:3 * FF])

            def scores(g, t, r):
                if t == 0 and r == 0:
                    for p in range(PAIRS):
                        drained(pe, g, f"q{p}")
                        drained(pe, g, f"k{p}")
                b = take(pe, g, f"at{t}r{r}")
                rows = slice(HD * r, HD * r + HD)
                for p in range(PAIRS):
                    ins = mm(b[:, tile(p)], kT[rows, p, tile(t)], qT[rows, p, tile(t)],
                             start=True, stop=True)
                done(ins, f"at{t}r{r}")

            def ahead_drained(g):
                for t in range(T):
                    drained(pe, g, f"v{t}")
                for t in range(2):
                    for r in range(2):
                        drained(pe, g, f"at{t}r{r}")

            turn_and_decay(None, 0)
            for p in range(PAIRS):
                queries(None, p)
                keys(None, p)
            for t in range(T):
                values(None, t)
            for t in range(2):
                for r in range(2):
                    scores(None, t, r)
            ahead_drained(None)

            with pe.Fori(0, G) as g:
                def weigh(t):
                    b = take(pe, g, f"hpv{t}")
                    for r in range(2):
                        if t >= 2:
                            drained(pe, g, f"at{t}r{r}")
                        for p in range(PAIRS):
                            h = 2 * p + r
                            ins = mm(b[HD * r:HD * r + HD, tile(p)], v_sb[:, t, h * HD:(h + 1) * HD],
                                     at[t % 2][:, r, p, :], start=True, stop=True)
                    done(ins, f"hpv{t}")

                def heb_out(t):
                    drained(pe, g, f"hpv{t}")
                    b = take(pe, g, f"wo{t}")
                    for p in range(PAIRS):
                        ins = mm(b[:, 0:P], hebT[t % 2][:, p, :], w_out[:, p, :], start=(p == 0),
                                 stop=(p == PAIRS - 1))
                    done(ins, f"wo{t}")

                weigh(0)
                scores(g, 2, 0)
                scores(g, 2, 1)
                weigh(1)
                heb_out(0)
                scores(g, 3, 0)
                scores(g, 3, 1)
                weigh(2)
                heb_out(1)
                weigh(3)
                heb_out(2)
                heb_out(3)

                pe.wait_ge(ctx_loaded, g * 16 + 16)
                pe.wait_ge(maskb_ready, g + 1)
                for c in range(XC):
                    b = take(pe, g, f"kp{c}")
                    mm(b[:, :], wk_pad[:, c, :], ctxT[:, :], start=True, stop=False)
                    done(mm(b[:, :], pos_only_b[:, :], mask_b[:, :], start=False,
                            stop=True), f"kp{c}")
                b = take(pe, g, "cv")
                for t in range(T):
                    ins = mm(b[:, tile(t)], ctxT[:, tile(t)], wv_t[:, :], start=True, stop=True)
                done(ins, "cv")

                turn(g, "xh3T", LN3, xn)
                drained(pe, g, "xh3T")
                for c in range(FC):
                    wide(g, f"ff1c{c}", w_ff1[:, tile(c)], xnT[:, :])
                for t in range(T):
                    b = take(pe, g, f"ff2t{t}")
                    for c in range(FC):
                        if t == 0:
                            drained(pe, g, f"ff1c{c}")
                        ins = mm(b[:, 0:P], hT[:, c, tile(t)], w_ff2[:, c, :], start=(c == 0),
                                 stop=(c == FC - 1))
                    done(ins, f"ff2t{t}")

                turn_and_decay(g, g + 1)

                turn(g, "xaT", LNA, xa)
                drained(pe, g, "xaT")
                for c in range(XC):
                    wide(g, f"qp{c}", wq_pad[:, c, :], xnT[:, :])

                for p in range(2):
                    queries(g, p)
                    keys(g, p)

                def max_scores(t):
                    if t == 0:
                        pe.wait_ge(qr_ready, g * XC + XC)
                        pe.wait_ge(kr_ready, g * XC + XC)
                    for i in range(4):
                        b = take(pe, g, f"mx{t}i{i}")
                        rows = slice(32 * i, 32 * i + 32)
                        for c in range(XC):
                            ins = mm(b[:, tile(c)], qr[rows, c, tile(t)], kr[rows, c, tile(t)],
                                     start=True, stop=True)
                        done(ins, f"mx{t}i{i}")

                def turn_max(t):
                    for i in range(4):
                        drained(pe, g, f"mx{t}i{i}")
                    b = take(pe, g, f"mT{t}")
                    done(nc.tensor.transpose(b[:, 0:P], negmax[t % 2][:, :, :].rearrange("p i n -> p (i n)"),
                                             ident[:, :]), f"mT{t}")

                def key_scores(t):
                    drained(pe, g, f"mT{t}")
                    for i in range(4):
                        b = take(pe, g, f"st{t}i{i}")
                        rows = slice(32 * i, 32 * i + 32)
                        for c in range(XC):
                            ins = mm(b[:, tile(c)], kr[rows, c, tile(t)], qm[t % 2][rows, c, :],
                                     start=True, stop=True)
                        done(ins, f"st{t}i{i}")

                def attend(t):
                    b = take(pe, g, f"xpv{t}")
                    for i in range(4):
                        drained(pe, g, f"st{t}i{i}")
                        for c in range(XC):
                            ins = mm(b[32 * i:32 * i + 32, tile(c)], vpad[:, t, 4 * c + i, :],
                                     pT[t % 2][:, i, c, :], start=True, stop=True)
                    done(ins, f"xpv{t}")
                    if t == 0:
                        keys(g, 2)
                    if t == 1:
                        queries(g, 3)
                    if t == 2:
                        keys(g, 3)
                    if t == 3:
                        values(g, 0)
                    drained(pe, g, f"xpv{t}")
                    b = take(pe, g, f"ctT{t}")
                    for c in range(XC):
                        ins = nc.tensor.transpose(b[:, tile(c)], cT[t % 2][:, c, :], ident[:, :])
                    done(ins, f"ctT{t}")

                max_scores(0)
                queries(g, 2)
                turn_max(0)
                for t in range(T):
                    if t + 1 < T:
                        max_scores(t + 1)
                    key_scores(t)
                    if t + 1 < T:
                        turn_max(t + 1)
                    attend(t)
                b = take(pe, g, "cxT")
                for t in range(T):
                    drained(pe, g, f"ctT{t}")
                    ins = nc.tensor.transpose(b[:, tile(t)], cx[:, t, :, :].rearrange("p h d -> p (h d)"),
                                              ident[:, :])
                done(ins, "cxT")
                values(g, 1)
                drained(pe, g, "cxT")
                for t in range(T):
                    b = take(pe, g, f"xo{t}")
                    done(mm(b[:, 0:P], cxT[:, tile(t)], wo_t[:, :], start=True, stop=True), f"xo{t}")

                values(g, 2)
                values(g, 3)
                scores(g, 0, 0)
                scores(g, 0, 1)

                turn(g, "xbT", LNB, xb)
                scores(g, 1, 0)
                drained(pe, g, "xbT")
                b = take(pe, g, "rl")
                for t in range(T):
                    ins = mm(b[:, t * EXP:(t + 1) * EXP], xnT[:, tile(t)], wr_t[:, :], start=True, stop=True)
                done(ins, "rl")
                scores(g, 1, 1)
                pe.wait_ge(chosen_ready, g + 1)
                b = take(pe, g, "rank")
                mm(b[:, 0:T * EXP], tri_b[:, :], chosen[:, :, :].rearrange("p t e -> p (t e)"), start=True,
                   stop=True)
                for t in range(T - 1):
                    later = T - 1 - t
                    mm(b[:, (t + 1) * EXP:T * EXP], ones_b[:, :],
                       chosen[:, t, :].unsqueeze(1).broadcast_to([P, later, EXP]), start=False, stop=True,
                       skip_group_check=True)
                for t in range(T):
                    ins = mm(b[:, T * EXP:T * EXP + EXP], ones_b[:, :], chosen[:, t, :], start=(t == 0),
                             stop=(t == T - 1))
                done(ins, "rank")
                ahead_drained(g)

            for b in range(NB):
                pe.wait_ge(free[b], G * PER_GROUP[b] + FIRST[b] + 1)
            pe.wait_ge(table_ready, 1)
            pe.sem_inc(turned, UNROLL)
            pe.sem_inc(h_mm, 2)
            pe.sem_inc(y_mm, 2)

            def turn_rows(j, i, n):
                pe.wait_ge(x_in[n], i * 16 + 16)
                pe.wait_ge(turned_copied, j + 1)
                nc.tensor.transpose(bank[n % 2][:, 0:P], xt[n], ident[:, :]).then_inc(turned, 1)

            def hidden(j, n):
                pe.wait_ge(turned_copied, j + 1 + 2)
                pe.wait_ge(w1_in, j + 1)
                pe.wait_ge(gelu_done, j + 1)
                for c in range(FC):
                    ins = mm(bank[2 + n % 2][:, c * P:(c + 1) * P], w1c[n % 2][:, c * P:(c + 1) * P],
                             xtT[n % 2], start=True, stop=True)
                ins.then_inc(h_mm, 1)

            def outputs(j, n):
                e = pe.value_load(tab[0:1, 0, bass.ds(j, 1)], min_val=0, max_val=EXP - 1)
                pe.wait_ge(gelu_done, j + 1 + 2)
                pe.wait_ge(y_added, j + 1)
                for c in range(FC):
                    ins = mm(bank[4 + n % 2][:, 0:P], hx[n % 2][:, c, :],
                             w2_t[:, bass.ds(e, 1), c, :].rearrange("p a n -> p (a n)"), start=(c == 0),
                             stop=(c == FC - 1))
                ins.then_inc(y_mm, 1)

            turn_rows(0, 0, 0)
            turn_rows(1, 0, 1)
            hidden(0, 0)
            with pe.Fori(0, TILES // UNROLL - 1) as i:
                for n in range(UNROLL):
                    ahead = n + 2
                    turn_rows(i * UNROLL + ahead, i + ahead // UNROLL, ahead % UNROLL)
                    hidden(i * UNROLL + (n + 1), n + 1)
                    outputs(i * UNROLL + n, n)
            for n in range(UNROLL):
                j = TILES - UNROLL + n
                if j + 2 < TILES:
                    turn_rows(j + 2, (j + 2) // UNROLL, (j + 2) % UNROLL)
                if j + 1 < TILES:
                    hidden(j + 1, n + 1)
                outputs(j, n)


def host_layout(inp):
    f = {k: np.asarray(v) for k, v in inp.items()}
    i128 = np.arange(P)
    c = np.ascontiguousarray

    def quadrants(w):
        src = w.reshape(XC, 4, XD, -1)
        dst = np.zeros((XC, 4, 32, src.shape[-1]), w.dtype)
        for n in range(3):
            dst[:, :, n * XD:(n + 1) * XD] = src
        return c(dst.reshape(XC, P, -1).transpose(2, 0, 1))

    row_one = np.zeros((4, 32, XC), np.float32)
    row_one[:, 24, :] = 1.0
    k_one = np.zeros((4, 32, XC), np.float32)
    for n in range(XC):
        k_one[:, 28 + n, n] = 1.0
    pos = np.zeros((1, 4, 32), np.float32)
    pos[:, :, 24] = MASKED
    low = np.zeros((4, 32, 2), np.float32)
    low[:, 16:24, 0] = -1.0
    low[:, 8:16, 1] = -1.0
    b = f["L0_attn_b_qkv"]
    return {
        "x": c(f["x"].transpose(1, 0, 2)), "xT": c(f["x"].reshape(SEQS * P, P).T),
        "ctxT": c(f["ctx_1024"].reshape(SEQS * P, P).T), "mask": c(f["mask_BxS2_ik1"].reshape(1, -1)),
        "w_pot": f["L0_attn_w_pot"], "b_pot": f["L0_attn_b_pot"].reshape(1, 2),
        "ln1_g": f["L0_attn_ln1_g"].reshape(P, 1), "ln1_b": f["L0_attn_ln1_b"].reshape(P, 1),
        "ln2_g": f["L0_attn_ln2_g"].reshape(P, 1), "ln2_b": f["L0_attn_ln2_b"].reshape(P, 1),
        "ln3_g": f["L0_attn_ln3_g"].reshape(P, 1), "ln3_b": f["L0_attn_ln3_b"].reshape(P, 1),
        "ident": np.eye(P, dtype=np.float32), "antid": c(np.eye(P, dtype=np.float32)[::-1]),
        "tri": (i128[:, None] <= i128[None, :]).astype(np.float32),
        "after": (i128[:, None] > i128[None, :]).astype(np.float32),
        "future": (i128[None, :] < i128[:, None]).astype(np.float32) * np.float32(FAR),
        "pos_only": pos.reshape(1, P),
        "fold_id": c(np.tile(np.eye(SEQS, dtype=np.float32), (2, 1))),
        "w_bk": f["L0_attn_w_bk"], "b_bk": f["L0_attn_b_bk"].reshape(1, P),
        "w_qkv": f["L0_attn_w_qkv"], "b_qk": c(b[:2 * FF].reshape(2 * PAIRS, P).T),
        "b_v": c(b[2 * FF:].reshape(1, FF)),
        "w_out": c(f["L0_attn_w_out"].reshape(PAIRS, P, P).transpose(1, 0, 2)),
        "b_out": f["L0_attn_b_out"].reshape(1, P),
        "w_ff1": f["L0_attn_w_ff1"], "b_ff1": c(f["L0_attn_b_ff1"].reshape(FC, P).T),
        "w_ff2": c(f["L0_attn_w_ff2"].reshape(FC, P, P).transpose(1, 0, 2)),
        "b_ff2": f["L0_attn_b_ff2"].reshape(1, P),
        "wq_pad": quadrants(f["L0_xattn_Wq"]), "wk_pad": quadrants(f["L0_xattn_Wk"]),
        "bq_pad": c(quadrants(f["L0_xattn_bq"].reshape(P, 1))[0].T),
        "bk_pad": c(quadrants(f["L0_xattn_bk"].reshape(P, 1))[0].T),
        "q_ones": row_one.reshape(P, XC), "k_ones": k_one.reshape(P, XC),
        "low_rows": low.reshape(P, 2),
        "wv_t": c(f["L0_xattn_Wv"].T), "wo_t": c(f["L0_xattn_Wo"].T),
        "bv": f["L0_xattn_bv"].reshape(P, 1), "bo": f["L0_xattn_bo"].reshape(1, P),
        "wr_t": c(f["L0_ffn_Wr"].T),
        "w1_t": c(np.concatenate([f["L0_ffn_W1"].transpose(2, 0, 1),
                                  f["L0_ffn_b1"].reshape(EXP, FC, P).transpose(2, 0, 1)], axis=2)),
        "w2_t": c(f["L0_ffn_W2"].reshape(EXP, P, FC, P).transpose(3, 0, 2, 1)),
        "b2": f["L0_ffn_b2"],
        "iota_e": np.arange(EXP, dtype=np.float32).reshape(1, EXP),
        "iota_t": np.arange(TILES, dtype=np.float32).reshape(1, TILES),
        "slot_base": (np.arange(EXP, dtype=np.float32) * REGION - 1).reshape(1, EXP),
    }


def kernel(**inputs):
    import concourse.bacc as bacc
    from concourse.bass_utils import run_bass_kernel_spmd

    arrays = {"in_" + k: np.ascontiguousarray(v) for k, v in host_layout(inputs).items()}
    nc = bacc.Bacc("TRN2", target_bir_lowering=False, num_devices=1)
    A = {k[3:]: nc.dram_tensor(k, v.shape, mybir.dt.from_np(v.dtype), kind="ExternalInput").ap()
         for k, v in arrays.items()}
    A["out"] = nc.dram_tensor("out", (P, SEQS, P), F32, kind="ExternalOutput").ap()
    bass_decoder(nc, A)
    r = run_bass_kernel_spmd(nc, [arrays], core_ids=[0])
    return np.ascontiguousarray(r.results[0]["out"].transpose(1, 0, 2))
```

```python
from contextlib import ExitStack

import numpy as np

import concourse.bass as bass
from concourse import mybir

F32 = mybir.dt.float32
BF16 = mybir.dt.bfloat16
U32 = mybir.dt.uint32
F32R = mybir.dt.float32r
I32 = mybir.dt.int32
ALU = mybir.AluOpType
ACT = mybir.ActivationFunctionType
AX = mybir.AxisListType

P = 128
SEQS = 32
T = 4
G = SEQS // T
GT = T * P
HEADS, HD = 8, 64
PAIRS = HEADS // 2
XH, XD = 16, 8
XC = XH // 4
FF = 512
FC = FF // P
EXP = 8
TOPK = 2
TILES = SEQS * TOPK + EXP
UNROLL = 4
REGION = (SEQS + TILES - SEQS * TOPK + 1) * P
ETA, DT, GAMMA_FLOOR, EPS = 0.1, 0.01, 0.1, 1e-5
XSCALE = XD ** -0.5
MASKED = -100.0
CL = 8
CN = P // CL
FAR = 1.0e5

AHEAD = (["xh2T", "decay"] + [f"{n}{p}" for p in range(PAIRS) for n in ("q", "k")]
         + [f"v{t}" for t in range(T)] + [f"at{t}r{r}" for t in range(2) for r in range(2)]
         + ["kp0", "kp1"])


def attention_jobs():
    jobs = [f"mx0i{i}" for i in range(4)] + ["q1", "mT0"]
    for t in range(T):
        if t + 1 < T:
            jobs += [f"mx{t + 1}i{i}" for i in range(4)] + [f"k{t + 1}"]
        jobs += [f"st{t}i{i}" for i in range(4)]
        if t + 1 < T:
            jobs += [f"mT{t + 1}"]
        jobs += [f"xpv{t}", ("q2", "q3", "v0", "v1")[t], f"ctT{t}"]
    return jobs


JOBS = (
    ["hpv0", "at2r0", "at2r1", "kp2", "hpv1", "wo0", "at3r0", "at3r1", "hpv2", "wo1",
     "kp3", "hpv3", "wo2", "wo3", "cv", "xh3T"]
    + [f"ff1c{c}" for c in range(FC)] + [f"ff2t{t}" for t in range(T)]
    + ["xh2T", "decay", "xaT"] + [f"qp{c}" for c in range(XC)] + ["q0", "k0"]
    + attention_jobs() + ["cxT", "v2"] + [f"xo{t}" for t in range(T)]
    + ["v3", "at0r0", "at0r1", "kp0", "xbT", "at1r0", "rl", "at1r1", "rank", "kp1"]
)
NB = 8
BANK = {name: n % NB for n, name in enumerate(JOBS)}
NTH = {name: sum(BANK[m] == BANK[name] for m in JOBS[:n]) for n, name in enumerate(JOBS)}
PER_GROUP = [sum(1 for b in BANK.values() if b == n) for n in range(NB)]
NTH_FIRST = {name: sum(BANK[m] == BANK[name] for m in AHEAD[:n]) for n, name in enumerate(AHEAD)}
FIRST = [sum(BANK[m] == n for m in AHEAD) for n in range(NB)]


def bass_decoder(nc, A):
    ctx = ExitStack()
    with ctx:
        def sb(name, shape, dt=F32):
            return ctx.enter_context(nc.sbuf_tensor(name, shape, dt))

        def sem(name):
            return ctx.enter_context(nc.semaphore(name))

        bank = [ctx.enter_context(nc.psum_tensor(f"bank{n}", [P, 512], F32)) for n in range(NB)]

        x_all = sb("x_all", [P, SEQS + T, P])
        ident = sb("ident", [P, P])
        antid = sb("antid", [P, P])
        tri = sb("tri", [P, P])
        after = sb("after", [P, P])
        ident_b = sb("ident_b", [P, P], BF16)
        future_b = sb("future_b", [P, P], BF16)
        ones = sb("ones", [P, P])
        pos_only = sb("pos_only", [1, P])
        pos_only_b = sb("pos_only_b", [1, P], BF16)
        mask_i = sb("mask_i", [1, GT], I32)
        mask_b = sb("mask_b", [1, GT], BF16)

        ln1_g, ln1_b = sb("ln1_g", [P, 1]), sb("ln1_b", [P, 1])
        ln2_g, ln2_b = sb("ln2_g", [P, 1]), sb("ln2_b", [P, 1])
        ln3_g, ln3_b = sb("ln3_g", [P, 1]), sb("ln3_b", [P, 1])
        w_pot, b_pot = sb("w_pot", [P, 2]), sb("b_pot", [1, 2])
        w_potg, w_potc = sb("w_potg", [P, 2]), sb("w_potc", [P, 2])
        pot_bias = sb("pot_bias", [P, 2])
        mean_w = sb("mean_w", [P, P])
        lnb_cols = sb("lnb_cols", [P, 3, P])
        w_bk_bc = sb("w_bk_bc", [P, 2, P])
        b_bk_bc = sb("b_bk_bc", [P, P])
        w_qkv = sb("w_qkv", [P, 3 * HEADS * HD])
        b_qk = sb("b_qk", [P, 2 * PAIRS])
        bg_qk = sb("bg_qk", [P, 2 * PAIRS])
        b_v_row = sb("b_v_row", [1, FF])
        bg_v = sb("bg_v", [P, FF])
        w_out = sb("w_out", [P, PAIRS, P])
        b_out_bc = sb("b_out_bc", [P, P])
        w_ff1 = sb("w_ff1", [P, FF])
        b_ff1, bg_ff1 = sb("b_ff1", [P, FC]), sb("bg_ff1", [P, FC])
        w_ff2 = sb("w_ff2", [P, FC, P])
        b_ff2_bc = sb("b_ff2_bc", [P, P])
        wq_pad, wk_pad = sb("wq_pad", [P, XC, P]), sb("wk_pad", [P, XC, P])
        bq_pad, bk_pad = sb("bq_pad", [P, XC]), sb("bk_pad", [P, XC])
        q_ones, k_ones = sb("q_ones", [P, XC]), sb("k_ones", [P, XC])
        low_rows = sb("low_rows", [P, 2])
        wv_t, wo_t = sb("wv_t", [P, P]), sb("wo_t", [P, P])
        bv_col, bo_row = sb("bv_col", [P, 1]), sb("bo_row", [1, P])
        bo_bc = sb("bo_bc", [P, P])
        wr_t = sb("wr_t", [P, EXP])
        w1_t = sb("w1_t", [P, EXP, FF + FC])
        w2_t = sb("w2_t", [P, EXP, FC, P])
        b2_bc = sb("b2_bc", [P, EXP, P])

        iota_e = sb("iota_e", [P, EXP])
        iota_t = sb("iota_t", [1, TILES])
        counts = sb("counts", [P, EXP])
        slot_base = sb("slot_base", [P, EXP])
        tri_b = sb("tri_b", [P, P], BF16)
        ones_b = sb("ones_b", [P, P], BF16)
        zeros = sb("zeros", [P, P])
        home_all = sb("home_all", [P, SEQS, TOPK], U32)
        home_now = sb("home_now", [P, T, TOPK], U32)
        gate_all = sb("gate_all", [P, SEQS, TOPK])
        n_rows = sb("n_rows", [P, EXP])
        n_rows_i = sb("n_rows_i", [P, EXP], I32)
        n_tiles_i = sb("n_tiles_i", [P, EXP], I32)
        n_tiles = sb("n_tiles", [P, EXP])
        starts = sb("starts", [1, EXP])
        ends_i = sb("ends_i", [1, EXP], I32)
        step_rows = sb("step_rows", [P, EXP])
        tab_f = sb("tab_f", [1, 2, TILES])
        tab = sb("tab", [1, 2, TILES], I32)

        minus_half = sb("minus_half", [P, SEQS])
        gamma = sb("gamma", [P, SEQS + T])
        green = sb("green", [P, 2, SEQS + T])
        vpad = sb("vpad", [P, T, XH, 32])
        negmax = [sb(f"negmax{n}", [P, 4, 32]) for n in range(2)]

        group_ctx, ctx = ctx, ctx.enter_context(ExitStack())
        xT_all = sb("xT_all", [P, SEQS * P])
        future = sb("future", [P, P])
        st1 = sb("st1", [P, SEQS, 6])
        mv1 = sb("mv1", [P, SEQS, 2])
        rstd1 = sb("rstd1", [P, SEQS])
        zpot_row = sb("zpot_row", [2, SEQS * P])
        zpot_seq = sb("zpot_seq", [2 * SEQS, P])
        zpot = sb("zpot", [P, 2, SEQS])
        zabs, zln = sb("zabs", [P, SEQS]), sb("zln", [P, SEQS])
        diag = sb("diag", [P, 2, SEQS])
        d_row = sb("d_row", [2 * SEQS, 2, P])
        di_sign = sb("di_sign", [2 * SEQS, 2, P])
        Y = sb("Y", [2 * SEQS, CL + 2, 2, 2, CN])
        Ya = sb("Ya", [2 * SEQS, 2, 2, CN])
        Yb = sb("Yb", [2 * SEQS, 2, 2, CN])
        Yc = sb("Yc", [2 * SEQS, 2, 2, CN])
        C = sb("C", [2 * SEQS, CN, 2, 2, 4])
        Cs = sb("Cs", [2 * SEQS, CN, 16])
        cmax, crec = sb("cmax", [2 * SEQS, CN]), sb("crec", [2 * SEQS, CN])
        S = sb("S", [2 * SEQS, CN + 1, 4])
        Sp = sb("Sp", [2 * SEQS, 4, 4])
        Sa = sb("Sa", [2 * SEQS, 2, 2, CN])
        Sb = sb("Sb", [2 * SEQS, 2, 2, CN])
        Z = sb("Z", [2 * SEQS, CL + 1, 4, CN])
        Zb = sb("Zb", [2 * SEQS, CL + 1, 4, CN])
        Pr = sb("Pr", [2 * SEQS, CN, CL + 1])
        Pi = sb("Pi", [2 * SEQS, CN, CL + 1])
        ra, rb = sb("ra", [2 * SEQS, P]), sb("rb", [2 * SEQS, P])
        rc, rd = sb("rc", [2 * SEQS, P]), sb("rd", [2 * SEQS, P])
        frac = sb("frac", [2 * SEQS, 2, P])
        neg_id = sb("neg_id", [SEQS, SEQS])
        fold_id = sb("fold_id", [2 * SEQS, SEQS])
        den = sb("den", [P, 2, SEQS])
        ga, gb = sb("ga", [P, SEQS]), sb("gb", [P, SEQS])

        ctx.close()
        ctx = group_ctx
        xbk = sb("xbk", [P, T, P])
        xqT = sb("xqT", [P, GT])
        x1 = sb("x1", [P, T, P])
        xf = sb("xf", [P, T, P])
        x1b = sb("x1b", [P, T, P])
        x2 = sb("x2", [P, T, P])
        xsum = xf
        xn = sb("xn", [P, T, P])
        xnT = sb("xnT", [P, GT])
        stats = sb("stats", [P, T, 6])
        mv = sb("mv", [P, T, 2])
        vare = sb("vare", [P, T])
        rstd = sb("rstd", [P, T])
        qT, kT = sb("qT", [P, PAIRS, GT]), sb("kT", [P, PAIRS, GT])
        cumg = sb("cumg", [P, T, P])
        decay = sb("decay", [P, T, P])
        mix = sb("mix", [P, 2, 4 * XC * P])
        pT = [mix[:, n, :].rearrange("p (i c n) -> p i c n", i=4, c=XC) for n in range(2)]
        v_sb = mix[:, 0, :].rearrange("p (t n) -> p t n", t=T)
        at = [mix[:, 1, n * GT * 2:(n + 1) * GT * 2].rearrange("p (r a n) -> p r a n", r=2, a=PAIRS)
              for n in range(2)]
        hebT = [sb(f"hebT{n}", [P, PAIRS, P]) for n in range(2)]
        hT = sb("hT", [P, FC, GT])
        ctxT = sb("ctxT", [P, GT])
        xa = sb("xa", [P, T, P])
        xab = sb("xab", [P, T, P])
        qp = kp = hT
        high = [sb(f"high{n}", [P, GT], F32R) for n in range(2)]
        qr, kr = sb("qr", [P, XC, GT], F32R), sb("kr", [P, XC, GT], F32R)
        qm = [sb(f"qm{n}", [P, XC, P], F32R) for n in range(2)]
        cT = [sb(f"cT{n}", [P, XC, P]) for n in range(2)]
        rsum = sb("rsum", [P, T, XH])
        cx = sb("cx", [P, T, XH, XD])
        cxT = sb("cxT", [P, GT])
        xb = sb("xb", [P, T, P])
        top8 = sb("top8", [P, T, 8])
        lg = sb("lg", [P, T, EXP])
        top_i = sb("top_i", [P, T, 8], U32)
        top_f = sb("top_f", [P, T, TOPK])
        onehot = sb("onehot", [P, T, TOPK, EXP], BF16)
        chosen = sb("chosen", [P, T, EXP], BF16)
        below = sb("below", [P, T])
        ratio = sb("ratio", [P, T])
        wsum, wrec = sb("wsum", [P, T]), sb("wrec", [P, T])
        places = sb("places", [P, T, EXP])
        picked = sb("picked", [P, T, TOPK, EXP])
        slot_f = sb("slot_f", [P, T, TOPK])
        slot_u = sb("slot_u", [P, T, TOPK], U32)

        xt = [xn[:, n, :] for n in range(UNROLL)]
        xtT = [xnT[:, n * P:(n + 1) * P] for n in range(2)]
        w1c = [qT[:, :, :].rearrange("p a n -> p (a n)")[:, n * (FF + FC):(n + 1) * (FF + FC)]
               for n in range(2)]
        hx = [hT[:, :, n * P:(n + 1) * P] for n in range(2)]
        ysb = [xa[:, n, :] for n in range(UNROLL)]
        home = sb("home", [P, 2 * UNROLL], U32)
        begun, begun_w = (kT[0:1, n, 0:(EXP - 1) * TILES].rearrange("p (e j) -> p e j", e=EXP - 1)
                          for n in range(2))
        two_rows = [mix[:, m // 2, m % 2 * 2 * GT:(m % 2 + 1) * 2 * GT].rearrange(
            "p (t k n) -> p t k n", t=T, k=TOPK) for m in range(4)]
        acc = [x1, x1b, xbk, cumg]
        mvc, varec, rstdc, shiftc = (
            [sb(f"{name}{m}", [P, T] + dims) for m in range(4)]
            for name, dims in (("mvc", [2]), ("varec", []), ("rstdc", []), ("shiftc", [])))
        part = [xf, xab]
        out_tiles = [x2, xb]

        full = [sem(f"bank{n}_full") for n in range(NB)]
        free = [sem(f"bank{n}_drained") for n in range(NB)]
        pre_loaded = sem("pre_loaded")
        xT_loaded = [sem(f"xT_loaded{q}") for q in range(4)]
        experts_loaded = sem("experts_loaded")
        x_loaded = [sem(f"x_loaded{q}") for q in range(4)]
        weights_loaded = sem("weights_loaded")
        ctx_loaded = sem("ctx_loaded")
        zseq_loaded = sem("zseq_loaded")
        mask_loaded, maskb_ready = sem("mask_loaded"), sem("maskb_ready")
        pool_const = sem("pool_const")
        wpotg_ready, wpotc_ready = sem("wpotg_ready"), sem("wpotc_ready")
        wmean_mm, potbias_mm, potbias_ready = sem("wmean_mm"), sem("potbias_mm"), sem("potbias_ready")
        lnb_ready, cols_ready = sem("lnb_ready"), sem("cols_ready")
        zrow_mm, zrow_copied = sem("zrow_mm"), sem("zrow_copied")
        bn1_ready, mv1_ready, vare1_ready, rstd1_ready = (
            sem("bn1_ready"), sem("mv1_ready"), sem("vare1_ready"), sem("rstd1_ready"))
        zpos_mm, zlink = sem("zpos_mm"), sem("zlink")
        z_ready, zln_ready, gamma_ready = sem("z_ready"), sem("zln_ready"), sem("gamma_ready")
        abs_done, exp_done = sem("abs_done"), sem("exp_done")
        drow_mm, scan_link, frac_ready, den_mm, green_ready = (
            sem("drow_mm"), sem("scan_link"), sem("frac_ready"), sem("den_mm"), sem("green_ready"))
        folded = sem("folded")
        bias_mm, bias_ready = sem("bias_mm"), sem("bias_ready")
        xbk_ready = sem("xbk_ready")
        x1_part = sem("x1_part")
        cumg_ready = sem("cumg_ready")
        sum_ready = sem("sum_ready")
        bn_ready = sem("bn_ready")
        mv_ready = sem("mv_ready")
        vare_ready = sem("vare_ready")
        rstd_ready = sem("rstd_ready")
        xn_ready = sem("xn_ready")
        x1b_ready, xf_ready, xsum_ready, xab_ready = (
            sem("x1b_ready"), sem("xf_ready"), sem("xsum_ready"), sem("xab_ready"))
        qhigh_ready, khigh_ready = sem("qhigh_ready"), sem("khigh_ready")
        qr_ready, kr_ready = sem("qr_ready"), sem("kr_ready")
        rsum_ready = sem("rsum_ready")
        below_ready, ratio_ready, route_link = sem("below_ready"), sem("ratio_ready"), sem("route_link")
        places_ready = sem("places_ready")
        chosen_ready, slot_ready = sem("chosen_ready"), sem("slot_ready")
        xkept = sem("xkept")
        home_free = sem("home_free")
        spare_filled, home_copied, home_scattered = (
            sem("spare_filled"), sem("home_copied"), sem("home_scattered"))
        scattered, xb_free = sem("scattered"), sem("xb_free")
        table_link, table_ready = sem("table_link"), sem("table_ready")
        padded, ends_ready = sem("padded"), sem("ends_ready")
        x_in = [sem(f"x_in{n}") for n in range(UNROLL)]
        home_in = [sem(f"home_in{n}") for n in range(2 * UNROLL)]
        y_out = [sem(f"y_out{n}") for n in range(UNROLL)]
        turned, turned_copied = sem("turned"), sem("turned_copied")
        w1_in, h_mm, gelu_done, y_mm, y_added = (
            sem("w1_in"), sem("h_mm"), sem("gelu_done"), sem("y_mm"), sem("y_added"))
        combined = sem("combined")
        y_back = [sem(f"y_back{n}") for n in range(4)]
        bnc_ready, mvc_ready, varc_ready, rstdc_ready, outc_ready = (
            sem("bnc_ready"), sem("mvc_ready"), sem("varc_ready"),
            sem("rstdc_ready"), sem("outc_ready"))
        stored = [sem(f"stored{n}") for n in range(2)]
        dve_held, pool_held, sp_held, act_held = (
            sem("dve_held"), sem("pool_held"), sem("sp_held"), sem("act_held"))
        part_ready, sum0_ready = sem("part_ready"), sem("sum0_ready")

        LN3, LN2, LNA, LNB = range(4)
        NLN = 4 * T
        xs = nc.dram_tensor("expert_in", (EXP * REGION, P), F32, kind="Internal").ap()
        homes = nc.dram_tensor("expert_home", (EXP * REGION + GT * TOPK, 1), U32, kind="Internal").ap()
        ys = nc.dram_tensor("expert_out", (SEQS * P * TOPK + EXP * REGION, P), F32, kind="Internal").ap()

        def nth(g, name):
            b = BANK[name]
            return NTH_FIRST[name] if g is None else g * PER_GROUP[b] + (FIRST[b] + NTH[name])

        def take(pe, g, name):
            b = BANK[name]
            pe.wait_ge(free[b], nth(g, name) + 1)
            return bank[b]

        def filled(eng, g, name):
            b = BANK[name]
            eng.wait_ge(full[b], nth(g, name) + 1)
            return bank[b]

        def drained(eng, g, name):
            eng.wait_ge(free[BANK[name]], nth(g, name) + 2)

        def pad(eng, experts):
            for e in experts:
                n_pad = 1 if e < EXP - 1 else TILES - SEQS * TOPK + 1
                end = eng.value_load(ends_i[0:1, e:e + 1], min_val=e * REGION, max_val=e * REGION + SEQS * P)
                eng.dma_start(xs[bass.ds(end, n_pad * P), :].rearrange("(a p) n -> p a n", p=P),
                              zeros[:, :].unsqueeze(1).broadcast_to([P, n_pad, P])).then_inc(padded, 16)

        def ln_nth(g, stage, t):
            return t if g is None else g * NLN + (T + stage * T + t)

        block = ctx.enter_context(nc.Block())

        PRE_LOADS = [
            (w_pot[:, :], A["w_pot"]), (b_pot[:, :], A["b_pot"]),
            (ln1_g[:, :], A["ln1_g"]), (ln1_b[:, :], A["ln1_b"]), (ident[:, :], A["ident"]),
            (antid[:, :], A["antid"]), (fold_id[:, :], A["fold_id"]),
        ]
        LOADS = [
            (tri[:, :], A["tri"]), (after[:, :], A["after"]), (future[:, :], A["future"]),
            (pos_only[:, :], A["pos_only"]),
            (ln2_g[:, :], A["ln2_g"]), (ln2_b[:, :], A["ln2_b"]),
            (ln3_g[:, :], A["ln3_g"]), (ln3_b[:, :], A["ln3_b"]),
            (w_bk_bc[:, 0, :], A["w_bk"][0:1, :].broadcast_to([P, P])),
            (w_bk_bc[:, 1, :], A["w_bk"][1:2, :].broadcast_to([P, P])),
            (b_bk_bc[:, :], A["b_bk"].broadcast_to([P, P])),
            (w_qkv[:, :], A["w_qkv"]), (b_qk[:, :], A["b_qk"]), (b_v_row[:, :], A["b_v"]),
            (w_out[:, :, :], A["w_out"]), (b_out_bc[:, :], A["b_out"].broadcast_to([P, P])),
            (w_ff1[:, :], A["w_ff1"]), (b_ff1[:, :], A["b_ff1"]), (w_ff2[:, :, :], A["w_ff2"]),
            (b_ff2_bc[:, :], A["b_ff2"].broadcast_to([P, P])),
            (wq_pad[:, :, :], A["wq_pad"]), (wk_pad[:, :, :], A["wk_pad"]),
            (bq_pad[:, :], A["bq_pad"]), (bk_pad[:, :], A["bk_pad"]),
            (q_ones[:, :], A["q_ones"]), (k_ones[:, :], A["k_ones"]),
            (low_rows[:, :], A["low_rows"]),
            (wv_t[:, :], A["wv_t"]), (wo_t[:, :], A["wo_t"]), (bv_col[:, :], A["bv"]),
            (bo_row[:, :], A["bo"]), (wr_t[:, :], A["wr_t"]),
            (iota_e[:, :], A["iota_e"].broadcast_to([P, EXP])), (iota_t[:, :], A["iota_t"]),
            (home_all[:, :, :], A["home"]), (home_now[:, :, :], A["home"][:, 0:T, :]),
            (slot_u[:, :, :], A["no_slot"]),
            (slot_base[:, :], A["slot_base"].broadcast_to([P, EXP])),
        ]
        EXPERT_LOADS = [
            (w1_t[:, :, :], A["w1_t"]), (w2_t[:, :, :, :], A["w2_t"]),
            (b2_bc[:, :, :], A["b2"].unsqueeze(0).broadcast_to([P, EXP, P])),
        ]

        @block.sync
        def _(sp):
            for dst, src in PRE_LOADS:
                sp.dma_start(dst, src).then_inc(pre_loaded, 16)
            for q in range(4):
                part = slice(q * 2 * GT, (q + 1) * 2 * GT)
                sp.dma_start(xT_all[:, part], A["xT"][:, part]).then_inc(xT_loaded[q], 16)
            for q in range(4):
                sp.dma_start(x_all[:, 8 * q:8 * q + 8, :],
                             A["x"][:, 8 * q:8 * q + 8, :]).then_inc(x_loaded[q], 16)
            for dst, src in LOADS:
                sp.dma_start(dst, src).then_inc(weights_loaded, 16)
            sp.dma_start(homes[0:EXP * REGION, :].rearrange("(p n) a -> p (n a)", p=P),
                         A["spare"].rearrange("(p n) a -> p (n a)", p=P)).then_inc(spare_filled, 16)
            sp.wait_ge(green_ready, 1)
            sp.dma_start(ctxT[:, :], A["ctxT"][:, 0:GT]).then_inc(ctx_loaded, 16)
            sp.dma_start(mask_i[:, :], A["mask"][:, 0:GT]).then_inc(mask_loaded, 16)
            with sp.Fori(0, G - 1) as g:
                filled(sp, g, "cv")
                sp.dma_start(ctxT[:, :], A["ctxT"][:, bass.ds(g * GT + GT, GT)]).then_inc(ctx_loaded, 16)
                sp.dma_start(mask_i[:, :], A["mask"][:, bass.ds(g * GT + GT, GT)]).then_inc(mask_loaded, 16)
                sp.wait_ge(home_scattered, g * (16 * T * TOPK) + 16 * T * TOPK)
                sp.sem_inc(home_free, 1)
                sp.wait_ge(scattered, g * (16 * T * TOPK) + 16 * T * TOPK)
                sp.sem_inc(xb_free, 1)

            filled(sp, G - 1, "cv")
            sp.dma_start(ctxT[:, :], A["ctxT"][:, 0:GT]).then_inc(ctx_loaded, 16)
            sp.dma_start(mask_i[:, :], A["mask"][:, 0:GT]).then_inc(mask_loaded, 16)

            sp.wait_ge(home_scattered, 16 * SEQS * TOPK)
            sp.sem_inc(home_free, 1)

            def row_of(j):
                return sp.value_load(tab[0:1, 1, bass.ds(j, 1)], min_val=0, max_val=EXP * REGION - P)

            sp.wait_ge(ends_ready, 1)
            pad(sp, range(0, EXP, 2))
            sp.wait_ge(table_ready, 1)
            rows = [row_of(n) for n in range(UNROLL)]
            sp.wait_ge(padded, 16 * EXP)
            sp.wait_ge(scattered, 16 * SEQS * TOPK)

            def row_in(j, n, row):
                sp.wait_ge(turned, j + 1)
                sp.sem_inc(sp_held, 1)
                sp.dma_start(xt[n % UNROLL], xs[bass.ds(row, P), :]).then_inc(x_in[n % UNROLL], 16)

            def home_of(n, row, pace):
                if pace is not None:
                    sp.wait_ge(y_out[n % UNROLL], pace)
                    sp.sem_inc(sp_held, 1)
                sp.dma_start(home[:, n:n + 1], homes[bass.ds(row, P), :]).then_inc(home_in[n], 16)

            for n in range(UNROLL):
                row_in(n, n, rows[n])
            sp.wait_ge(home_scattered, 16 * (SEQS + T) * TOPK)
            for n in range(UNROLL):
                home_of(n, rows[n], None)
            for n in range(UNROLL, 2 * UNROLL):
                row = row_of(n)
                row_in(n, n, row)
                home_of(n, row, None)
            with sp.Fori(0, TILES // (2 * UNROLL) - 1) as i:
                for n in range(2 * UNROLL):
                    j = i * (2 * UNROLL) + (2 * UNROLL + n)
                    row = row_of(j)
                    row_in(j, n, row)
                    home_of(n, row, i * 32 + (16 + 16 * (n // UNROLL)))

            for n in range(UNROLL):
                sp.wait_ge(y_out[n], 16 * (TILES // UNROLL))
            both = ys[0:SEQS * P * TOPK, :].rearrange("(s p k) n -> p s (k n)", p=P, k=TOPK)

            def rows_back(g, n):
                sp.wait_ge(combined, g * T + T)
                sp.sem_inc(sp_held, 1)
                sp.dma_start(two_rows[n].rearrange("p t k n -> p t (k n)"), both[:, bass.ds(g * T, T), :]
                             ).then_inc(y_back[n], 16)

            def store(g, n):
                sp.wait_ge(outc_ready, g + 1 + 4)
                sp.sem_inc(sp_held, 1)
                sp.dma_start(A["out"][:, bass.ds(g * T, T), :], out_tiles[n][:, :, :]).then_inc(stored[n], 16)

            for g in range(4):
                rows_back(g, g)
            with sp.Fori(0, G // 4 - 1) as i:
                for m in range(4):
                    store(i * 4 + m, m % 2)
                    rows_back(i * 4 + (m + 4), m)
            for g in range(G - 4, G):
                store(g, g % 2)
            for n in range(2):
                sp.wait_ge(stored[n], 16 * (G // 2) + 1)

        @block.scalar
        def _(act):
            for n in range(G):
                act.wait_ge(zrow_mm, n + 1)
                nc.scalar.activation(zpot_row[:, n * GT:(n + 1) * GT], bank[n % 2][0:2, :],
                                     ACT.Copy).then_inc(zrow_copied, 1)
            act.wait_ge(zrow_copied, G)
            for n in range(2):
                act.dma_start(zpot_seq[SEQS * n:SEQS * n + SEQS, :],
                              zpot_row[n:n + 1, :].rearrange("a (s p) -> a s p", p=P)
                              ).then_inc(zseq_loaded, 16)
            act.wait_ge(zseq_loaded, 32)
            for dst, src in EXPERT_LOADS:
                act.dma_start(dst, src).then_inc(experts_loaded, 16)
            act.wait_ge(z_ready, 1)
            nc.scalar.activation(zabs[:, :], zpot[:, 1, :], ACT.Abs).then_inc(abs_done, 1)
            act.wait_ge(abs_done, 1)
            nc.scalar.activation(zln[:, :], zabs[:, :], ACT.Exp, scale=-1.0).then_inc(exp_done, 1)
            act.wait_ge(exp_done, 1)
            nc.scalar.activation(zabs[:, :], zln[:, :], ACT.Ln, bias=1.0).then_inc(zln_ready, 1)
            act.wait_ge(bias_ready, 4)
            act.wait_ge(folded, 12)

            def drain(g, name, dst, func=ACT.Copy, bias=None, scale=1.0, src=None):
                b = filled(act, g, name)
                src_ap = b[:, :] if src is None else src(b)
                kw = {} if bias is None else {"bias": bias}
                nc.scalar.activation(dst, src_ap, func, scale=scale, **kw).then_inc(free[BANK[name]], 1)

            def turned_and_decay(g):
                drain(g, "xh2T", xqT[:, :])
                drain(g, "decay", decay[:, :, :].rearrange("p t n -> p (t n)"), ACT.Exp, scale=-DT)

            def queries(g, p):
                drain(g, f"q{p}", qT[:, p, :], ACT.Identity, bias=bg_qk[:, p:p + 1])

            def split(g, name, c, full, bias, high_ready, before):
                b = filled(act, g, name)
                if before is not None:
                    act.wait_ge(*before)
                nc.scalar.activation(high[c % 2][:, :], b[:, :], ACT.Identity, bias=bias
                                     ).then_inc(high_ready, 1)
                nc.scalar.activation(full, b[:, :], ACT.Identity, bias=bias
                                     ).then_inc(free[BANK[name]], 1)

            def split_keys(g, k, c):
                if c >= 2:
                    before = (kr_ready, k * XC + c - 1)
                else:
                    before = None if g is None else (qr_ready, g * XC + c + 3)
                split(g, f"kp{c}", c, kp[:, c, :], bk_pad[:, c:c + 1], khigh_ready, before)

            def split_queries(g, c):
                before = (qr_ready, g * XC + c - 1) if c >= 2 else (kr_ready, g * XC + c + 3)
                split(g, f"qp{c}", c, qp[:, c, :], bq_pad[:, c:c + 1], qhigh_ready, before)

            turned_and_decay(None)
            for p in range(PAIRS):
                queries(None, p)
            split_keys(None, 0, 0)
            split_keys(None, 0, 1)

            with act.Fori(0, G) as g:
                for t in range(T):
                    drain(g, f"hpv{t}", hebT[t % 2][:, :, :].rearrange("p a n -> p (a n)"))
                    if t in (0, 2):
                        split_keys(g, g, 2 + t // 2)
                drain(g, "cv", vpad[:, :, :, 0:XD].rearrange("p t h d -> p (t h) d"),
                      src=lambda b: b[:, :].rearrange("p (n d) -> p n d", d=XD))
                drain(g, "xh3T", xnT[:, :])
                act.wait_ge(kr_ready, g * XC + XC)
                for c in range(FC):
                    drain(g, f"ff1c{c}", hT[:, c, :], ACT.Gelu_apprx_tanh, bias=bg_ff1[:, c:c + 1])
                turned_and_decay(g)
                drain(g, "xaT", xnT[:, :])
                for c in range(XC):
                    split_queries(g, c)
                queries(g, 0)
                queries(g, 1)
                for t in range(T):
                    for i in range(4):
                        drain(g, f"st{t}i{i}", pT[t % 2][:, i, :, :].rearrange("p c n -> p (c n)"), ACT.Exp)
                    drain(g, f"xpv{t}", cT[t % 2][:, :, :].rearrange("p c n -> p (c n)"))
                    if t < 2:
                        queries(g, 2 + t)
                drain(g, "cxT", cxT[:, :])
                drain(g, "xbT", xnT[:, :])
                act.wait_ge(below_ready, g + 1)
                nc.scalar.activation(ratio[:, :], below[:, :], ACT.Exp).then_inc(ratio_ready, 1)
                split_keys(g, g + 1, 0)
                split_keys(g, g + 1, 1)

            act.wait_ge(ends_ready, 1)
            pad(act, range(1, EXP, 2))

            act.sem_inc(gelu_done, 2)

            def gelu(j, n):
                act.wait_ge(h_mm, j + 1 + 2)
                act.wait_ge(y_mm, j + 1)
                for c in range(FC):
                    ins = nc.scalar.activation(hx[n][:, c, :], bank[2 + n][:, c * P:(c + 1) * P], ACT.Gelu,
                                               bias=w1c[n][:, FF + c:FF + c + 1])
                ins.then_inc(gelu_done, 1)

            in_turn = 6 * UNROLL
            with act.Fori(0, TILES // in_turn) as i:
                for n in range(in_turn):
                    gelu(i * in_turn + n, n % 2)

            def first_part(g, m, turns):
                n = m % 2
                act.wait_ge(y_back[m], turns)
                act.wait_ge(sum0_ready, g + 1)
                act.sem_inc(act_held, 1)
                for t in range(T):
                    ins = nc.scalar.activation(part[n][:, t, :], two_rows[m][:, t, 0, :], ACT.Copy,
                                               scale=gate_all[:, bass.ds(g * T + t, 1), 0])
                ins.then_inc(part_ready, 1)

            def last_norm(g, m, stores):
                n = m % 2
                act.wait_ge(rstdc_ready, g + 1)
                act.wait_ge(stored[n], stores)
                for t in range(T):
                    ins = nc.scalar.activation(out_tiles[n][:, t, :], acc[m][:, t, :], ACT.Identity,
                                               scale=rstdc[m][:, t:t + 1], bias=shiftc[m][:, t:t + 1])
                ins.then_inc(outc_ready, 1)

            first_part(0, 0, 16)
            first_part(1, 1, 16)
            with act.Fori(0, G // 4 - 1) as i:
                for m in range(4):
                    first_part(i * 4 + (m + 2), (m + 2) % 4, i * 16 + (16 + 16 * ((m + 2) // 4)))
                    last_norm(i * 4 + m, m, i * 32 + (16 * (m // 2) + 1))
            for g in range(G - 4, G):
                if g + 2 < G:
                    first_part(g + 2, (g + 2) % 4, 16 * (G // 4))
                last_norm(g, g % 4, 16 * (g // 2) + 1)

        @block.gpsimd
        def _(pool):
            nc.gpsimd.memset(ones[:, :], 1.0).then_inc(pool_const, 1)
            nc.gpsimd.memset(mean_w[:, :], 1.0 / P).then_inc(pool_const, 1)
            nc.gpsimd.memset(minus_half[:, :], -0.5).then_inc(pool_const, 1)
            nc.gpsimd.memset(Y[:, 0:2, :, :, :], 0.0).then_inc(pool_const, 1)
            nc.gpsimd.memset(S[:, 0, :], 0.0).then_inc(pool_const, 1)
            nc.gpsimd.memset(vpad[:, :, :, :], 0.0).then_inc(pool_const, 1)
            nc.gpsimd.memset(zeros[:, :], 0.0).then_inc(pool_const, 1)
            nc.gpsimd.memset(ones_b[:, :], 1.0).then_inc(pool_const, 1)
            for n in range(2):
                nc.gpsimd.memset(negmax[n][:, :, :], 0.0).then_inc(pool_const, 1)
            pool.wait_ge(pool_const, 10)
            nc.gpsimd.memset(Y[:, 0, 0, 0, :], 1.0).then_inc(pool_const, 1)
            nc.gpsimd.memset(Y[:, 1, 1, 0, :], 1.0).then_inc(pool_const, 1)
            nc.gpsimd.memset(S[:, 0, 2:3], 1.0).then_inc(pool_const, 1)
            nc.gpsimd.memset(vpad[:, :, :, XD:XD + 1], 1.0).then_inc(pool_const, 1)
            pool.wait_ge(mv1_ready, 1)
            nc.gpsimd.tensor_scalar(rstd1[:, :], mv1[:, :, 1], EPS, None, ALU.add).then_inc(vare1_ready, 1)
            pool.wait_ge(vare1_ready, 1)
            nc.gpsimd.tensor_tensor(rstd1[:, :], rstd1[:, :], minus_half[:, :], ALU.pow
                                    ).then_inc(rstd1_ready, 1)
            pool.wait_ge(weights_loaded, 16 * len(LOADS))
            nc.gpsimd.tensor_scalar(lnb_cols[:, 1, :], ones[:, :], ln2_b[:, 0:1], None, ALU.mult
                                    ).then_inc(cols_ready, 1)
            nc.gpsimd.tensor_scalar(lnb_cols[:, 2, :], ones[:, :], bv_col[:, 0:1], None, ALU.mult
                                    ).then_inc(cols_ready, 1)
            nc.gpsimd.tensor_scalar(w_out[:, :, :], w_out[:, :, :], ETA, None, ALU.mult).then_inc(folded, 1)
            nc.gpsimd.tensor_scalar(wq_pad[:, :, :], wq_pad[:, :, :], XSCALE, None, ALU.mult).then_inc(folded, 1)
            nc.gpsimd.tensor_copy(ident_b[:, :], ident[:, :]).then_inc(folded, 1)
            nc.gpsimd.tensor_copy(future_b[:, :], future[:, :]).then_inc(folded, 1)
            nc.gpsimd.tensor_copy(pos_only_b[:, :], pos_only[:, :]).then_inc(folded, 1)
            nc.gpsimd.tensor_copy(tri_b[:, :], tri[:, :]).then_inc(folded, 1)
            nc.gpsimd.tensor_copy(counts[:, :], slot_base[:, :]).then_inc(folded, 1)
            nc.gpsimd.memset(x_all[:, SEQS:, :], 0.0).then_inc(folded, 1)
            pool.wait_ge(bias_mm, 3)
            pool.sem_inc(pool_held, 1)
            nc.gpsimd.tensor_scalar(w_qkv[:, :], w_qkv[:, :], ln2_g[:, 0:1], None, ALU.mult).then_inc(folded, 1)
            nc.gpsimd.tensor_scalar(w_ff1[:, :], w_ff1[:, :], ln3_g[:, 0:1], None, ALU.mult).then_inc(folded, 1)
            pool.wait_ge(green_ready, 1)
            for q in range(4):
                pool.wait_ge(x_loaded[q], 16)
            pool.wait_ge(spare_filled, 16)

            def ln_scale(g, stage, t):
                n = ln_nth(g, stage, t)
                pool.wait_ge(mv_ready, n + 1)
                pool.sem_inc(pool_held, 1)
                nc.gpsimd.tensor_scalar(vare[:, t:t + 1], mv[:, t, 1:2], EPS, None, ALU.add
                                        ).then_inc(vare_ready, 1)
                pool.wait_ge(vare_ready, n + 1)
                nc.gpsimd.tensor_tensor(rstd[:, t:t + 1], vare[:, t:t + 1], minus_half[:, 0:1],
                                        ALU.pow).then_inc(rstd_ready, 1)

            def first_sums(k):
                nc.gpsimd.tensor_tensor(
                    xbk[:, :, :], x_all[:, bass.ds(k * T, T), :],
                    b_bk_bc[:, :].unsqueeze(1).broadcast_to([P, T, P]), ALU.add).then_inc(xbk_ready, 1)
                nc.gpsimd.tensor_tensor(
                    cumg[:, :, :], gamma[:, bass.ds(k * T, T)].unsqueeze(2).broadcast_to([P, T, P]),
                    tri[:, :].unsqueeze(1).broadcast_to([P, T, P]), ALU.mult).then_inc(cumg_ready, 1)

            def masks(k):
                pool.wait_ge(mask_loaded, k * 16 + 16)
                pool.sem_inc(pool_held, 1)
                nc.gpsimd.tensor_copy(mask_b[:, :], mask_i[:, :]).then_inc(maskb_ready, 1)

            def residuals(k):
                nc.gpsimd.tensor_tensor(
                    x1b[:, :, :], x1[:, :, :],
                    b_out_bc[:, :].unsqueeze(1).broadcast_to([P, T, P]), ALU.add).then_inc(x1b_ready, 1)
                nc.gpsimd.tensor_tensor(
                    xf[:, :, :], x_all[:, bass.ds(k * T, T), :],
                    b_ff2_bc[:, :].unsqueeze(1).broadcast_to([P, T, P]), ALU.add).then_inc(xf_ready, 1)

            first_sums(0)
            masks(0)
            for t in range(T):
                ln_scale(None, LN2, t)
            residuals(0)

            def homes_out():
                for t in range(T):
                    for k in range(TOPK):
                        nc.gpsimd.indirect_dma_start(
                            homes[:, :], bass.IndirectOffsetOnAxis(ap=slot_u[:, t, k:k + 1], axis=0),
                            home_now[:, t, k:k + 1], None).then_inc(home_scattered, 16)

            with pool.Fori(0, G) as g:
                for t in range(T):
                    ln_scale(g, LN3, t)
                first_sums(g + 1)
                pool.wait_ge(xf_ready, g + 1)
                nc.gpsimd.tensor_tensor(xsum[:, :, :], xf[:, :, :], x2[:, :, :], ALU.add
                                        ).then_inc(xsum_ready, 1)
                for t in range(T):
                    ln_scale(g, LN2, t)
                for t in range(T):
                    ln_scale(g, LNA, t)
                pool.wait_ge(xn_ready, ln_nth(g, LNA, T - 1) + 1)
                nc.gpsimd.tensor_tensor(
                    xab[:, :, :], xa[:, :, :],
                    bo_bc[:, :].unsqueeze(1).broadcast_to([P, T, P]), ALU.add).then_inc(xab_ready, 1)
                homes_out()
                filled(pool, g, "cv")
                masks(g + 1)
                residuals(g + 1)
                for t in range(T):
                    ln_scale(g, LNB, t)
                pool.wait_ge(xn_ready, ln_nth(g, LNB, T - 1) + 1)
                pool.sem_inc(pool_held, 1)
                nc.gpsimd.tensor_copy(x_all[:, bass.ds(g * T, T), :], xb[:, :, :]).then_inc(xkept, 1)
                pool.wait_ge(home_free, g + 1)
                pool.sem_inc(pool_held, 1)
                nc.gpsimd.tensor_copy(home_now[:, :, :], home_all[:, bass.ds(g * T, T), :]
                                      ).then_inc(home_copied, 1)
                pool.wait_ge(slot_ready, g + 1)
                pool.wait_ge(home_copied, g + 1)
                pool.sem_inc(pool_held, 1)
                for t in range(T):
                    for k in range(TOPK):
                        nc.gpsimd.indirect_dma_start(
                            xs[:, :], bass.IndirectOffsetOnAxis(ap=slot_u[:, t, k:k + 1], axis=0),
                            xb[:, t, :], None).then_inc(scattered, 16)

            homes_out()

            def results_out(j, n, first):
                pool.wait_ge(y_added, j + 1 + 2)
                pool.wait_ge(home_in[n], first)
                pool.sem_inc(pool_held, 1)
                nc.gpsimd.indirect_dma_start(
                    ys[:, :], bass.IndirectOffsetOnAxis(ap=home[:, n:n + 1], axis=0),
                    ysb[n % UNROLL], None).then_inc(y_out[n % UNROLL], 16)

            with pool.Fori(0, TILES // (2 * UNROLL)) as i:
                for n in range(2 * UNROLL):
                    results_out(i * (2 * UNROLL) + n, n, i * 16 + 16)

            def first_sum(g, m):
                n = m % 2
                pool.wait_ge(part_ready, g + 1)
                pool.wait_ge(outc_ready, g + 1)
                pool.sem_inc(pool_held, 1)
                nc.gpsimd.tensor_tensor(acc[m][:, :, :], part[n][:, :, :], x_all[:, bass.ds(g * T, T), :],
                                        ALU.add).then_inc(sum0_ready, 1)

            def last_scale(g, m):
                pool.wait_ge(mvc_ready, g * T + T)
                pool.sem_inc(pool_held, 1)
                nc.gpsimd.tensor_scalar(varec[m][:, :], mvc[m][:, :, 1], EPS, None, ALU.add
                                        ).then_inc(varc_ready, 1)
                pool.wait_ge(varc_ready, g * 3 + 1)
                nc.gpsimd.tensor_tensor(rstdc[m][:, :], varec[m][:, :], minus_half[:, 0:T], ALU.pow
                                        ).then_inc(varc_ready, 1)
                pool.wait_ge(varc_ready, g * 3 + 2)
                nc.gpsimd.tensor_tensor(shiftc[m][:, :], mvc[m][:, :, 0], rstdc[m][:, :], ALU.mult
                                        ).then_inc(varc_ready, 1)
                pool.wait_ge(varc_ready, g * 3 + 3)
                pool.sem_inc(pool_held, 1)
                nc.gpsimd.tensor_scalar(shiftc[m][:, :], shiftc[m][:, :], -1.0, None, ALU.mult
                                        ).then_inc(rstdc_ready, 1)

            pool.sem_inc(sum0_ready, 2)
            pool.sem_inc(outc_ready, 4)
            first_sum(0, 0)
            with pool.Fori(0, G // 4 - 1) as i:
                for m in range(4):
                    first_sum(i * 4 + (m + 1), (m + 1) % 4)
                    last_scale(i * 4 + m, m)
            for g in range(G - 4, G):
                if g + 1 < G:
                    first_sum(g + 1, (g + 1) % 4)
                last_scale(g, g % 4)

        @block.vector
        def _(dve):
            nc.vector.memset(gamma[:, SEQS:], 0.0).then_inc(scan_link, 1)
            nc.vector.memset(green[:, :, SEQS:], 0.0).then_inc(scan_link, 1)
            dve.wait_ge(pre_loaded, 16 * len(PRE_LOADS))
            dve.wait_ge(pool_const, 14)
            nc.vector.tensor_scalar(w_potg[:, :], w_pot[:, :], ln1_g[:, 0:1], None, ALU.mult
                                    ).then_inc(wpotg_ready, 1)
            nc.vector.tensor_scalar(lnb_cols[:, 0, :], ones[:, :], ln1_b[:, 0:1], None, ALU.mult
                                    ).then_inc(lnb_ready, 1)
            dve.wait_ge(wmean_mm, 1)
            nc.vector.tensor_tensor(w_potc[:, :], w_potg[:, :], bank[2][:, 0:2], ALU.subtract
                                    ).then_inc(wpotc_ready, 1)
            dve.wait_ge(potbias_mm, 1)
            nc.vector.tensor_copy(pot_bias[:, :], bank[3][:, 0:2]).then_inc(potbias_ready, 1)
            for q in range(4):
                dve.wait_ge(x_loaded[q], 16)
                for n in range(8 * q, 8 * q + 8):
                    nc.vector.bn_stats(st1[:, n, :], x_all[:, n, :]).then_inc(bn1_ready, 1)
            dve.wait_ge(bn1_ready, SEQS)
            for n in range(SEQS):
                last = nc.vector.bn_aggr(mv1[:, n, :], st1[:, n, :])
            last.then_inc(mv1_ready, 1)
            dve.wait_ge(zpos_mm, 1)
            dve.wait_ge(rstd1_ready, 1)
            dve.wait_ge(potbias_ready, 1)
            nc.vector.tensor_tensor(
                zpot[:, :, :], bank[4][:, 0:2 * SEQS].rearrange("p (a s) -> p a s", a=2),
                rstd1[:, :].unsqueeze(1).broadcast_to([P, 2, SEQS]), ALU.mult).then_inc(zlink, 1)
            dve.wait_ge(zlink, 1)
            nc.vector.tensor_scalar(zpot[:, 1, :], zpot[:, 1, :], pot_bias[:, 1:2], None, ALU.add
                                    ).then_inc(z_ready, 1)
            nc.vector.tensor_scalar(diag[:, 0, :], zpot[:, 0, :], pot_bias[:, 0:1], 2.0, ALU.add,
                                    ALU.add).then_inc(zlink, 1)
            dve.wait_ge(zln_ready, 1)
            dve.wait_ge(z_ready, 1)
            nc.vector.scalar_tensor_tensor(out=gamma[:, 0:SEQS], in0=zpot[:, 1, :], scalar=0.0,
                                           in1=zabs[:, :], op0=ALU.max, op1=ALU.add).then_inc(zlink, 1)
            dve.wait_ge(zlink, 3)
            nc.vector.tensor_scalar(diag[:, 1, :], gamma[:, 0:SEQS], GAMMA_FLOOR, -1.0, ALU.add, ALU.mult
                                    ).then_inc(zlink, 1)
            dve.wait_ge(zlink, 4)
            nc.vector.tensor_scalar(gamma[:, 0:SEQS], gamma[:, 0:SEQS], GAMMA_FLOOR, None, ALU.add
                                    ).then_inc(gamma_ready, 1)

            links = [2]

            def link(ins):
                links[0] += 1
                ins.then_inc(scan_link, 1)
                dve.wait_ge(scan_link, links[0])

            def side(ins):
                links[0] += 1
                ins.then_inc(scan_link, 1)

            dve.wait_ge(drow_mm, 1)
            rows = 2 * SEQS
            link(nc.vector.tensor_copy(d_row[:, :, :].rearrange("p a n -> p (a n)"), bank[5][0:rows, 0:2 * P]))
            side(nc.vector.tensor_scalar(di_sign[:, 0, :], d_row[:, 1, :], -1.0, None, ALU.mult))
            link(nc.vector.tensor_copy(di_sign[:, 1, :], d_row[:, 1, :]))
            dre = d_row[:, 0, :].rearrange("p (c j) -> p c j", j=CL)
            dim = di_sign[:, :, :].rearrange("p a (c j) -> p a c j", j=CL)
            for j in range(CL):
                y1 = Y[:, j + 1, :, :, :]
                side(nc.vector.tensor_tensor(
                    Ya[:, :, :, :].rearrange("p a b c -> p (a b) c"), y1.rearrange("p a b c -> p (a b) c"),
                    dre[:, :, j].unsqueeze(1).broadcast_to([rows, 4, CN]), ALU.mult))
                link(nc.vector.tensor_tensor(
                    Yb[:, :, :, :], y1[:, :, ::-1, :],
                    dim[:, :, :, j].unsqueeze(1).broadcast_to([rows, 2, 2, CN]), ALU.mult))
                link(nc.vector.tensor_tensor(Yc[:, :, :, :], Ya[:, :, :, :], Y[:, j, :, :, :], ALU.subtract))
                link(nc.vector.tensor_tensor(Y[:, j + 2, :, :, :], Yc[:, :, :, :], Yb[:, :, :, :], ALU.add))
            for out_j in range(2):
                yj = Y[:, CL + out_j, :, :, :]
                for out_r, in_r, part, sign in ((0, 0, 0, 1.0), (0, 1, 1, -1.0), (1, 0, 1, 1.0), (1, 1, 0, 1.0)):
                    side(nc.vector.tensor_scalar(
                        C[:, :, out_j, out_r, in_r:in_r + 3:2].rearrange("p c a -> p a c"),
                        yj[:, :, part, :], sign, None, ALU.mult))
            dve.wait_ge(scan_link, links[0])
            Cf = C[:, :, :, :, :].rearrange("p c a b n -> p c (a b n)")
            link(nc.vector.tensor_reduce(cmax[:, :], Cf, AX.X, ALU.max, apply_absolute_value=True))
            link(nc.vector.reciprocal(crec[:, :], cmax[:, :]))
            link(nc.vector.tensor_tensor(Cs[:, :, :], Cf, crec[:, :].unsqueeze(2).broadcast_to([rows, CN, 16]),
                                         ALU.mult))
            for c in range(CN - 1):
                link(nc.vector.tensor_tensor(
                    Sp[:, :, :], Cs[:, c, :].rearrange("p (o n) -> p o n", o=4),
                    S[:, c, :].unsqueeze(1).broadcast_to([rows, 4, 4]), ALU.mult))
                link(nc.vector.tensor_reduce(S[:, c + 1, :], Sp[:, :, :], AX.X, ALU.add))
            Sc = S[:, 0:CN, :].rearrange("p c (a b) -> p a b c", a=2)
            side(nc.vector.tensor_copy(Sa[:, :, 0, :], Sc[:, :, 0, :]))
            side(nc.vector.tensor_scalar(Sa[:, :, 1, :], Sc[:, :, 1, :], -1.0, None, ALU.mult))
            side(nc.vector.tensor_copy(Sb[:, :, 0, :], Sc[:, :, 1, :]))
            link(nc.vector.tensor_copy(Sb[:, :, 1, :], Sc[:, :, 0, :]))
            Yf = Y[:, 1:CL + 2, :, :, :].rearrange("p j a b c -> p j (a b c)")
            for Sx, Zx, Px in ((Sa, Z, Pr), (Sb, Zb, Pi)):
                link(nc.vector.tensor_tensor(
                    Zx[:, :, :, :].rearrange("p j n c -> p j (n c)"), Yf,
                    Sx[:, :, :, :].rearrange("p a b c -> p (a b c)").unsqueeze(1).broadcast_to(
                        [rows, CL + 1, 4 * CN]), ALU.mult))
                link(nc.vector.tensor_reduce(Px[:, :, :].rearrange("p c j -> p j c"),
                                             Zx[:, :, :, :].rearrange("p j n c -> p j c n"), AX.X, ALU.add))
            pr1, pi1 = Pr[:, :, 1:CL + 1], Pi[:, :, 1:CL + 1]
            pr0, pi0 = Pr[:, :, 0:CL], Pi[:, :, 0:CL]

            def v3(buf):
                return buf[:, :].rearrange("p (c j) -> p c j", j=CL)

            side(nc.vector.tensor_tensor(v3(ra), pr0, pr0, ALU.mult))
            link(nc.vector.tensor_tensor(v3(rb), pi0, pi0, ALU.mult))
            link(nc.vector.tensor_tensor(rc[:, :], ra[:, :], rb[:, :], ALU.add))
            link(nc.vector.reciprocal(rd[:, :], rc[:, :]))
            for part, (p0, q0, p1, q1, op) in enumerate(((pr1, pr0, pi1, pi0, ALU.add),
                                                         (pi1, pr0, pr1, pi0, ALU.subtract))):
                side(nc.vector.tensor_tensor(v3(ra), p0, q0, ALU.mult))
                link(nc.vector.tensor_tensor(v3(rb), p1, q1, ALU.mult))
                link(nc.vector.tensor_tensor(rc[:, :], ra[:, :], rb[:, :], op))
                side(nc.vector.tensor_tensor(frac[0:SEQS, part, :], rc[0:SEQS, :], rd[0:SEQS, :], ALU.mult))
                link(nc.vector.tensor_tensor(frac[SEQS:rows, part, ::-1], rc[SEQS:rows, :], rd[SEQS:rows, :],
                                             ALU.mult))
            nc.vector.tensor_scalar(neg_id[:, :], ident[0:SEQS, 0:SEQS], -1.0, None, ALU.mult
                                    ).then_inc(frac_ready, 1)
            dve.wait_ge(den_mm, 1)
            link(nc.vector.tensor_copy(den[:, :, :].rearrange("p a s -> p (a s)"), bank[6][:, 0:2 * SEQS]))
            side(nc.vector.tensor_tensor(ga[:, :], den[:, 0, :], den[:, 0, :], ALU.mult))
            link(nc.vector.tensor_tensor(gb[:, :], den[:, 1, :], den[:, 1, :], ALU.mult))
            link(nc.vector.tensor_tensor(ga[:, :], ga[:, :], gb[:, :], ALU.add))
            link(nc.vector.reciprocal(gb[:, :], ga[:, :]))
            link(nc.vector.tensor_tensor(green[:, 0, 0:SEQS], den[:, 0, :], gb[:, :], ALU.mult))
            nc.vector.scalar_tensor_tensor(out=green[:, 1, 0:SEQS], in0=den[:, 1, :], scalar=-1.0,
                                           in1=gb[:, :], op0=ALU.mult, op1=ALU.mult).then_inc(green_ready, 1)

            dve.wait_ge(weights_loaded, 16 * len(LOADS))
            nc.vector.scalar_tensor_tensor(out=bq_pad[:, :], in0=bq_pad[:, :], scalar=XSCALE, in1=q_ones[:, :],
                                           op0=ALU.mult, op1=ALU.add).then_inc(folded, 1)
            nc.vector.tensor_tensor(bk_pad[:, :], bk_pad[:, :], k_ones[:, :], ALU.add).then_inc(folded, 1)
            dve.wait_ge(bias_mm, 1)
            nc.vector.tensor_tensor(bg_qk[:, :], bank[7][:, 0:2 * PAIRS], b_qk[:, :], ALU.add
                                    ).then_inc(bias_ready, 1)
            dve.wait_ge(bias_mm, 2)
            nc.vector.tensor_copy(bg_v[:, :], bank[2][:, :]).then_inc(bias_ready, 1)
            dve.wait_ge(bias_mm, 3)
            nc.vector.tensor_tensor(bg_ff1[:, :], bank[3][:, 0:FC], b_ff1[:, :], ALU.add).then_inc(bias_ready, 1)
            dve.wait_ge(bias_mm, 4)
            nc.vector.tensor_copy(bo_bc[:, :], bank[4][:, 0:P]).then_inc(bias_ready, 1)

            def ln_stats(g, stage, t, src):
                dve.wait_ge(sum_ready, ln_nth(g, stage, t) + 1)
                nc.vector.bn_stats(stats[:, t, :], src).then_inc(bn_ready, 1)

            def ln_moments(g, stage, t):
                dve.wait_ge(bn_ready, ln_nth(g, stage, t) + 1)
                dve.sem_inc(dve_held, 1)
                nc.vector.bn_aggr(mv[:, t, :], stats[:, t, :]).then_inc(mv_ready, 1)

            def ln_apply(g, stage, t, src, dst):
                dve.wait_ge(rstd_ready, ln_nth(g, stage, t) + 1)
                nc.vector.tensor_scalar(dst, src, mv[:, t, 0:1], rstd[:, t:t + 1], ALU.subtract,
                                        ALU.mult).then_inc(xn_ready, 1)

            def first_sums(g, k):
                dve.wait_ge(xbk_ready, k + 1)
                for t in range(T):
                    nc.vector.scalar_tensor_tensor(
                        out=x1[:, t, :], in0=w_bk_bc[:, 0, :], scalar=green[:, 0, bass.ds(k * T + t, 1)],
                        in1=xbk[:, t, :], op0=ALU.mult, op1=ALU.add).then_inc(x1_part, 1)
                for t in range(T + 2):
                    if t < T:
                        dve.wait_ge(x1_part, k * T + t + 1)
                        nc.vector.scalar_tensor_tensor(
                            out=x1[:, t, :], in0=w_bk_bc[:, 1, :], scalar=green[:, 1, bass.ds(k * T + t, 1)],
                            in1=x1[:, t, :], op0=ALU.mult, op1=ALU.add).then_inc(sum_ready, 1)
                    if 0 <= t - 1 < T:
                        ln_stats(g, LN2, t - 1, x1[:, t - 1, :])
                    if 0 <= t - 2 < T:
                        ln_moments(g, LN2, t - 2)
                if g is not None:
                    filled(dve, g, "xh3T")
                for t in range(T):
                    ln_apply(g, LN2, t, x1[:, t, :], xn[:, t, :])

            def keys(g, p):
                b = filled(dve, g, f"k{p}")
                nc.vector.tensor_scalar(kT[:, p, :], b[:, :], bg_qk[:, PAIRS + p:PAIRS + p + 1], None,
                                        ALU.add).then_inc(free[BANK[f"k{p}"]], 1)

            def values(g, t):
                b = filled(dve, g, f"v{t}")
                nc.vector.tensor_tensor(v_sb[:, t, :], b[:, :], bg_v[:, :], ALU.add
                                        ).then_inc(free[BANK[f"v{t}"]], 1)

            def decayed(g, t):
                if t == 0:
                    drained(dve, g, "decay")
                for r in range(2):
                    b = filled(dve, g, f"at{t}r{r}")
                    nc.vector.tensor_tensor(
                        at[t % 2][:, r, :, :], b[:, :].rearrange("p (a n) -> p a n", a=PAIRS),
                        decay[:, t, :].unsqueeze(1).broadcast_to([P, PAIRS, P]), ALU.mult
                    ).then_inc(free[BANK[f"at{t}r{r}"]], 1)

            def split(g, k, name, which, c, full, out, high_ready, split_ready):
                dve.wait_ge(high_ready, k * XC + c + 1)
                drained(dve, g, name)
                nc.vector.scalar_tensor_tensor(
                    out=out, in0=high[c % 2][:, :].bitcast(F32),
                    scalar=low_rows[:, which:which + 1], in1=full, op0=ALU.mult, op1=ALU.add
                ).then_inc(split_ready, 1)

            def split_keys(g, k, c):
                split(g, k, f"kp{c}", 1, c, kp[:, c, :], kr[:, c, :], khigh_ready, kr_ready)

            dve.sem_inc(xb_free, 1)
            first_sums(None, 0)
            for p in range(PAIRS):
                keys(None, p)
            for t in range(T):
                values(None, t)
            decayed(None, 0)
            decayed(None, 1)
            split_keys(None, 0, 0)
            split_keys(None, 0, 1)

            with dve.Fori(0, G) as g:
                def heb_sum(t):
                    if t == 0:
                        dve.wait_ge(x1b_ready, g + 1)
                    b = filled(dve, g, f"wo{t}")
                    nc.vector.tensor_tensor(x2[:, t, :], b[:, 0:P], x1b[:, t, :], ALU.add
                                            ).then_inc(free[BANK[f"wo{t}"]], 1)
                    drained(dve, g, f"wo{t}")
                    dve.sem_inc(sum_ready, 1)
                    ln_stats(g, LN3, t, x2[:, t, :])
                    ln_moments(g, LN3, t)

                decayed(g, 2)
                split_keys(g, g, 2)
                heb_sum(0)
                decayed(g, 3)
                heb_sum(1)
                ln_apply(g, LN3, 0, x2[:, 0, :], xn[:, 0, :])
                split_keys(g, g, 3)
                heb_sum(2)
                ln_apply(g, LN3, 1, x2[:, 1, :], xn[:, 1, :])
                heb_sum(3)
                ln_apply(g, LN3, 2, x2[:, 2, :], xn[:, 2, :])
                ln_apply(g, LN3, 3, x2[:, 3, :], xn[:, 3, :])

                first_sums(g, g + 1)

                def residual(name, dst, other):
                    b = filled(dve, g, name)
                    nc.vector.tensor_tensor(dst, b[:, 0:P], other, ALU.add).then_inc(free[BANK[name]], 1)

                def residual_stats(stage, name, t, src):
                    drained(dve, g, name)
                    dve.sem_inc(sum_ready, 1)
                    ln_stats(g, stage, t, src)

                dve.wait_ge(xsum_ready, g + 1)
                for t in range(T):
                    residual(f"ff2t{t}", x2[:, t, :], xsum[:, t, :])
                    residual_stats(LNA, f"ff2t{t}", t, x2[:, t, :])
                    ln_moments(g, LNA, t)
                for t in range(T):
                    ln_apply(g, LNA, t, x2[:, t, :], xa[:, t, :])

                def maxima(t):
                    for i in range(4):
                        b = filled(dve, g, f"mx{t}i{i}")
                        nc.vector.tensor_reduce(
                            negmax[t % 2][:, i, 28:28 + XC], b[:, :].rearrange("p (c n) -> p c n", c=XC),
                            AX.X, ALU.max, negate=True).then_inc(free[BANK[f"mx{t}i{i}"]], 1)
                    if t > 0:
                        keys(g, t)
                    b = filled(dve, g, f"mT{t}")
                    nc.vector.tensor_tensor(
                        qm[t % 2][:, :, :], b[:, 0:P].unsqueeze(1).broadcast_to([P, XC, P]),
                        qr[:, :, t * P:(t + 1) * P].bitcast(F32), ALU.add).then_inc(free[BANK[f"mT{t}"]], 1)

                def normalise(t):
                    b = filled(dve, g, f"ctT{t}")
                    heads = b[:, :].rearrange("p (h n) -> p h n", n=32)
                    nc.vector.reciprocal(rsum[:, t, :], heads[:, :, XD]).then_inc(rsum_ready, 1)
                    dve.wait_ge(rsum_ready, g * T + t + 1)
                    nc.vector.tensor_tensor(
                        cx[:, t, :, :], heads[:, :, 0:XD],
                        rsum[:, t, :].unsqueeze(2).broadcast_to([P, XH, XD]), ALU.mult
                    ).then_inc(free[BANK[f"ctT{t}"]], 1)

                for c in range(XC):
                    split(g, g, f"qp{c}", 0, c, qp[:, c, :], qr[:, c, :], qhigh_ready, qr_ready)
                keys(g, 0)
                maxima(0)
                for t in range(T):
                    if t + 1 < T:
                        maxima(t + 1)
                    if t >= 2:
                        values(g, t - 2)
                    normalise(t)
                dve.wait_ge(xab_ready, g + 1)
                values(g, 2)
                for t in range(T + 2):
                    if t < T:
                        residual(f"xo{t}", x2[:, t, :], xab[:, t, :])
                    if 0 <= t - 1 < T:
                        residual_stats(LNB, f"xo{t - 1}", t - 1, x2[:, t - 1, :])
                    if 0 <= t - 2 < T:
                        ln_moments(g, LNB, t - 2)
                dve.wait_ge(xb_free, g + 1)
                for t in range(T):
                    ln_apply(g, LNB, t, x2[:, t, :], xb[:, t, :])
                values(g, 3)
                decayed(g, 0)

                b = filled(dve, g, "rl")
                nc.vector.tensor_copy(lg[:, :, :].rearrange("p t e -> p (t e)"), b[:, 0:T * EXP]
                                      ).then_inc(free[BANK["rl"]], 1)
                drained(dve, g, "rl")
                dve.sem_inc(dve_held, 1)
                for t in range(T):
                    ins = nc.vector.max(top8[:, t, :], lg[:, t, :])
                ins.then_inc(route_link, 1)
                dve.wait_ge(route_link, g * 6 + 1)
                dve.sem_inc(dve_held, 1)
                nc.vector.tensor_tensor(below[:, :], top8[:, :, 1], top8[:, :, 0], ALU.subtract
                                        ).then_inc(below_ready, 1)
                for t in range(T):
                    ins = nc.vector.max_index(top_i[:, t, :], top8[:, t, :], lg[:, t, :])
                ins.then_inc(route_link, 1)
                dve.wait_ge(route_link, g * 6 + 2)
                nc.vector.tensor_copy(top_f[:, :, :], top_i[:, :, 0:TOPK]).then_inc(route_link, 1)
                dve.wait_ge(route_link, g * 6 + 3)
                nc.vector.tensor_tensor(
                    onehot[:, :, :, :].rearrange("p t k e -> p (t k) e"),
                    iota_e[:, :].unsqueeze(1).broadcast_to([P, T * TOPK, EXP]),
                    top_f[:, :, :].rearrange("p t k -> p (t k)").unsqueeze(2).broadcast_to(
                        [P, T * TOPK, EXP]), ALU.is_equal).then_inc(route_link, 1)
                dve.wait_ge(route_link, g * 6 + 4)
                nc.vector.tensor_tensor(chosen[:, :, :], onehot[:, :, 0, :], onehot[:, :, 1, :], ALU.add
                                        ).then_inc(chosen_ready, 1)
                decayed(g, 1)
                dve.wait_ge(ratio_ready, g + 1)
                nc.vector.tensor_scalar(wsum[:, :], ratio[:, :], 1.0, None, ALU.add).then_inc(route_link, 1)
                dve.wait_ge(route_link, g * 6 + 5)
                nc.vector.reciprocal(gate_all[:, bass.ds(g * T, T), 0], wsum[:, :])
                nc.vector.reciprocal(wrec[:, :], wsum[:, :]).then_inc(route_link, 1)
                dve.wait_ge(route_link, g * 6 + 6)
                nc.vector.tensor_tensor(gate_all[:, bass.ds(g * T, T), 1], ratio[:, :], wrec[:, :], ALU.mult)
                split_keys(g, g + 1, 0)
                b = filled(dve, g, "rank")
                nc.vector.tensor_tensor(
                    places[:, :, :], b[:, 0:T * EXP].rearrange("p (t e) -> p t e", t=T),
                    counts[:, :].unsqueeze(1).broadcast_to([P, T, EXP]), ALU.add).then_inc(places_ready, 1)
                dve.wait_ge(places_ready, g * 3 + 1)
                nc.vector.tensor_tensor(counts[:, :], counts[:, :], b[:, T * EXP:T * EXP + EXP], ALU.add
                                        ).then_inc(free[BANK["rank"]], 1)
                for k in range(TOPK):
                    ins = nc.vector.tensor_tensor(picked[:, :, k, :], onehot[:, :, k, :], places[:, :, :],
                                                  ALU.mult)
                ins.then_inc(places_ready, 1)
                dve.wait_ge(places_ready, g * 3 + 2)
                nc.vector.tensor_reduce(slot_f[:, :, :], picked[:, :, :, :], AX.X, ALU.add
                                        ).then_inc(places_ready, 1)
                dve.wait_ge(places_ready, g * 3 + 3)
                dve.wait_ge(home_free, g + 1)
                nc.vector.tensor_copy(slot_u[:, :, :], slot_f[:, :, :]).then_inc(slot_ready, 1)
                split_keys(g, g + 1, 1)

            tl = [0]

            def tlink(ins):
                tl[0] += 1
                ins.then_inc(table_link, 1)
                dve.wait_ge(table_link, tl[0])

            drained(dve, G - 1, "rank")
            nc.vector.tensor_scalar(ends_i[:, :], counts[0:1, :], 1.0, None, ALU.add).then_inc(ends_ready, 1)
            tlink(nc.vector.tensor_tensor(n_rows[:, :], counts[:, :], slot_base[:, :], ALU.subtract))
            tlink(nc.vector.tensor_scalar(n_rows[:, :], n_rows[:, :], float(P - 1), None, ALU.add))
            tlink(nc.vector.tensor_copy(n_rows_i[:, :], n_rows[:, :]))
            tlink(nc.vector.tensor_scalar(n_tiles_i[:, :], n_rows_i[:, :], 7, None, ALU.arith_shift_right))
            tlink(nc.vector.tensor_copy(n_tiles[:, :], n_tiles_i[:, :]))
            tlink(nc.vector.tensor_scalar(step_rows[:, :], n_tiles[:, :], -float(P), float(REGION), ALU.mult,
                                          ALU.add))
            tlink(nc.vector.tensor_copy(starts[:, 1:2], n_tiles[0:1, 0:1]))
            for e in range(2, EXP):
                tlink(nc.vector.tensor_tensor(starts[:, e:e + 1], starts[:, e - 1:e], n_tiles[0:1, e - 1:e],
                                              ALU.add))
            tlink(nc.vector.tensor_tensor(
                begun, iota_t[:, :].unsqueeze(1).broadcast_to([1, EXP - 1, TILES]),
                starts[:, 1:EXP].unsqueeze(2).broadcast_to([1, EXP - 1, TILES]), ALU.is_ge))
            tlink(nc.vector.tensor_tensor(
                begun_w, begun,
                step_rows[0:1, 0:EXP - 1].unsqueeze(2).broadcast_to([1, EXP - 1, TILES]), ALU.mult))
            tlink(nc.vector.tensor_reduce(tab_f[:, 0, :], begun.rearrange("p e j -> p j e"),
                                          AX.X, ALU.add))
            tlink(nc.vector.tensor_reduce(tab_f[:, 1, :], begun_w.rearrange("p e j -> p j e"),
                                          AX.X, ALU.add))
            tlink(nc.vector.scalar_tensor_tensor(out=tab_f[:, 1, :], in0=iota_t[:, :], scalar=float(P),
                                                 in1=tab_f[:, 1, :], op0=ALU.mult, op1=ALU.add))
            nc.vector.tensor_copy(tab[:, :, :], tab_f[:, :, :]).then_inc(table_ready, 1)
            dve.sem_inc(turned_copied, 2)
            dve.sem_inc(y_added, 2)
            dve.sem_inc(combined, 4 * T)
            for n in range(2):
                dve.sem_inc(stored[n], 1)

            def turned_rows(j, n):
                dve.wait_ge(turned, j + 1 + UNROLL)
                dve.wait_ge(h_mm, j + 1)
                nc.vector.tensor_copy(xtT[n], bank[n][:, 0:P]).then_inc(turned_copied, 1)

            def weights(j, n):
                e = dve.value_load(tab[0:1, 0, bass.ds(j, 1)], min_val=0, max_val=EXP - 1)
                dve.wait_ge(gelu_done, j + 1)
                nc.vector.tensor_copy(w1c[n], w1_t[:, bass.ds(e, 1), :].rearrange("p a n -> p (a n)")
                                      ).then_inc(w1_in, 1)

            def results(j, i, n):
                e = dve.value_load(tab[0:1, 0, bass.ds(j, 1)], min_val=0, max_val=EXP - 1)
                dve.wait_ge(y_mm, j + 1 + 2)
                if i is not None:
                    dve.wait_ge(y_out[n], i * 16 + 16)
                nc.vector.tensor_tensor(ysb[n], bank[4 + n % 2][:, 0:P],
                                        b2_bc[:, bass.ds(e, 1), :].rearrange("p a n -> p (a n)"), ALU.add
                                        ).then_inc(y_added, 1)

            dve.wait_ge(table_ready, 1)
            dve.wait_ge(experts_loaded, 16 * len(EXPERT_LOADS))
            weights(0, 0)
            weights(1, 1)
            turned_rows(0, 0)
            turned_rows(1, 1)
            for n in range(UNROLL):
                turned_rows(n + 2, n % 2)
                weights(n + 2, n % 2)
                results(n, None, n)
            with dve.Fori(0, TILES // UNROLL - 2) as i:
                for n in range(UNROLL):
                    turned_rows(i * UNROLL + (UNROLL + n + 2), n % 2)
                    weights(i * UNROLL + (UNROLL + n + 2), n % 2)
                    results(i * UNROLL + (UNROLL + n), i, n)
            for n in range(UNROLL):
                j = TILES - UNROLL + n
                if j + 2 < TILES:
                    turned_rows(j + 2, n % 2)
                    weights(j + 2, n % 2)
                results(j, TILES // UNROLL - 2, n)

            def combine(g, m):
                n = m % 2
                dve.wait_ge(sum0_ready, g + 1 + 2)
                for t in range(T):
                    nc.vector.scalar_tensor_tensor(
                        out=acc[m][:, t, :], in0=two_rows[m][:, t, 1, :],
                        scalar=gate_all[:, bass.ds(g * T + t, 1), 1],
                        in1=acc[m][:, t, :], op0=ALU.mult, op1=ALU.add).then_inc(combined, 1)
                for t in range(T):
                    dve.wait_ge(combined, g * T + (t + 1 + 4 * T))
                    nc.vector.bn_stats(stats[:, t, :], acc[m][:, t, :]).then_inc(bnc_ready, 1)
                for t in range(T):
                    dve.wait_ge(bnc_ready, g * T + t + 1)
                    dve.sem_inc(dve_held, 1)
                    nc.vector.bn_aggr(mvc[m][:, t, :], stats[:, t, :]).then_inc(mvc_ready, 1)

            with dve.Fori(0, G // 4) as i:
                for m in range(4):
                    combine(i * 4 + m, m)

        @block.tensor
        def _(pe):
            mm = nc.tensor.matmul
            pe.wait_ge(pre_loaded, 16 * len(PRE_LOADS))
            pe.wait_ge(pool_const, 14)
            pe.wait_ge(wpotg_ready, 1)
            mm(bank[2][:, 0:2], mean_w[:, :], w_potg[:, :], start=True, stop=True).then_inc(wmean_mm, 1)
            pe.wait_ge(lnb_ready, 1)
            mm(bank[3][:, 0:2], lnb_cols[:, 0, :], w_pot[:, :], start=True, stop=False)
            mm(bank[3][:, 0:2], ones[0:1, :], b_pot[:, :], start=False, stop=True).then_inc(potbias_mm, 1)
            pe.wait_ge(wpotc_ready, 1)
            for n in range(G):
                if n % 2 == 0:
                    pe.wait_ge(xT_loaded[n // 2], 16)
                if n >= 2:
                    pe.wait_ge(zrow_copied, n - 1)
                mm(bank[n % 2][0:2, :], w_potc[:, :], xT_all[:, n * GT:(n + 1) * GT], start=True,
                   stop=True).then_inc(zrow_mm, 1)
            pe.wait_ge(zseq_loaded, 32)
            nc.tensor.transpose(bank[4][:, 0:2 * SEQS], zpot_seq[:, :], ident[0:2 * SEQS, 0:2 * SEQS]
                                ).then_inc(zpos_mm, 1)
            pe.wait_ge(zlink, 4)
            for part in range(2):
                for way, perm in enumerate((ident, antid)):
                    last = mm(bank[5][SEQS * way:SEQS * way + SEQS, P * part:P * part + P],
                              diag[:, part, :], perm[:, :], start=True, stop=True)
            last.then_inc(drow_mm, 1)
            pe.wait_ge(weights_loaded, 16 * len(LOADS))
            for j in range(2 * PAIRS):
                last = mm(bank[7][:, j:j + 1], w_qkv[:, j * P:(j + 1) * P], ln2_b[:, :], start=True, stop=True)
            last.then_inc(bias_mm, 1)
            pe.wait_ge(cols_ready, 2)
            mm(bank[2][:, :], lnb_cols[:, 1, :], w_qkv[:, 2 * FF:3 * FF], start=True, stop=False)
            mm(bank[2][:, :], ones[0:1, :], b_v_row[:, :], start=False, stop=True).then_inc(bias_mm, 1)
            for j in range(FC):
                last = mm(bank[3][:, j:j + 1], w_ff1[:, j * P:(j + 1) * P], ln3_b[:, :], start=True, stop=True)
            last.then_inc(bias_mm, 1)
            mm(bank[4][:, 0:P], lnb_cols[:, 2, :], wo_t[:, :], start=True, stop=False)
            mm(bank[4][:, 0:P], ones[0:1, :], bo_row[:, :], start=False, stop=True).then_inc(bias_mm, 1)
            pe.wait_ge(frac_ready, 1)
            for part in range(2):
                o = bank[6][:, SEQS * part:SEQS * part + SEQS]
                mm(o, frac[0:2 * SEQS, part, :], fold_id[:, :], start=True, stop=False)
                last = mm(o, d_row[0:SEQS, part, :], neg_id[:, :], start=False, stop=True)
            last.then_inc(den_mm, 1)
            pe.wait_ge(bias_ready, 4)
            pe.wait_ge(folded, 12)
            for b in range(NB):
                pe.sem_inc(free[b], 1)

            def done(ins, name):
                ins.then_inc(full[BANK[name]], 1)

            def tile(t):
                return slice(t * P, (t + 1) * P)

            def turn(g, name, stage, src):
                for t in range(T):
                    pe.wait_ge(xn_ready, ln_nth(g, stage, t) + 1)
                    if t == 0:
                        b = take(pe, g, name)
                    ins = nc.tensor.transpose(b[:, tile(t)], src[:, t, :], ident[:, :])
                done(ins, name)

            def wide(g, name, lhsT, rhs):
                b = take(pe, g, name)
                done(mm(b[:, :], lhsT, rhs, start=True, stop=True), name)

            def turn_and_decay(g, k):
                turn(g, "xh2T", LN2, xn)
                pe.wait_ge(cumg_ready, k + 1)
                b = take(pe, g, "decay")
                mm(b[:, :], after[:, :], cumg[:, :, :].rearrange("p t n -> p (t n)"), start=True, stop=True)
                for t in range(T):
                    ins = mm(b[:, tile(t)], ident_b[:, :], future_b[:, :], start=False,
                             stop=True, skip_group_check=True)
                done(ins, "decay")

            def queries(g, p):
                if p == 0:
                    drained(pe, g, "xh2T")
                wide(g, f"q{p}", w_qkv[:, tile(p)], xqT[:, :])

            def keys(g, p):
                wide(g, f"k{p}", w_qkv[:, FF + p * P:FF + (p + 1) * P], xqT[:, :])

            def values(g, t):
                wide(g, f"v{t}", xqT[:, tile(t)], w_qkv[:, 2 * FF:3 * FF])

            def all_drained(g, names):
                order = NTH_FIRST if g is None else NTH
                for name in names:
                    if not any(BANK[m] == BANK[name] and order[m] > order[name] for m in names):
                        drained(pe, g, name)

            def scores(g, t, r):
                if t == 0 and r == 0:
                    all_drained(g, [f"{n}{p}" for p in range(PAIRS) for n in ("q", "k")])
                b = take(pe, g, f"at{t}r{r}")
                rows = slice(HD * r, HD * r + HD)
                for p in range(PAIRS):
                    ins = mm(b[:, tile(p)], kT[rows, p, tile(t)], qT[rows, p, tile(t)],
                             start=True, stop=True)
                done(ins, f"at{t}r{r}")

            def context_keys(g, k, c):
                if c == 0:
                    pe.wait_ge(ctx_loaded, k * 16 + 16)
                    pe.wait_ge(maskb_ready, k + 1)
                b = take(pe, g, f"kp{c}")
                mm(b[:, :], wk_pad[:, c, :], ctxT[:, :], start=True, stop=False)
                done(mm(b[:, :], pos_only_b[:, :], mask_b[:, :], start=False, stop=True), f"kp{c}")

            def ahead_drained(g):
                all_drained(g, [f"v{t}" for t in range(T)] + [f"at{t}r{r}" for t in range(2) for r in range(2)])

            turn_and_decay(None, 0)
            for p in range(PAIRS):
                queries(None, p)
                keys(None, p)
            for t in range(T):
                values(None, t)
            for t in range(2):
                for r in range(2):
                    scores(None, t, r)
            context_keys(None, 0, 0)
            context_keys(None, 0, 1)
            ahead_drained(None)

            with pe.Fori(0, G) as g:
                def weigh(t):
                    b = take(pe, g, f"hpv{t}")
                    for r in range(2):
                        if t >= 2:
                            drained(pe, g, f"at{t}r{r}")
                        for p in range(PAIRS):
                            h = 2 * p + r
                            ins = mm(b[HD * r:HD * r + HD, tile(p)], v_sb[:, t, h * HD:(h + 1) * HD],
                                     at[t % 2][:, r, p, :], start=True, stop=True)
                    done(ins, f"hpv{t}")

                def heb_out(t):
                    drained(pe, g, f"hpv{t}")
                    b = take(pe, g, f"wo{t}")
                    for p in range(PAIRS):
                        ins = mm(b[:, 0:P], hebT[t % 2][:, p, :], w_out[:, p, :], start=(p == 0),
                                 stop=(p == PAIRS - 1))
                    done(ins, f"wo{t}")

                weigh(0)
                scores(g, 2, 0)
                scores(g, 2, 1)
                context_keys(g, g, 2)
                weigh(1)
                heb_out(0)
                scores(g, 3, 0)
                scores(g, 3, 1)
                weigh(2)
                heb_out(1)
                context_keys(g, g, 3)
                weigh(3)
                heb_out(2)
                heb_out(3)

                b = take(pe, g, "cv")
                for t in range(T):
                    ins = mm(b[:, tile(t)], ctxT[:, tile(t)], wv_t[:, :], start=True, stop=True)
                done(ins, "cv")

                turn(g, "xh3T", LN3, xn)
                drained(pe, g, "xh3T")
                for c in range(FC):
                    wide(g, f"ff1c{c}", w_ff1[:, tile(c)], xnT[:, :])
                for t in range(T):
                    b = take(pe, g, f"ff2t{t}")
                    for c in range(FC):
                        if t == 0:
                            drained(pe, g, f"ff1c{c}")
                        ins = mm(b[:, 0:P], hT[:, c, tile(t)], w_ff2[:, c, :], start=(c == 0),
                                 stop=(c == FC - 1))
                    done(ins, f"ff2t{t}")

                turn_and_decay(g, g + 1)

                turn(g, "xaT", LNA, xa)
                drained(pe, g, "xaT")
                for c in range(XC):
                    wide(g, f"qp{c}", wq_pad[:, c, :], xnT[:, :])

                queries(g, 0)
                keys(g, 0)

                def max_scores(t):
                    if t == 0:
                        pe.wait_ge(qr_ready, g * XC + XC)
                        pe.wait_ge(kr_ready, g * XC + XC)
                    for i in range(4):
                        b = take(pe, g, f"mx{t}i{i}")
                        rows = slice(32 * i, 32 * i + 32)
                        for c in range(XC):
                            ins = mm(b[:, tile(c)], qr[rows, c, tile(t)], kr[rows, c, tile(t)],
                                     start=True, stop=True)
                        done(ins, f"mx{t}i{i}")

                def turn_max(t):
                    for i in range(4):
                        drained(pe, g, f"mx{t}i{i}")
                    b = take(pe, g, f"mT{t}")
                    done(nc.tensor.transpose(b[:, 0:P], negmax[t % 2][:, :, :].rearrange("p i n -> p (i n)"),
                                             ident[:, :]), f"mT{t}")

                def key_scores(t):
                    drained(pe, g, f"mT{t}")
                    for i in range(4):
                        b = take(pe, g, f"st{t}i{i}")
                        rows = slice(32 * i, 32 * i + 32)
                        for c in range(XC):
                            ins = mm(b[:, tile(c)], kr[rows, c, tile(t)], qm[t % 2][rows, c, :],
                                     start=True, stop=True)
                        done(ins, f"st{t}i{i}")

                def attend(t):
                    b = take(pe, g, f"xpv{t}")
                    for i in range(4):
                        drained(pe, g, f"st{t}i{i}")
                        for c in range(XC):
                            ins = mm(b[32 * i:32 * i + 32, tile(c)], vpad[:, t, 4 * c + i, :],
                                     pT[t % 2][:, i, c, :], start=True, stop=True)
                    done(ins, f"xpv{t}")
                    if t < 2:
                        queries(g, 2 + t)
                    else:
                        values(g, t - 2)
                    drained(pe, g, f"xpv{t}")
                    b = take(pe, g, f"ctT{t}")
                    for c in range(XC):
                        ins = nc.tensor.transpose(b[:, tile(c)], cT[t % 2][:, c, :], ident[:, :])
                    done(ins, f"ctT{t}")

                max_scores(0)
                queries(g, 1)
                turn_max(0)
                for t in range(T):
                    if t + 1 < T:
                        max_scores(t + 1)
                        keys(g, t + 1)
                    key_scores(t)
                    if t + 1 < T:
                        turn_max(t + 1)
                    attend(t)
                b = take(pe, g, "cxT")
                for t in range(T):
                    drained(pe, g, f"ctT{t}")
                    ins = nc.tensor.transpose(b[:, tile(t)], cx[:, t, :, :].rearrange("p h d -> p (h d)"),
                                              ident[:, :])
                done(ins, "cxT")
                values(g, 2)
                drained(pe, g, "cxT")
                for t in range(T):
                    b = take(pe, g, f"xo{t}")
                    done(mm(b[:, 0:P], cxT[:, tile(t)], wo_t[:, :], start=True, stop=True), f"xo{t}")

                values(g, 3)
                scores(g, 0, 0)
                scores(g, 0, 1)
                context_keys(g, g + 1, 0)
                turn(g, "xbT", LNB, xb)
                scores(g, 1, 0)
                drained(pe, g, "xbT")
                b = take(pe, g, "rl")
                for t in range(T):
                    ins = mm(b[:, t * EXP:(t + 1) * EXP], xnT[:, tile(t)], wr_t[:, :], start=True, stop=True)
                done(ins, "rl")
                scores(g, 1, 1)
                pe.wait_ge(chosen_ready, g + 1)
                b = take(pe, g, "rank")
                mm(b[:, 0:T * EXP], tri_b[:, :], chosen[:, :, :].rearrange("p t e -> p (t e)"), start=True,
                   stop=True)
                for t in range(T - 1):
                    later = T - 1 - t
                    mm(b[:, (t + 1) * EXP:T * EXP], ones_b[:, :],
                       chosen[:, t, :].unsqueeze(1).broadcast_to([P, later, EXP]), start=False, stop=True,
                       skip_group_check=True)
                for t in range(T):
                    ins = mm(b[:, T * EXP:T * EXP + EXP], ones_b[:, :], chosen[:, t, :], start=(t == 0),
                             stop=(t == T - 1))
                done(ins, "rank")
                context_keys(g, g + 1, 1)
                ahead_drained(g)

            for b in range(NB):
                pe.wait_ge(free[b], G * PER_GROUP[b] + FIRST[b] + 1)
            pe.wait_ge(table_ready, 1)
            pe.wait_ge(experts_loaded, 16 * len(EXPERT_LOADS))
            pe.sem_inc(turned, UNROLL)
            pe.sem_inc(h_mm, 2)
            pe.sem_inc(y_mm, 2)

            def turn_rows(j, i, n):
                pe.wait_ge(x_in[n], i * 16 + 16)
                pe.wait_ge(turned_copied, j + 1)
                nc.tensor.transpose(bank[n % 2][:, 0:P], xt[n], ident[:, :]).then_inc(turned, 1)

            def hidden(j, n):
                pe.wait_ge(turned_copied, j + 1 + 2)
                pe.wait_ge(w1_in, j + 1)
                pe.wait_ge(gelu_done, j + 1)
                for c in range(FC):
                    ins = mm(bank[2 + n % 2][:, c * P:(c + 1) * P], w1c[n % 2][:, c * P:(c + 1) * P],
                             xtT[n % 2], start=True, stop=True)
                ins.then_inc(h_mm, 1)

            def outputs(j, n):
                e = pe.value_load(tab[0:1, 0, bass.ds(j, 1)], min_val=0, max_val=EXP - 1)
                pe.wait_ge(gelu_done, j + 1 + 2)
                pe.wait_ge(y_added, j + 1)
                for c in range(FC):
                    ins = mm(bank[4 + n % 2][:, 0:P], hx[n % 2][:, c, :],
                             w2_t[:, bass.ds(e, 1), c, :].rearrange("p a n -> p (a n)"), start=(c == 0),
                             stop=(c == FC - 1))
                ins.then_inc(y_mm, 1)

            turn_rows(0, 0, 0)
            turn_rows(1, 0, 1)
            hidden(0, 0)
            with pe.Fori(0, TILES // UNROLL - 1) as i:
                for n in range(UNROLL):
                    ahead = n + 2
                    turn_rows(i * UNROLL + ahead, i + ahead // UNROLL, ahead % UNROLL)
                    hidden(i * UNROLL + (n + 1), n + 1)
                    outputs(i * UNROLL + n, n)
            for n in range(UNROLL):
                j = TILES - UNROLL + n
                if j + 2 < TILES:
                    turn_rows(j + 2, (j + 2) // UNROLL, (j + 2) % UNROLL)
                if j + 1 < TILES:
                    hidden(j + 1, n + 1)
                outputs(j, n)


def host_layout(inp):
    f = {k: np.asarray(v) for k, v in inp.items()}
    i128 = np.arange(P)
    c = np.ascontiguousarray

    def quadrants(w):
        src = w.reshape(XC, 4, XD, -1)
        dst = np.zeros((XC, 4, 32, src.shape[-1]), w.dtype)
        for n in range(3):
            dst[:, :, n * XD:(n + 1) * XD] = src
        return c(dst.reshape(XC, P, -1).transpose(2, 0, 1))

    row_one = np.zeros((4, 32, XC), np.float32)
    row_one[:, 24, :] = 1.0
    k_one = np.zeros((4, 32, XC), np.float32)
    for n in range(XC):
        k_one[:, 28 + n, n] = 1.0
    pos = np.zeros((1, 4, 32), np.float32)
    pos[:, :, 24] = MASKED
    low = np.zeros((4, 32, 2), np.float32)
    low[:, 16:24, 0] = -1.0
    low[:, 8:16, 1] = -1.0
    b = f["L0_attn_b_qkv"]
    return {
        "x": c(f["x"].transpose(1, 0, 2)), "xT": c(f["x"].reshape(SEQS * P, P).T),
        "ctxT": c(f["ctx_1024"].reshape(SEQS * P, P).T), "mask": c(f["mask_BxS2_ik1"].reshape(1, -1)),
        "w_pot": f["L0_attn_w_pot"], "b_pot": f["L0_attn_b_pot"].reshape(1, 2),
        "ln1_g": f["L0_attn_ln1_g"].reshape(P, 1), "ln1_b": f["L0_attn_ln1_b"].reshape(P, 1),
        "ln2_g": f["L0_attn_ln2_g"].reshape(P, 1), "ln2_b": f["L0_attn_ln2_b"].reshape(P, 1),
        "ln3_g": f["L0_attn_ln3_g"].reshape(P, 1), "ln3_b": f["L0_attn_ln3_b"].reshape(P, 1),
        "ident": np.eye(P, dtype=np.float32), "antid": c(np.eye(P, dtype=np.float32)[::-1]),
        "tri": (i128[:, None] <= i128[None, :]).astype(np.float32),
        "after": (i128[:, None] > i128[None, :]).astype(np.float32),
        "future": (i128[None, :] < i128[:, None]).astype(np.float32) * np.float32(FAR),
        "pos_only": pos.reshape(1, P),
        "fold_id": c(np.tile(np.eye(SEQS, dtype=np.float32), (2, 1))),
        "w_bk": f["L0_attn_w_bk"], "b_bk": f["L0_attn_b_bk"].reshape(1, P),
        "w_qkv": f["L0_attn_w_qkv"], "b_qk": c(b[:2 * FF].reshape(2 * PAIRS, P).T),
        "b_v": c(b[2 * FF:].reshape(1, FF)),
        "w_out": c(f["L0_attn_w_out"].reshape(PAIRS, P, P).transpose(1, 0, 2)),
        "b_out": f["L0_attn_b_out"].reshape(1, P),
        "w_ff1": f["L0_attn_w_ff1"], "b_ff1": c(f["L0_attn_b_ff1"].reshape(FC, P).T),
        "w_ff2": c(f["L0_attn_w_ff2"].reshape(FC, P, P).transpose(1, 0, 2)),
        "b_ff2": f["L0_attn_b_ff2"].reshape(1, P),
        "wq_pad": quadrants(f["L0_xattn_Wq"]), "wk_pad": quadrants(f["L0_xattn_Wk"]),
        "bq_pad": c(quadrants(f["L0_xattn_bq"].reshape(P, 1))[0].T),
        "bk_pad": c(quadrants(f["L0_xattn_bk"].reshape(P, 1))[0].T),
        "q_ones": row_one.reshape(P, XC), "k_ones": k_one.reshape(P, XC),
        "low_rows": low.reshape(P, 2),
        "wv_t": c(f["L0_xattn_Wv"].T), "wo_t": c(f["L0_xattn_Wo"].T),
        "bv": f["L0_xattn_bv"].reshape(P, 1), "bo": f["L0_xattn_bo"].reshape(1, P),
        "wr_t": c(f["L0_ffn_Wr"].T),
        "w1_t": c(np.concatenate([f["L0_ffn_W1"].transpose(2, 0, 1),
                                  f["L0_ffn_b1"].reshape(EXP, FC, P).transpose(2, 0, 1)], axis=2)),
        "w2_t": c(f["L0_ffn_W2"].reshape(EXP, P, FC, P).transpose(3, 0, 2, 1)),
        "b2": f["L0_ffn_b2"],
        "iota_e": np.arange(EXP, dtype=np.float32).reshape(1, EXP),
        "home": c(np.arange(SEQS * P * TOPK, dtype=np.uint32).reshape(SEQS, P, TOPK).transpose(1, 0, 2)),
        "no_slot": c(np.arange(P * T * TOPK, dtype=np.uint32).reshape(P, T, TOPK) + EXP * REGION),
        "spare": (np.arange(EXP * REGION, dtype=np.uint32) + SEQS * P * TOPK).reshape(EXP * REGION, 1),
        "iota_t": np.arange(TILES, dtype=np.float32).reshape(1, TILES),
        "slot_base": (np.arange(EXP, dtype=np.float32) * REGION - 1).reshape(1, EXP),
    }


def kernel(**inputs):
    import concourse.bacc as bacc
    from concourse.bass_utils import run_bass_kernel_spmd

    arrays = {"in_" + k: np.ascontiguousarray(v) for k, v in host_layout(inputs).items()}
    nc = bacc.Bacc("TRN2", target_bir_lowering=False, num_devices=1)
    A = {k[3:]: nc.dram_tensor(k, v.shape, mybir.dt.from_np(v.dtype), kind="ExternalInput").ap()
         for k, v in arrays.items()}
    A["out"] = nc.dram_tensor("out", (P, SEQS, P), F32, kind="ExternalOutput").ap()
    bass_decoder(nc, A)
    r = run_bass_kernel_spmd(nc, [arrays], core_ids=[0])
    return np.ascontiguousarray(r.results[0]["out"].transpose(1, 0, 2))
```
